# Optimizing a Trainium2 kernel written in Bass

```python
import numpy as np
import jax
import jax.numpy as jnp

def _softmax(x, axis=-1):
    return jax.nn.softmax(x, axis=axis)

def _gelu(x):
    return jax.nn.gelu(x, approximate=True)

def _silu(x):
    return jax.nn.silu(x)

def _sigmoid(x):
    return jax.nn.sigmoid(x)

def _layernorm(x, axis=-1, eps=1e-05):
    m = jnp.mean(x, axis=axis, keepdims=True)
    v = jnp.var(x, axis=axis, keepdims=True)
    return (x - m) / jnp.sqrt(v + eps)

def _scatter_add(tgt, idx, src, axis=0):
    return tgt.at[idx].add(src)

def _segment_sum(src, seg, n):
    return jax.ops.segment_sum(src, seg, n)
kernel_name = 'mk_adj_preln_d4_adj_r2_7bc2c4'

def setup_inputs(seed: int=0):
    np.random.seed(seed)
    _w = jnp.asarray

    def _rec_inputs():
        import jax
        import jax.numpy as jnp
        _gk = jax.random.key(seed)
        x = -0.000125 + 0.9999 * jax.random.normal(jax.random.fold_in(_gk, 1), (64, 128, 256), jnp.float32)
        _w = (1.0 + jnp.arange(128, dtype=jnp.float32)) ** (-0.5)
        _w = _w / _w.mean()
        _pij = jnp.clip(0.0625 * _w[:, None] * _w[None, :], 0.0, 1.0)
        _a = jax.random.uniform(jax.random.fold_in(_gk, 2), (128, 128)) < _pij
        _af = _a.astype(jnp.float32)
        adj = _af
        return (x, adj)
    x, adj = _rec_inputs()

    def _L0_gnn_setup():
        import jax, jax.numpy as jnp
        import numpy as np
        ALPHA = 0.2
        key = jax.random.key(seed)
        k0, k1, k2, k3 = jax.random.split(key, 4)
        B, N, C, F = (64, 512, 256, 256)
        x = jax.random.normal(k0, (B, N, C), dtype=jnp.float32)
        W = jax.random.normal(k1, (C, F), dtype=jnp.float32) * (1.414 / np.sqrt(C + F))
        a = jax.random.normal(k2, (2 * F, 1), dtype=jnp.float32) * (1.414 / np.sqrt(2 * F + 1))
        beta = jnp.ones((1,), dtype=jnp.float32)
        mask = (jax.random.uniform(k3, (N, N)) < 0.3).astype(jnp.float32)
        return {'x': x, 'W': W, 'a': a, 'beta': beta, 'mask': mask}
    _L0_gnn_all = _L0_gnn_setup()
    _L0_gnn_in = {k: v for k, v in _L0_gnn_all.items() if k in ('W', 'a', 'beta')}
    del _L0_gnn_all

    def _L1_gnn_setup():
        import jax, jax.numpy as jnp
        import numpy as np
        B, N, D, O = (8, 2048, 256, 256)
        key = jax.random.key(seed)
        k1, k2, k3, k4 = jax.random.split(key, 4)
        x = jax.random.normal(k1, (B, N, D), dtype=jnp.float32)
        adj = jax.random.uniform(k2, (N, N), dtype=jnp.float32)
        weight = jax.random.normal(k3, (D, O), dtype=jnp.float32) * 0.02
        bias = jax.random.normal(k4, (O,), dtype=jnp.float32) * 0.02
        return {'x': x, 'adj': adj, 'weight': weight, 'bias': bias}
    _L1_gnn_all = _L1_gnn_setup()
    _L1_gnn_in = {k: v for k, v in _L1_gnn_all.items() if k in ('weight', 'bias')}
    del _L1_gnn_all

    def _L2_gnn_setup():
        import jax, jax.numpy as jnp
        import numpy as np
        B, N, D, T = (64, 128, 256, 3)

        def _lin(v, W, b):
            return jnp.einsum('...i,oi->...o', v, W) + b
        key = jax.random.key(seed)
        ks = jax.random.split(key, 12)
        s2 = 1.0 / np.sqrt(2 * D)
        s1 = 1.0 / np.sqrt(D)
        return {'x': jax.random.normal(ks[0], (B, N, D), jnp.float32), 'in_mat': jax.random.uniform(ks[1], (N, N), jnp.float32) / N, 'out_mat': jax.random.uniform(ks[2], (N, N), jnp.float32) / N, 'w3_w': jax.random.normal(ks[3], (D, 2 * D), jnp.float32) * s2, 'w3_b': jnp.zeros((D,), jnp.float32), 'u3_w': jax.random.normal(ks[4], (D, D), jnp.float32) * s1, 'u3_b': jnp.zeros((D,), jnp.float32), 'w4_w': jax.random.normal(ks[5], (D, 2 * D), jnp.float32) * s2, 'w4_b': jnp.zeros((D,), jnp.float32), 'w5_w': jax.random.normal(ks[6], (D, 2 * D), jnp.float32) * s2, 'w5_b': jnp.zeros((D,), jnp.float32), 'u5_w': jax.random.normal(ks[7], (D, D), jnp.float32) * s1, 'u5_b': jnp.zeros((D,), jnp.float32)}
    _L2_gnn_all = _L2_gnn_setup()
    _L2_gnn_in = {k: v for k, v in _L2_gnn_all.items() if k in ('w3_w', 'w3_b', 'u3_w', 'u3_b', 'w4_w', 'w4_b', 'w5_w', 'w5_b', 'u5_w', 'u5_b')}
    del _L2_gnn_all

    def _L3_gnn_setup():
        import jax, jax.numpy as jnp
        import numpy as np
        B, N, D, H = (4, 1024, 256, 8)
        HD = D // H
        key = jax.random.key(seed)
        ks = jax.random.split(key, 10)
        x = jax.random.normal(ks[0], (B, N, D), dtype=jnp.float32)
        adj = (jax.random.uniform(ks[1], (N, N)) < 0.1).astype(jnp.float32)
        s = 1.0 / np.sqrt(D)
        Wq = jax.random.normal(ks[2], (D, D), dtype=jnp.float32) * s
        Wk = jax.random.normal(ks[3], (D, D), dtype=jnp.float32) * s
        Wv = jax.random.normal(ks[4], (D, D), dtype=jnp.float32) * s
        Wo = jax.random.normal(ks[5], (D, D), dtype=jnp.float32) * s
        bq = jnp.zeros((D,), jnp.float32)
        bk = jnp.zeros((D,), jnp.float32)
        bv = jnp.zeros((D,), jnp.float32)
        bo = jnp.zeros((D,), jnp.float32)
        return {'x': x, 'adj': adj, 'Wq': Wq, 'bq': bq, 'Wk': Wk, 'bk': bk, 'Wv': Wv, 'bv': bv, 'Wo': Wo, 'bo': bo}
    _L3_gnn_all = _L3_gnn_setup()
    _L3_gnn_in = {k: v for k, v in _L3_gnn_all.items() if k in ('Wq', 'bq', 'Wk', 'bk', 'Wv', 'bv', 'Wo', 'bo')}
    del _L3_gnn_all
    return {'x': x, 'adj': adj, 'L0_gnn_W': _L0_gnn_in['W'], 'L0_gnn_a': _L0_gnn_in['a'], 'L0_gnn_beta': _L0_gnn_in['beta'], 'L1_gnn_weight': _L1_gnn_in['weight'], 'L1_gnn_bias': _L1_gnn_in['bias'], 'L2_gnn_w3_w': _L2_gnn_in['w3_w'], 'L2_gnn_w3_b': _L2_gnn_in['w3_b'], 'L2_gnn_u3_w': _L2_gnn_in['u3_w'], 'L2_gnn_u3_b': _L2_gnn_in['u3_b'], 'L2_gnn_w4_w': _L2_gnn_in['w4_w'], 'L2_gnn_w4_b': _L2_gnn_in['w4_b'], 'L2_gnn_w5_w': _L2_gnn_in['w5_w'], 'L2_gnn_w5_b': _L2_gnn_in['w5_b'], 'L2_gnn_u5_w': _L2_gnn_in['u5_w'], 'L2_gnn_u5_b': _L2_gnn_in['u5_b'], 'L3_gnn_Wq': _L3_gnn_in['Wq'], 'L3_gnn_bq': _L3_gnn_in['bq'], 'L3_gnn_Wk': _L3_gnn_in['Wk'], 'L3_gnn_bk': _L3_gnn_in['bk'], 'L3_gnn_Wv': _L3_gnn_in['Wv'], 'L3_gnn_bv': _L3_gnn_in['bv'], 'L3_gnn_Wo': _L3_gnn_in['Wo'], 'L3_gnn_bo': _L3_gnn_in['bo']}

def reference(x, adj, L0_gnn_W, L0_gnn_a, L0_gnn_beta, L1_gnn_weight, L1_gnn_bias, L2_gnn_w3_w, L2_gnn_w3_b, L2_gnn_u3_w, L2_gnn_u3_b, L2_gnn_w4_w, L2_gnn_w4_b, L2_gnn_w5_w, L2_gnn_w5_b, L2_gnn_u5_w, L2_gnn_u5_b, L3_gnn_Wq, L3_gnn_bq, L3_gnn_Wk, L3_gnn_bk, L3_gnn_Wv, L3_gnn_bv, L3_gnn_Wo, L3_gnn_bo):
    import jax
    import jax.numpy as jnp

    def _L0_gnn_ref(x, W, a, beta, mask):
        import jax, jax.numpy as jnp
        import numpy as np
        ALPHA = 0.2
        F_ = W.shape[1]
        h = jnp.einsum('bnc,cf->bnf', x, W)
        a1, a2 = (a[:F_, 0], a[F_:, 0])
        s1 = jnp.einsum('bnf,f->bn', h, a1)
        s2 = jnp.einsum('bnf,f->bn', h, a2)
        e = jax.nn.leaky_relu(s1[:, :, None] + s2[:, None, :], negative_slope=ALPHA)
        e = e * mask[None, :, :]
        att = jax.nn.softmax(e, axis=2)
        h_prime = jnp.einsum('bij,bjf->bif', att, h)
        return jax.nn.elu(h_prime + beta * h)

    def _L1_gnn_ref(x, adj, weight, bias):
        import jax, jax.numpy as jnp
        import numpy as np
        B, N, D, O = (8, 2048, 256, 256)
        y = jnp.einsum('nm,bmd->bnd', adj, x)
        out = jnp.einsum('bnd,do->bno', y, weight) + bias
        return out

    def _L2_gnn_ref(x, in_mat, out_mat, w3_w, w3_b, u3_w, u3_b, w4_w, w4_b, w5_w, w5_b, u5_w, u5_b):
        import jax, jax.numpy as jnp
        import numpy as np
        B, N, D, T = (64, 128, 256, 3)

        def _lin(v, W, b):
            return jnp.einsum('...i,oi->...o', v, W) + b
        h = x
        for _ in range(T):
            a_in = jnp.einsum('nm,bmd->bnd', in_mat, h)
            a_out = jnp.einsum('nm,bmd->bnd', out_mat, h)
            av = jnp.concatenate([a_in, a_out], axis=-1)
            z = jax.nn.sigmoid(_lin(av, w3_w, w3_b) + _lin(h, u3_w, u3_b))
            r = jax.nn.sigmoid(_lin(av, w4_w, w4_b) + _lin(h, u3_w, u3_b))
            hv = jnp.tanh(_lin(av, w5_w, w5_b) + _lin(r * h, u5_w, u5_b))
            h = (1.0 - z) * h + z * hv
        return h

    def _L3_gnn_ref(x, adj, Wq, bq, Wk, bk, Wv, bv, Wo, bo):
        import jax, jax.numpy as jnp
        import numpy as np
        B, N, D, H = (4, 1024, 256, 8)
        HD = D // H
        b, n, d = x.shape
        q = (x @ Wq + bq).reshape(b, n, H, HD)
        k = (x @ Wk + bk).reshape(b, n, H, HD)
        v = (x @ Wv + bv).reshape(b, n, H, HD)
        scores = jnp.einsum('bqhd,bkhd->bhqk', q, k) / jnp.sqrt(jnp.float32(HD))
        scores = scores + (1.0 - adj)[None, None, :, :] * -1000000000.0
        attn = jax.nn.softmax(scores, axis=-1)
        out = jnp.einsum('bhqk,bkhd->bqhd', attn, v).reshape(b, n, d)
        return out @ Wo + bo
    h = jnp.maximum(_layernorm(x, axis=-1), 0.0)
    x = x + _L0_gnn_ref(h, L0_gnn_W, L0_gnn_a, L0_gnn_beta, adj)
    h = jnp.maximum(_layernorm(x, axis=-1), 0.0)
    x = x + _L1_gnn_ref(h, adj, L1_gnn_weight, L1_gnn_bias)
    h = jnp.maximum(_layernorm(x, axis=-1), 0.0)
    x = x + _L2_gnn_ref(h, adj, adj, L2_gnn_w3_w, L2_gnn_w3_b, L2_gnn_u3_w, L2_gnn_u3_b, L2_gnn_w4_w, L2_gnn_w4_b, L2_gnn_w5_w, L2_gnn_w5_b, L2_gnn_u5_w, L2_gnn_u5_b)
    h = jnp.maximum(_layernorm(x, axis=-1), 0.0)
    x = x + _L3_gnn_ref(h, adj, L3_gnn_Wq, L3_gnn_bq, L3_gnn_Wk, L3_gnn_bk, L3_gnn_Wv, L3_gnn_bv, L3_gnn_Wo, L3_gnn_bo)
    return x

_drawn_inputs = setup_inputs


def setup_inputs(seed=0):
    import zlib

    import numpy as np

    out = dict(_drawn_inputs(seed))
    spreads = {'L2_gnn_w3_b': (0.0, 0.425),
     'L2_gnn_u3_b': (0.0, 0.418),
     'L2_gnn_w4_b': (0.0, 2.0),
     'L2_gnn_w5_b': (0.0, 0.1),
     'L2_gnn_u5_b': (0.0, 0.1),
     'L3_gnn_bq': (0.0, 2.0),
     'L3_gnn_bk': (0.0, 2.0),
     'L3_gnn_bv': (0.0, 0.1),
     'L3_gnn_bo': (0.0, 0.1)}
    factors = {'L0_gnn_a': 3.806, 'L1_gnn_bias': 2.991}
    for name, (base, spread) in spreads.items():
        noise = np.random.default_rng([zlib.crc32(name.encode()), seed]).standard_normal(out[name].shape)
        drawn = base * np.exp(spread * noise) if base else spread * noise
        out[name] = jnp.asarray(drawn.astype(out[name].dtype))
    for name, factor in factors.items():
        out[name] = (out[name] * factor).astype(out[name].dtype)
    return out
```

```python
import numpy as np
import concourse.bass as bass
from concourse import mybir
from contextlib import ExitStack

F32 = mybir.dt.float32
F32R = mybir.dt.float32r
ACT = mybir.ActivationFunctionType
ALU = mybir.AluOpType
AX = mybir.AxisListType

B, N, D = 64, 128, 256
GB = 4
G = B // GB
C = D // 128
TOK = GB * N
H, HD = 8, 32
HR = 128 // HD
EPS = 1e-5
STEPS = 3
NCHUNK = 8

INPUTS = ['x', 'adj', 'L0_gnn_W', 'L0_gnn_a', 'L0_gnn_beta', 'L1_gnn_weight', 'L1_gnn_bias',
          'L2_gnn_w3_w', 'L2_gnn_w3_b', 'L2_gnn_u3_w', 'L2_gnn_u3_b', 'L2_gnn_w4_w', 'L2_gnn_w4_b',
          'L2_gnn_w5_w', 'L2_gnn_w5_b', 'L2_gnn_u5_w', 'L2_gnn_u5_b', 'L3_gnn_Wq', 'L3_gnn_bq',
          'L3_gnn_Wk', 'L3_gnn_bk', 'L3_gnn_Wv', 'L3_gnn_bv', 'L3_gnn_Wo', 'L3_gnn_bo']


def need(eng, sem, value):
    if not isinstance(value, int) or value > 0:
        eng.wait_ge(sem, value)


def settle(eng, settled):
    eng.sem_inc(settled, 1)


def over_groups(eng, body, peel=2):
    for g in range(peel):
        body(g, g % 2)
    with eng.Fori(peel, G - peel, 2) as g:
        for p in range(2):
            body(g + p, p)
    for g in range(G - peel, G):
        body(g, g % 2)


def exists(g, end=G):
    return not isinstance(g, int) or g < end


def bcast(ap, n):
    return ap.unsqueeze(2).to_broadcast([ap.shape[0], ap.shape[1], n])


def bcast_mid(ap, n):
    return ap.unsqueeze(1).to_broadcast([ap.shape[0], n, ap.shape[1]])


class Chip:
    pass


def prepare(nc, t, c):
    with ExitStack() as ctx:
        sb = lambda n, s, d=F32: ctx.enter_context(nc.sbuf_tensor(n, s, d))
        sem = lambda n: ctx.enter_context(nc.semaphore(n))
        w_raw = {k: sb(f"raw_{k}", [128, C, 2 * D]) for k in ('w3', 'w4', 'w5')}
        u_raw = {k: sb(f"raw_{k}", [128, C, D]) for k in ('u3', 'u5')}
        sums = {k: sb(f"sum_{k}", [128, C, D]) for k in ('w3', 'w4', 'w5')}
        p_raw = {k: sb(f"raw_{k}", [128, C, D]) for k in ('Wq', 'Wk', 'Wv', 'Wo')}
        a_bc = sb("a_bc", [128, 2, D])
        wa_prod = sb("wa_prod", [128, 2, C, D])
        wa = sb("wa", [128, 2, C])
        b_raw = {k: sb(f"raw_{k}", [128, C]) for k in ('w3_b', 'w4_b', 'w5_b', 'u3_b', 'u5_b', 'bq')}
        not_adj = sb("not_adj", [128, N])
        stats = sb("stats0", [128, B, 6])
        banks = [ctx.enter_context(nc.psum_tensor(f"prep_bank{i}", [128, 512], F32)) for i in range(8)]
        x_landed = [sem(f"x_landed{i}") for i in range(NCHUNK)]
        graph_landed, l0_landed, l2_landed, l3_landed = map(
            sem, ('graph_landed', 'l0_landed', 'l2_landed', 'l3_landed'))
        ident_zero, ident_ready, sums_ready, transposed, evacuated, split_hi, split_lo = map(
            sem, ('ident_zero', 'ident_ready', 'sums_ready', 'transposed', 'evacuated', 'split_hi', 'split_lo'))
        prod_ready, wa_ready, mask_half, stats_ready, fold, ones_ready = map(
            sem, ('prod_ready', 'wa_ready', 'mask_half', 'stats_ready', 'fold', 'ones_ready'))
        block = ctx.enter_context(nc.Block())
        per = B // NCHUNK
        n_graph, n_l0, n_l2, n_l3 = 1, 5, 10, 8

        @block.sync
        def _(sp):
            sp.dma_start(c.adj[:], t['adj']).then_inc(graph_landed, 16)
            rows = lambda w: w.rearrange("(c p) d -> p c d", p=128)
            column = lambda v: v.rearrange("(c p) -> p c", p=128)
            row = lambda v, k: v.rearrange("(a n) -> a n", a=1).to_broadcast([128, k])
            for i in range(NCHUNK):
                sp.dma_start(c.x[:, i * per:(i + 1) * per, :],
                             t['x'][i * per:(i + 1) * per].rearrange("b n d -> n b d")
                             ).then_inc(x_landed[i], 16)
                if i == 1:
                    for k in ('w3', 'w4', 'w5'):
                        sp.dma_start(w_raw[k][:], rows(t[f'L2_gnn_{k}_w'])).then_inc(l2_landed, 16)
                    for k in ('u3', 'u5'):
                        sp.dma_start(u_raw[k][:], rows(t[f'L2_gnn_{k}_w'])).then_inc(l2_landed, 16)
            sp.dma_start(c.W0[:], rows(t['L0_gnn_W'])).then_inc(l0_landed, 16)
            sp.dma_start(c.W1[:], rows(t['L1_gnn_weight'])).then_inc(l0_landed, 16)
            sp.dma_start(a_bc[:].rearrange("p a b -> p (a b)"),
                         row(t['L0_gnn_a'].rearrange("n a -> (n a)"), 2 * D)).then_inc(l0_landed, 16)
            sp.dma_start(c.beta[:], row(t['L0_gnn_beta'], 1)).then_inc(l0_landed, 16)
            sp.dma_start(c.bias1[:], row(t['L1_gnn_bias'], D)).then_inc(l0_landed, 16)
            for k in ('w3', 'w4', 'w5', 'u3', 'u5'):
                sp.dma_start(b_raw[k + '_b'][:], column(t[f'L2_gnn_{k}_b']), allow_slow_non_contiguous=True).then_inc(l2_landed, 16)
            for k in ('Wq', 'Wk', 'Wv', 'Wo'):
                sp.dma_start(p_raw[k][:], rows(t[f'L3_gnn_{k}'])).then_inc(l3_landed, 16)
            sp.dma_start(b_raw['bq'][:], column(t['L3_gnn_bq']), allow_slow_non_contiguous=True).then_inc(l3_landed, 16)
            sp.dma_start(c.bk[:], column(t['L3_gnn_bk']), allow_slow_non_contiguous=True).then_inc(l3_landed, 16)
            sp.dma_start(c.bv[:], column(t['L3_gnn_bv']), allow_slow_non_contiguous=True).then_inc(l3_landed, 16)
            sp.dma_start(c.bias3[:], row(t['L3_gnn_bo'], D)).then_inc(l3_landed, 16)

        @block.gpsimd
        def _(pool):
            pool.memset(c.ident[:], 0.0).then_inc(ident_zero, 1)
            pool.memset(c.v_aug[:], 1.0).then_inc(ones_ready, 1)
            pool.memset(c.eps[:], EPS).then_inc(ones_ready, 1)
            pool.wait_ge(ident_zero, 1)
            pool.affine_select(out=c.ident[:], in_=c.ident[:], compare_op=ALU.not_equal, fill=1.0,
                               base=0, pattern=[[-1, N]], channel_multiplier=1).then_inc(ident_ready, 1)
            pool.wait_ge(l2_landed, 16 * n_l2)
            for k in ('w3', 'w4', 'w5'):
                pool.tensor_tensor(sums[k][:], w_raw[k][:, :, 0:D], w_raw[k][:, :, D:2 * D],
                                   ALU.add).then_inc(sums_ready, 1)
            pool.tensor_tensor(c.bz[:], b_raw['w3_b'][:], b_raw['u3_b'][:], ALU.add).then_inc(fold, 1)
            pool.tensor_tensor(c.br[:], b_raw['w4_b'][:], b_raw['u3_b'][:], ALU.add).then_inc(fold, 1)
            pool.tensor_tensor(c.bh[:], b_raw['w5_b'][:], b_raw['u5_b'][:], ALU.add).then_inc(fold, 1)

        order = [('w3', c.w3), ('w4', c.w4), ('w5', c.w5), ('u3', c.u3), ('u5', c.u5)]

        @block.tensor
        def _(pe):
            pe.wait_ge(ident_ready, 1)
            pe.wait_ge(graph_landed, 16)
            pe.transpose(banks[7][:, 0:N], c.adj[:], c.ident[:]).then_inc(transposed, 1)
            pe.wait_ge(sums_ready, 3)
            pe.wait_ge(l2_landed, 16 * n_l2)
            for n, (k, _) in enumerate(order):
                src = sums.get(k, u_raw.get(k))
                for ci in range(C):
                    for co in range(C):
                        last = pe.transpose(banks[n][:, ci * D + co * 128:ci * D + co * 128 + 128],
                                            src[:, co, ci * 128:ci * 128 + 128], c.ident[:])
                last.then_inc(transposed, 1)

        @block.scalar
        def _(act):
            act.wait_ge(transposed, 1)
            act.activation(c.adjT[:], banks[7][:, 0:N], ACT.Copy).then_inc(evacuated, 1)
            act.activation(c.adjT_s[0][:], banks[7][:, 0:N], ACT.Copy).then_inc(evacuated, 1)
            for n, (_, (hi, lo)) in enumerate(order):
                act.wait_ge(transposed, n + 2)
                act.activation(hi[:].rearrange("p c d -> p (c d)"), banks[n][:], ACT.Copy).then_inc(split_hi, 1)
            act.wait_ge(l3_landed, 16 * n_l3)
            for k, (hi, lo) in zip(('Wq', 'Wk', 'Wv', 'Wo'), (c.wq, c.wk, c.wv, c.wo)):
                act.activation(hi[:], p_raw[k][:], ACT.Copy).then_inc(split_hi, 1)
            act.mul(c.bq[:], b_raw['bq'][:], float(HD) ** -0.5).then_inc(evacuated, 1)

        @block.vector
        def _(dve):
            dve.wait_ge(graph_landed, 16 * n_graph)
            dve.tensor_scalar(not_adj[:], c.adj[:], -1.0, 1.0, ALU.mult, ALU.add).then_inc(mask_half, 1)
            dve.wait_ge(mask_half, 1)
            dve.tensor_scalar(c.mask[:], not_adj[:], -1e9, None, ALU.mult).then_inc(mask_half, 1)
            for i in range(NCHUNK):
                dve.wait_ge(x_landed[i], 16)
                for b in range(i * per, (i + 1) * per):
                    dve.bn_stats(stats[:, b, :], c.x[:, b, :]).then_inc(stats_ready, 1)
                dve.wait_ge(stats_ready, (i + 1) * per)
                for b in range(i * per, (i + 1) * per):
                    dve.bn_aggr(c.mv[:, b, :], stats[:, b, :]).then_inc(fold, 1)
            dve.wait_ge(evacuated, 2)
            dve.tensor_tensor(c.adjT_s[1][:], banks[7][:, 0:N], c.adjT_s[0][:].bitcast(F32), ALU.subtract
                              ).then_inc(split_lo, 1)
            dve.wait_ge(l0_landed, 16 * n_l0)
            for k in range(2):
                dve.tensor_tensor(wa_prod[:, k], c.W0[:], bcast_mid(a_bc[:, k, :], C), ALU.mult).then_inc(prod_ready, 1)
            dve.wait_ge(prod_ready, 2)
            dve.tensor_reduce(wa[:], wa_prod[:], AX.X, ALU.add).then_inc(wa_ready, 1)
            dve.wait_ge(wa_ready, 1)
            for k in range(2):
                dve.tensor_copy(c.wa_bc[:, k], bcast(wa[:, k, :], 128)).then_inc(wa_ready, 1)
            for n, (_, (hi, lo)) in enumerate(order):
                dve.wait_ge(split_hi, n + 1)
                dve.tensor_tensor(lo[:].rearrange("p c d -> p (c d)"), banks[n][:],
                                  hi[:].bitcast(F32).rearrange("p c d -> p (c d)"), ALU.subtract).then_inc(split_lo, 1)
            dve.wait_ge(l3_landed, 16 * n_l3)
            for n, (k, (hi, lo)) in enumerate(zip(('Wq', 'Wk', 'Wv', 'Wo'), (c.wq, c.wk, c.wv, c.wo))):
                dve.wait_ge(split_hi, len(order) + n + 1)
                dve.tensor_tensor(lo[:], p_raw[k][:], hi[:].bitcast(F32), ALU.subtract).then_inc(split_lo, 1)


def norm_factors(nc, c, tag):
    with ExitStack() as ctx:
        sb = lambda n: ctx.enter_context(nc.sbuf_tensor(f"{n}{tag}", [128, B], F32))
        sem = lambda n: ctx.enter_context(nc.semaphore(f"{n}{tag}"))
        ve, root, inv, mean_half = sb("ve"), sb("root"), sb("inv"), sb("half")
        root_ready, step = sem("root_ready"), sem("norm_step")
        block = ctx.enter_context(nc.Block())

        @block.scalar
        def _(act):
            act.activation(root[:], c.mv[:, :, 1], ACT.Sqrt, bias=c.eps[:]).then_inc(root_ready, 1)

        @block.vector
        def _(dve):
            dve.tensor_scalar(ve[:], c.mv[:, :, 1], EPS, None, ALU.add).then_inc(step, 1)
            dve.wait_ge(root_ready, 1)
            dve.reciprocal(inv[:], root[:]).then_inc(step, 1)
            dve.wait_ge(step, 2)
            dve.tensor_tensor(mean_half[:], ve[:], inv[:], ALU.mult).then_inc(step, 1)
            dve.wait_ge(step, 3)
            dve.tensor_tensor(ve[:], mean_half[:], root[:], ALU.add).then_inc(step, 1)
            dve.wait_ge(step, 4)
            dve.tensor_scalar(root[:], ve[:], 0.5, None, ALU.mult).then_inc(step, 1)
            dve.wait_ge(step, 5)
            dve.reciprocal(c.rstd[:], root[:]).then_inc(step, 1)
            dve.wait_ge(step, 6)
            dve.scalar_tensor_tensor(c.nmr[:], c.mv[:, :, 0], -1.0, c.rstd[:], ALU.mult, ALU.mult).then_inc(step, 1)


def group_stats(dve, c, g, stats, x_ready, x_count, stats_ready, aggregated, mv_ready):
    dve.wait_ge(x_ready, x_count)
    settle(dve, c.settled_dve)
    for b in range(GB):
        dve.bn_stats(stats[:, b, :], c.x[:, bass.ds(g * GB + b, 1), :].rearrange("p a d -> p (a d)")
                     ).then_inc(stats_ready, 1)
    dve.wait_ge(stats_ready, g * GB + GB)
    need(dve, mv_ready, g)
    settle(dve, c.settled_dve)
    for b in range(GB):
        dve.bn_aggr(c.mv_group[:, b, :], stats[:, b, :]).then_inc(aggregated, 1)
    dve.wait_ge(aggregated, g * GB + GB)
    settle(dve, c.settled_dve)
    dve.tensor_copy(c.mv[:, bass.ds(g * GB, GB), :], c.mv_group[:]).then_inc(mv_ready, 1)


def layer0(nc, c):
    with ExitStack() as ctx:
        sb = lambda n, s, d=F32: ctx.enter_context(nc.sbuf_tensor("l0_" + n, s, d))
        sem = lambda n: ctx.enter_context(nc.semaphore("l0_" + n))
        bank = lambda n: ctx.enter_context(nc.psum_tensor("l0_" + n, [128, 512], F32))
        xn = [sb(f"xn{p}", [128, GB, D]) for p in range(2)]
        hT = [sb(f"hT{p}", [128, C, TOK]) for p in range(2)]
        hw = [sb(f"hw{p}", [128, GB, D]) for p in range(2)]
        bhw = [sb(f"bhw{p}", [128, GB, D]) for p in range(2)]
        leak, e, prob = sb("leak", [128, GB, N]), sb("e", [128, GB, N]), sb("prob", [128, GB, N])
        probT = sb("probT", [128, TOK])
        top, total, rtotal = sb("top", [128, GB]), sb("total", [128, GB]), sb("rtotal", [128, GB])
        u, low, ex = sb("u", [128, GB, D]), sb("low", [128, GB, D]), sb("ex", [128, GB, D])
        stats = sb("stats", [128, GB, 6])
        pT = [bank("pT0"), bank("pT1")]
        pW = [bank("pW0"), bank("pW1")]
        pS, pP = bank("pS"), bank("pP")
        pO = [bank("pO0"), bank("pO1")]
        (normed, t_ready, hT_ready, s_ready, w_ready, hw_ready, bhw_ready, leak_ready, lrelu_ready, e_ready, top_ready,
         shift_ready, prob_ready, total_ready, rtotal_ready, pt_ready, probT_ready, o_ready, u_ready, low_ready, ex_ready,
         elu_ready, x_ready, stats_ready, aggregated, mv_ready) = map(sem, (
            'normed', 't_ready', 'hT_ready', 's_ready', 'w_ready', 'hw_ready', 'bhw_ready', 'leak_ready', 'lrelu_ready', 'e_ready',
            'top_ready', 'shift_ready', 'prob_ready', 'total_ready', 'rtotal_ready', 'pt_ready', 'probT_ready', 'o_ready',
            'u_ready', 'low_ready', 'ex_ready', 'elu_ready', 'x_ready', 'stats_ready', 'aggregated', 'mv_ready'))
        block = ctx.enter_context(nc.Block())

        @block.tensor
        def _(pe):
            def turn_tokens(g, p):
                pe.wait_ge(normed, g * GB + GB)
                need(pe, hT_ready, g * C)
                for k in range(C):
                    for b in range(GB):
                        last = pe.transpose(pT[k][:, b * N:b * N + N], xn[p][:, b, k * 128:k * 128 + 128], c.ident[:])
                    last.then_inc(t_ready, 1)

            def scores(g, p):
                pe.wait_ge(hT_ready, g * C + C)
                need(pe, lrelu_ready, g)
                for k in range(C):
                    pe.matmul(pS[:], c.wa_bc[:, 1, k, :], hT[p][:, k, :], start=(k == 0), stop=False)
                for b in range(GB):
                    for k in range(C):
                        last = pe.matmul(pS[:, b * N:b * N + N], hT[p][:, k, b * N:b * N + N], c.wa_bc[:, 0, k, :],
                                         start=False, stop=(b == GB - 1 and k == C - 1))
                last.then_inc(s_ready, 1)

            def project(g, p):
                need(pe, bhw_ready, g * 2)
                need(pe, hw_ready, g * 2)
                for b in range(GB):
                    for k in range(C):
                        last = pe.matmul(pW[b // 2][:, (b % 2) * D:(b % 2) * D + D], hT[p][:, k, b * N:b * N + N],
                                         c.W0[:, k, :], start=(k == 0), stop=(k == C - 1))
                    if b % 2:
                        last.then_inc(w_ready, 1)

            def attend(g, p):
                pe.wait_ge(prob_ready, g + 1)
                need(pe, probT_ready, g)
                for b in range(GB):
                    last = pe.transpose(pP[:, b * N:b * N + N], prob[:, b, :], c.ident[:])
                last.then_inc(pt_ready, 1)
                pe.wait_ge(probT_ready, g + 1)
                pe.wait_ge(hw_ready, g * 2 + 2)
                need(pe, u_ready, g * GB)
                for b in range(GB):
                    last = pe.matmul(pO[b // 2][:, (b % 2) * D:(b % 2) * D + D], probT[:, b * N:b * N + N],
                                     hw[p][:, b, :], start=True, stop=True)
                    if b % 2:
                        last.then_inc(o_ready, 1)

            def body(g, p):
                if exists(g + 1):
                    scores(g + 1, 1 - p)
                if exists(g + 2):
                    turn_tokens(g + 2, p)
                if exists(g + 1):
                    project(g + 1, 1 - p)
                attend(g, p)

            turn_tokens(0, 0)
            scores(0, 0)
            turn_tokens(1, 1)
            project(0, 0)
            over_groups(pe, body)

        @block.scalar
        def _(act):
            def take_hT(g, p):
                for k in range(C):
                    act.wait_ge(t_ready, g * C + k + 1)
                    act.activation(hT[p][:, k, :], pT[k][:], ACT.Relu).then_inc(hT_ready, 1)

            def take_scores(g):
                act.wait_ge(s_ready, g + 1)
                need(act, lrelu_ready, g)
                act.mul(leak[:].rearrange("p a b -> p (a b)"), pS[:], 0.2).then_inc(leak_ready, 1)

            def take_hw(g, p):
                need(act, o_ready, (g - 1) * 2)
                need(act, u_ready, (g - 1) * GB)
                for k in range(2):
                    act.wait_ge(w_ready, g * 2 + k + 1)
                    act.activation(hw[p][:, 2 * k:2 * k + 2, :].rearrange("p a b -> p (a b)"), pW[k][:], ACT.Copy
                                   ).then_inc(hw_ready, 1)
                    act.activation(bhw[p][:, 2 * k:2 * k + 2, :].rearrange("p a b -> p (a b)"), pW[k][:], ACT.Copy,
                                   scale=c.beta[:]).then_inc(bhw_ready, 1)

            def take_probT(g):
                act.wait_ge(pt_ready, g + 1)
                need(act, o_ready, g * 2)
                act.activation(probT[:], pP[:], ACT.Copy).then_inc(probT_ready, 1)

            def probs(g):
                act.wait_ge(shift_ready, g + 1)
                need(act, pt_ready, g)
                need(act, total_ready, g)
                act.activation(prob[:], e[:], ACT.Exp).then_inc(prob_ready, 1)

            def body(g, p):
                if exists(g + 1):
                    take_scores(g + 1)
                if exists(g + 2):
                    take_hT(g + 2, p)
                take_probT(g)
                if exists(g + 1):
                    take_hw(g + 1, 1 - p)
                    probs(g + 1)
                act.wait_ge(low_ready, g + 1)
                need(act, elu_ready, g)
                act.activation(ex[:], low[:], ACT.Exp).then_inc(ex_ready, 1)

            take_hT(0, 0)
            take_scores(0)
            take_hT(1, 1)
            take_hw(0, 0)
            probs(0)
            over_groups(act, body)

        @block.gpsimd
        def _(pool):
            def body(g, p):
                pool.wait_ge(u_ready, g * GB + GB)
                need(pool, ex_ready, g)
                settle(pool, c.settled_pool)
                pool.tensor_scalar(low[:], u[:], 0.0, None, ALU.min).then_inc(low_ready, 1)
            over_groups(pool, body)

        @block.vector
        def _(dve):
            def norm(g, p):
                need(dve, t_ready, (g - 1) * C)
                for b in range(GB):
                    i = g * GB + b
                    dve.tensor_scalar(xn[p][:, b, :], c.x[:, bass.ds(i, 1), :].rearrange("p a d -> p (a d)"),
                                      c.rstd[:, bass.ds(i, 1)], c.nmr[:, bass.ds(i, 1)], ALU.mult, ALU.add
                                      ).then_inc(normed, 1)

            def softmax(g):
                dve.wait_ge(leak_ready, g + 1)
                need(dve, prob_ready, g)
                dve.tensor_tensor(e[:].rearrange("p a b -> p (a b)"), pS[:], leak[:].rearrange("p a b -> p (a b)"),
                                  ALU.max).then_inc(lrelu_ready, 1)
                dve.wait_ge(lrelu_ready, g + 1)
                dve.tensor_tensor(e[:], e[:], bcast_mid(c.adj[:], GB), ALU.mult).then_inc(e_ready, 1)
                dve.wait_ge(e_ready, g + 1)
                dve.tensor_reduce(top[:], e[:], AX.X, ALU.max).then_inc(top_ready, 1)
                dve.wait_ge(top_ready, g + 1)
                dve.tensor_tensor(e[:], e[:], bcast(top[:], N), ALU.subtract).then_inc(shift_ready, 1)

            def combine(g, p):
                dve.wait_ge(prob_ready, g + 1)
                dve.tensor_reduce(total[:], prob[:], AX.X, ALU.add).then_inc(total_ready, 1)
                dve.wait_ge(total_ready, g + 1)
                need(dve, u_ready, g * GB)
                dve.reciprocal(rtotal[:], total[:]).then_inc(rtotal_ready, 1)
                dve.wait_ge(rtotal_ready, g + 1)
                dve.wait_ge(bhw_ready, g * 2 + 2)
                need(dve, low_ready, g)
                need(dve, elu_ready, g)
                for b in range(GB):
                    dve.wait_ge(o_ready, g * 2 + b // 2 + 1)
                    dve.scalar_tensor_tensor(u[:, b, :], pO[b // 2][:, (b % 2) * D:(b % 2) * D + D],
                                             rtotal[:, b:b + 1], bhw[p][:, b, :], ALU.mult, ALU.add
                                             ).then_inc(u_ready, 1)

            def residual(g):
                dve.wait_ge(ex_ready, g + 1)
                dve.wait_ge(u_ready, g * GB + GB)
                dve.scalar_tensor_tensor(u[:].rearrange("p a b -> p (a b)"), u[:].rearrange("p a b -> p (a b)"), 0.0,
                                         ex[:].rearrange("p a b -> p (a b)"), ALU.max, ALU.add).then_inc(elu_ready, 1)
                dve.wait_ge(elu_ready, g + 1)
                xg = c.x[:, bass.ds(g * GB, GB), :].rearrange("p a b -> p (a b)")
                dve.scalar_tensor_tensor(xg, u[:].rearrange("p a b -> p (a b)"), -1.0, xg, ALU.add, ALU.add
                                         ).then_inc(x_ready, 1)
                group_stats(dve, c, g, stats, x_ready, g + 1, stats_ready, aggregated, mv_ready)

            def body(g, p):
                if exists(g + 1):
                    softmax(g + 1)
                if exists(g + 3):
                    norm(g + 3, 1 - p)
                combine(g, p)
                residual(g)

            norm(0, 0)
            norm(1, 1)
            softmax(0)
            norm(2, 0)
            over_groups(dve, body, peel=4)


def layer1(nc, c):
    with ExitStack() as ctx:
        sb = lambda n, s, d=F32: ctx.enter_context(nc.sbuf_tensor("l1_" + n, s, d))
        sem = lambda n: ctx.enter_context(nc.semaphore("l1_" + n))
        bank = lambda n: ctx.enter_context(nc.psum_tensor("l1_" + n, [128, 512], F32))
        h = [sb(f"h{p}", [128, GB, D]) for p in range(2)]
        yT = [sb(f"yT{p}", [128, C, TOK]) for p in range(2)]
        stats = sb("stats", [128, GB, 6])
        pY = [[bank(f"pY{p}{k}") for k in range(C)] for p in range(2)]
        pZ = [[bank(f"pZ{p}{k}") for k in range(2)] for p in range(2)]
        h_ready, biased, y_ready, yT_ready, z_ready, x_ready, stats_ready, aggregated, mv_ready = map(
            sem, ('h_ready', 'biased', 'y_ready', 'yT_ready', 'z_ready', 'x_ready', 'stats_ready', 'aggregated', 'mv_ready'))
        block = ctx.enter_context(nc.Block())

        @block.scalar
        def _(act):
            def body(g, p):
                need(act, y_ready, (g - 1) * C)
                for b in range(GB):
                    i = g * GB + b
                    act.activation(h[p][:, b, :], c.x[:, bass.ds(i, 1), :].rearrange("p a d -> p (a d)"), ACT.Relu,
                                   bias=c.nmr[:, bass.ds(i, 1)], scale=c.rstd[:, bass.ds(i, 1)]).then_inc(h_ready, 1)
            over_groups(act, body)

        @block.gpsimd
        def _(pool):
            def body(g, p):
                pool.wait_ge(h_ready, g * GB + GB)
                xg = c.x[:, bass.ds(g * GB, GB), :]
                pool.tensor_tensor(xg, xg, bcast_mid(c.bias1[:], GB), ALU.add).then_inc(biased, 1)
            over_groups(pool, body)

        @block.tensor
        def _(pe):
            def gather(g, p):
                pe.wait_ge(h_ready, g * GB + GB)
                need(pe, yT_ready, (g - 1) * C)
                for k in range(C):
                    for b in range(GB):
                        last = pe.matmul(pY[p][k][:, b * N:b * N + N], h[p][:, b, k * 128:k * 128 + 128], c.adjT[:],
                                         start=True, stop=True)
                    last.then_inc(y_ready, 1)

            def project(g, p):
                pe.wait_ge(yT_ready, g * C + C)
                need(pe, x_ready, (g - 1) * 2)
                for b in range(GB):
                    for k in range(C):
                        last = pe.matmul(pZ[p][b // 2][:, (b % 2) * D:(b % 2) * D + D], yT[p][:, k, b * N:b * N + N],
                                         c.W1[:, k, :], start=(k == 0), stop=(k == C - 1))
                    if b % 2:
                        last.then_inc(z_ready, 1)

            def body(g, p):
                if exists(g + 1):
                    gather(g + 1, 1 - p)
                project(g, p)
            gather(0, 0)
            over_groups(pe, body)

        @block.vector
        def _(dve):
            def take_y(g, p):
                need(dve, z_ready, (g - 1) * 2)
                for k in range(C):
                    dve.wait_ge(y_ready, g * C + k + 1)
                    dve.tensor_copy(yT[p][:, k, :], pY[p][k][:]).then_inc(yT_ready, 1)

            def body(g, p):
                if exists(g + 1):
                    take_y(g + 1, 1 - p)
                dve.wait_ge(biased, g + 1)
                for k in range(2):
                    dve.wait_ge(z_ready, g * 2 + k + 1)
                    xk = c.x[:, bass.ds(g * GB + 2 * k, 2), :].rearrange("p a b -> p (a b)")
                    dve.tensor_tensor(xk, pZ[p][k][:], xk, ALU.add).then_inc(x_ready, 1)
                group_stats(dve, c, g, stats, x_ready, g * 2 + 2, stats_ready, aggregated, mv_ready)
            take_y(0, 0)
            over_groups(dve, body)


def layer2(nc, c):
    PAIRS, TURNS = G // 2, 2 * STEPS
    with ExitStack() as ctx:
        sb = lambda n, s, d=F32: ctx.enter_context(nc.sbuf_tensor("l2_" + n, s, d))
        bank = lambda n: ctx.enter_context(nc.psum_tensor("l2_" + n, [128, 512], F32))
        h0 = sb("h0", [128, GB, D])
        nat = [sb(n, [128, GB, D], F32R) for n in ("nat_hi", "nat_lo")]
        hT = [sb(f"hT{q}", [128, C, TOK]) for q in range(2)]
        hT_s = [[sb(f"hT_{n}{q}", [128, C, TOK], F32R) for n in ("hi", "lo")] for q in range(2)]
        aT = [sb(n, [128, C, TOK], F32R) for n in ("aT_hi", "aT_lo")]
        r, z, hv, rh, d = (sb(n, [128, C, TOK]) for n in ("r", "z", "hv", "rh", "d"))
        rh_s = [sb(n, [128, C, TOK], F32R) for n in ("rh_hi", "rh_lo")]
        stats = sb("stats", [128, GB, 6])
        pR, pZ, pH, pT = ([bank(f"p{n}{k}") for k in range(C)] for n in "RZHT")
        (h0_ready, nat_hi_ready, nat_lo_ready, t_ready, hT0_ready, hT_hi_ready, hT_lo_ready, a_ready, a_hi_ready,
         a_lo_ready, r_ready, z_ready, hv_ready, r_sig, z_sig, hv_tanh, rh_ready, rh_hi_ready, rh_lo_ready, d_ready,
         zd_ready, new_h, f_ready, x_ready, stats_ready, aggregated, mv_ready) = (
            ctx.enter_context(nc.semaphore("l2_" + n)) for n in (
                'h0_ready', 'nat_hi_ready', 'nat_lo_ready', 't_ready', 'hT0_ready', 'hT_hi_ready', 'hT_lo_ready',
                'a_ready', 'a_hi_ready', 'a_lo_ready', 'r_ready', 'z_ready', 'hv_ready', 'r_sig', 'z_sig', 'hv_tanh',
                'rh_ready', 'rh_hi_ready', 'rh_lo_ready', 'd_ready', 'zd_ready', 'new_h', 'f_ready', 'x_ready',
                'stats_ready', 'aggregated', 'mv_ready'))
        block = ctx.enter_context(nc.Block())
        flat = lambda ap: ap.rearrange("p a b -> p (a b)")

        def over_turns(eng, turn):
            for pos in range(TURNS):
                turn(0, pos)
            with eng.Fori(1, PAIRS - 1) as j:
                for pos in range(TURNS):
                    turn(j, pos)
            for pos in range(TURNS):
                turn(PAIRS - 1, pos)

        def following(j, pos):
            if pos + 1 < TURNS:
                return j, pos + 1
            return None if isinstance(j, int) and j == PAIRS - 1 else (j + 1, 0)

        def preceding(j, pos):
            if pos:
                return j, pos - 1
            return None if isinstance(j, int) and j == 0 else (j - 1, TURNS - 1)

        def first_step(pos):
            return pos < 2

        def last_step(pos):
            return pos >= TURNS - 2

        @block.tensor
        def _(pe):
            def passes(out, weight, moving, co, first, last):
                todo = [(k, wi, mi) for k in range(C) for wi, mi in ((0, 0), (0, 1), (1, 0))]
                for n, (k, wi, mi) in enumerate(todo):
                    ins = pe.matmul(out[:], weight[wi][:, k, co * 128:co * 128 + 128], moving[mi][:, k, :],
                                    start=first and n == 0, stop=last and n == len(todo) - 1)
                return ins

            def gate(K, out, weight, q, ready, taken):
                need(pe, taken, K * C)
                for co in range(C):
                    passes(out[co], c.u3, hT_s[q], co, True, False)
                    passes(out[co], weight, aT, co, False, True).then_inc(ready, 1)

            def back_to_nodes(q, ready):
                for half in range(2):
                    for b in (2 * half, 2 * half + 1):
                        for k in range(C):
                            at = (b % 2) * D + k * 128
                            last = pe.transpose(pT[half][:, at:at + 128], hT[q][:, k, b * N:b * N + N], c.ident[:])
                    last.then_inc(ready, 1)

            def turn_h(j, pos):
                K = j * TURNS + pos
                need(pe, a_lo_ready, K * C)
                if first_step(pos):
                    need(pe, x_ready, (2 * j - 1 + pos) * 2)
                    pe.wait_ge(h0_ready, (2 * j + pos + 1) * GB)
                    for k in range(C):
                        for b in range(GB):
                            last = pe.transpose(pT[k][:, b * N:b * N + N], h0[:, b, k * 128:k * 128 + 128], c.ident[:])
                        last.then_inc(t_ready, 1)
                else:
                    pe.wait_ge(new_h, (K - 1) * C)
                    back_to_nodes(pos % 2, t_ready)

            def gather(j, pos):
                K = j * TURNS + pos
                pe.wait_ge(nat_hi_ready, K * 2 + 2)
                pe.wait_ge(nat_lo_ready, K * 2 + 2)
                if first_step(pos):
                    pe.wait_ge(hT0_ready, (2 * j + pos + 1) * C)
                    pe.wait_ge(hT_hi_ready, K * C + C)
                    pe.wait_ge(hT_lo_ready, K * C + C)
                for k in range(C):
                    for b in range(GB):
                        for n, (hi, ai) in enumerate(((0, 0), (0, 1), (1, 0))):
                            last = pe.matmul(pT[k][:, b * N:b * N + N], nat[hi][:, b, k * 128:k * 128 + 128],
                                             c.adjT_s[ai][:], start=(n == 0), stop=(n == 2))
                    last.then_inc(a_ready, 1)

            def final_h(K, q):
                pe.wait_ge(new_h, K * C)
                back_to_nodes(q, f_ready)

            def turn(j, pos):
                K = j * TURNS + pos
                nxt, prev = following(j, pos), preceding(j, pos)
                pe.wait_ge(hT_hi_ready, K * C + C)
                pe.wait_ge(hT_lo_ready, K * C + C)
                pe.wait_ge(a_hi_ready, K * C + C)
                pe.wait_ge(a_lo_ready, K * C + C)
                gate(K, pR, c.w4, pos % 2, r_ready, r_sig)
                if prev and last_step(prev[1]):
                    final_h(K, prev[1] % 2)
                gate(K, pZ, c.w3, pos % 2, z_ready, z_sig)
                if nxt:
                    turn_h(*nxt)
                need(pe, hv_tanh, K * C)
                for co in range(C):
                    passes(pH[co], c.w5, aT, co, True, False)
                if nxt:
                    gather(*nxt)
                pe.wait_ge(rh_hi_ready, K * C + C)
                pe.wait_ge(rh_lo_ready, K * C + C)
                for co in range(C):
                    passes(pH[co], c.u5, rh_s, co, False, True).then_inc(hv_ready, 1)

            turn_h(0, 0)
            gather(0, 0)
            over_turns(pe, turn)
            pe.wait_ge(a_lo_ready, PAIRS * TURNS * C)
            pe.wait_ge(x_ready, (G - 1) * 2)
            final_h(PAIRS * TURNS, 1)

        @block.scalar
        def _(act):
            def make_h0(j, pos):
                K, g = j * TURNS + pos, 2 * j + pos
                need(act, a_ready, K * C)
                for b in range(GB):
                    i = g * GB + b
                    act.activation(h0[:, b, :], flat(c.x[:, bass.ds(i, 1), :]), ACT.Relu,
                                   bias=c.nmr[:, bass.ds(i, 1)], scale=c.rstd[:, bass.ds(i, 1)]).then_inc(h0_ready, 1)
                act.wait_ge(h0_ready, (g + 1) * GB)
                for half in range(2):
                    act.activation(nat[0][:, 2 * half:2 * half + 2, :], h0[:, 2 * half:2 * half + 2, :], ACT.Copy
                                   ).then_inc(nat_hi_ready, 1)

            def take_turned(j, pos):
                K = j * TURNS + pos
                for k in range(2):
                    act.wait_ge(t_ready, K * 2 + k + 1)
                    if first_step(pos):
                        act.activation(hT[pos % 2][:, k, :], pT[k][:], ACT.Copy).then_inc(hT0_ready, 1)
                        act.activation(hT_s[pos % 2][0][:, k, :], pT[k][:], ACT.Copy).then_inc(hT_hi_ready, 1)
                    else:
                        act.activation(flat(nat[0][:, 2 * k:2 * k + 2, :]), pT[k][:], ACT.Copy).then_inc(nat_hi_ready, 1)

            def take_gathered(j, pos):
                K = j * TURNS + pos
                for k in range(C):
                    act.wait_ge(a_ready, K * C + k + 1)
                    act.activation(aT[0][:, k, :], pT[k][:], ACT.Copy).then_inc(a_hi_ready, 1)

            def finish(j, pos):
                K = j * TURNS + pos
                need(act, d_ready, K)
                for co in range(C):
                    act.wait_ge(hv_ready, K * C + co + 1)
                    act.activation(hv[:, co, :], pH[co][:], ACT.Tanh, bias=c.bh[:, co:co + 1]).then_inc(hv_tanh, 1)

            def split_new_h(j, pos):
                K = j * TURNS + pos
                for k in range(C):
                    act.wait_ge(new_h, K * C + k + 1)
                    act.activation(hT_s[pos % 2][0][:, k, :], hT[pos % 2][:, k, :], ACT.Copy).then_inc(hT_hi_ready, 1)

            def turn(j, pos):
                K = j * TURNS + pos
                nxt, prev = following(j, pos), preceding(j, pos)
                if prev:
                    finish(*prev)
                if nxt and first_step(nxt[1]):
                    make_h0(*nxt)
                if prev and not last_step(prev[1]):
                    split_new_h(*prev)
                for co in range(C):
                    act.wait_ge(r_ready, K * C + co + 1)
                    act.activation(r[:, co, :], pR[co][:], ACT.Sigmoid, bias=c.br[:, co:co + 1]).then_inc(r_sig, 1)
                for co in range(C):
                    act.wait_ge(rh_ready, K * C + co + 1)
                    act.activation(rh_s[0][:, co, :], rh[:, co, :], ACT.Copy).then_inc(rh_hi_ready, 1)
                need(act, zd_ready, K * C)
                for co in range(C):
                    act.wait_ge(z_ready, K * C + co + 1)
                    act.activation(z[:, co, :], pZ[co][:], ACT.Sigmoid, bias=c.bz[:, co:co + 1]).then_inc(z_sig, 1)
                if nxt:
                    take_turned(*nxt)
                    take_gathered(*nxt)

            make_h0(0, 0)
            take_turned(0, 0)
            take_gathered(0, 0)
            over_turns(act, turn)
            finish(PAIRS - 1, TURNS - 1)

        @block.vector
        def _(dve):
            def take_turned(j, pos):
                K = j * TURNS + pos
                if first_step(pos):
                    for half in range(2):
                        dve.wait_ge(nat_hi_ready, K * 2 + half + 1)
                        dve.tensor_tensor(nat[1][:, 2 * half:2 * half + 2, :], h0[:, 2 * half:2 * half + 2, :],
                                          nat[0][:, 2 * half:2 * half + 2, :].bitcast(F32), ALU.subtract
                                          ).then_inc(nat_lo_ready, 1)
                for k in range(2):
                    if first_step(pos):
                        dve.wait_ge(hT_hi_ready, K * C + k + 1)
                        dve.tensor_tensor(hT_s[pos % 2][1][:, k, :], pT[k][:],
                                          hT_s[pos % 2][0][:, k, :].bitcast(F32), ALU.subtract).then_inc(hT_lo_ready, 1)
                    else:
                        dve.wait_ge(nat_hi_ready, K * 2 + k + 1)
                        dve.tensor_tensor(flat(nat[1][:, 2 * k:2 * k + 2, :]), pT[k][:],
                                          flat(nat[0][:, 2 * k:2 * k + 2, :].bitcast(F32)), ALU.subtract
                                          ).then_inc(nat_lo_ready, 1)

            def take_gathered(j, pos):
                K = j * TURNS + pos
                for k in range(C):
                    dve.wait_ge(a_hi_ready, K * C + k + 1)
                    dve.tensor_tensor(aT[1][:, k, :], pT[k][:], aT[0][:, k, :].bitcast(F32), ALU.subtract
                                      ).then_inc(a_lo_ready, 1)

            def finish(j, pos):
                K, q = j * TURNS + pos, pos % 2
                dve.wait_ge(hv_tanh, K * C + C)
                need(dve, zd_ready, K * C)
                dve.tensor_tensor(d[:], hv[:], hT[q][:], ALU.subtract).then_inc(d_ready, 1)
                dve.wait_ge(d_ready, K + 1)
                dve.wait_ge(z_sig, K * C + C)
                need(dve, new_h, K * C)
                for co in range(C):
                    dve.tensor_tensor(d[:, co, :], z[:, co, :], d[:, co, :], ALU.mult).then_inc(zd_ready, 1)
                for co in range(C):
                    dve.wait_ge(zd_ready, K * C + co + 1)
                    dve.tensor_tensor(hT[q][:, co, :], hT[q][:, co, :], d[:, co, :], ALU.add).then_inc(new_h, 1)
                if not last_step(pos):
                    for co in range(C):
                        dve.wait_ge(hT_hi_ready, (K + 2) * C + co + 1)
                        dve.tensor_tensor(hT_s[q][1][:, co, :], hT[q][:, co, :], hT_s[q][0][:, co, :].bitcast(F32),
                                          ALU.subtract).then_inc(hT_lo_ready, 1)

            def add_final(g):
                for half in range(2):
                    dve.wait_ge(f_ready, g * 2 + half + 1)
                    xh = flat(c.x[:, bass.ds(g * GB + 2 * half, 2), :])
                    dve.tensor_tensor(xh, pT[half][:], xh, ALU.add).then_inc(x_ready, 1)

            def turn(j, pos):
                K, q = j * TURNS + pos, pos % 2
                nxt, prev = following(j, pos), preceding(j, pos)
                if prev:
                    finish(*prev)
                for co in range(C):
                    dve.wait_ge(r_sig, K * C + co + 1)
                    dve.tensor_tensor(rh[:, co, :], r[:, co, :], hT[q][:, co, :], ALU.mult).then_inc(rh_ready, 1)
                if prev and last_step(prev[1]):
                    g = 2 * prev[0] + prev[1] % 2
                    add_final(g)
                for co in range(C):
                    dve.wait_ge(rh_hi_ready, K * C + co + 1)
                    dve.tensor_tensor(rh_s[1][:, co, :], rh[:, co, :], rh_s[0][:, co, :].bitcast(F32), ALU.subtract
                                      ).then_inc(rh_lo_ready, 1)
                if nxt:
                    take_turned(*nxt)
                    take_gathered(*nxt)
                if prev and last_step(prev[1]):
                    group_stats(dve, c, g, stats, x_ready, g * 2 + 2, stats_ready, aggregated, mv_ready)

            take_turned(0, 0)
            take_gathered(0, 0)
            over_turns(dve, turn)
            finish(PAIRS - 1, TURNS - 1)
            add_final(G - 1)
            group_stats(dve, c, G - 1, stats, x_ready, G * 2, stats_ready, aggregated, mv_ready)


def layer3(nc, c, out):
    UB = GB // 2
    with ExitStack() as ctx:
        sb = lambda n, s, d=F32: ctx.enter_context(nc.sbuf_tensor("l3_" + n, s, d))
        bank = lambda n: ctx.enter_context(nc.psum_tensor("l3_" + n, [128, 512], F32))
        xn = sb("xn", [128, GB, D])
        hT = [sb(n, [128, C, TOK], F32R) for n in ("hT_hi", "hT_lo")]
        qT, kT = sb("qT", [128, C, TOK]), sb("kT", [128, C, TOK])
        logit = sb("logit", [128, HR, UB * C, N])
        prob = [sb(f"prob{e}", [128, HR, UB * C, N]) for e in range(2)]
        top = sb("top", [128, HR, UB * C])
        probT = sb("probT", [128, HR, UB * C * N])
        rtotal = sb("rtotal", [128, UB, H])
        o = sb("o", [128, UB, D])
        oT = [sb(n, [128, C, UB * N], F32R) for n in ("oT_hi", "oT_lo")]
        pS = [bank(f"pS{r}") for r in range(HR)]
        pT = [bank(f"pT{k}") for k in range(2)]
        pJ = [bank(f"pJ{k}") for k in range(2)]
        (normed, biased, t_ready, hT_hi_ready, hT_lo_ready, q_ready, qT_ready, k_ready, kT_ready, v_ready, v_taken,
         s_ready, masked, top_ready, shifted, prob_ready, pt_ready, probT_ready, pv_ready, rtotal_ready, o_ready,
         ot_ready, oT_hi_ready, oT_lo_ready, w_ready, x_ready, stored) = (
            ctx.enter_context(nc.semaphore("l3_" + n)) for n in (
                'normed', 'biased', 't_ready', 'hT_hi_ready', 'hT_lo_ready', 'q_ready', 'qT_ready', 'k_ready',
                'kT_ready', 'v_ready', 'v_taken', 's_ready', 'masked', 'top_ready', 'shifted', 'prob_ready',
                'pt_ready', 'probT_ready', 'pv_ready', 'rtotal_ready', 'o_ready', 'ot_ready', 'oT_hi_ready',
                'oT_lo_ready', 'w_ready', 'x_ready', 'stored'))
        block = ctx.enter_context(nc.Block())
        flat = lambda ap: ap.rearrange("p a b -> p (a b)")

        def over_turns(eng, turn):
            turn(0, 0)
            turn(0, 1)
            with eng.Fori(1, G - 1) as g:
                turn(g, 0)
                turn(g, 1)
            turn(G - 1, 0)
            turn(G - 1, 1)

        def coming(g, e):
            return (g, 1) if e == 0 else (g + 1, 0) if exists(g + 1) else None

        @block.tensor
        def _(pe):
            def turn_tokens(g):
                pe.wait_ge(normed, g * GB + GB)
                need(pe, probT_ready, g * 2 * HR - HR)
                for k in range(C):
                    for b in range(GB):
                        last = pe.transpose(pT[k][:, b * N:b * N + N], xn[:, b, k * 128:k * 128 + 128], c.ident[:])
                    last.then_inc(t_ready, 1)

            def project(weight, ready):
                for co in range(C):
                    todo = [(k, wi, mi) for k in range(C) for wi, mi in ((0, 0), (0, 1), (1, 0))]
                    for n, (k, wi, mi) in enumerate(todo):
                        last = pe.matmul(pJ[co][:], weight[wi][:, k, co * 128:co * 128 + 128], hT[mi][:, k, :],
                                         start=(n == 0), stop=(n == len(todo) - 1))
                    last.then_inc(ready, 1)

            def queries_and_keys(g):
                pe.wait_ge(hT_hi_ready, g * C + C)
                pe.wait_ge(hT_lo_ready, g * C + C)
                need(pe, o_ready, (2 * g - 1) * UB)
                project(c.wq, q_ready)
                pe.wait_ge(qT_ready, g * C + C)
                project(c.wk, k_ready)

            def values(g):
                need(pe, o_ready, 2 * g * UB)
                for b in range(GB):
                    todo = [(k, wi, mi) for k in range(C) for wi, mi in ((0, 0), (0, 1), (1, 0))]
                    for n, (k, wi, mi) in enumerate(todo):
                        last = pe.matmul(pJ[b // 2][:, (b % 2) * D:(b % 2) * D + D], hT[mi][:, k, b * N:b * N + N],
                                         c.wv[wi][:, k, :], start=(n == 0), stop=(n == len(todo) - 1))
                    if b % 2:
                        last.then_inc(v_ready, 1)

            def scores(g, e):
                U = 2 * g + e
                pe.wait_ge(qT_ready, g * C + C)
                pe.wait_ge(kT_ready, g * C + C)
                need(pe, masked, U * HR)
                for b in range(UB):
                    for k in range(C):
                        for r in range(HR):
                            cols = slice((e * UB + b) * N, (e * UB + b) * N + N)
                            at = (b * C + k) * N
                            last = pe.matmul(pS[r][:, at:at + N], qT[r * HD:r * HD + HD, k, cols],
                                             kT[r * HD:r * HD + HD, k, cols], start=True, stop=True)
                            if b == UB - 1 and k == C - 1:
                                last.then_inc(s_ready, 1)

            def turn(g, e):
                U = 2 * g + e
                nxt = coming(g, e)
                if nxt:
                    scores(*nxt)
                need(pe, oT_lo_ready, U * C)
                if e == 1 and exists(g + 1):
                    pe.wait_ge(hT_lo_ready, (g + 1) * C + C)
                for r in range(HR):
                    pe.wait_ge(prob_ready, U * HR + r + 1)
                    if r >= 2:
                        pe.wait_ge(probT_ready, U * HR + r - 1)
                    for m in range(UB * C):
                        last = pe.transpose(pT[r % 2][:, m * N:m * N + N], prob[e][:, r, m, :], c.ident[:])
                    last.then_inc(pt_ready, 1)
                pe.wait_ge(probT_ready, U * HR + HR)
                pe.wait_ge(v_taken, g * 2 + 2)
                need(pe, x_ready, U)
                for b in range(UB):
                    for k in range(C):
                        for r in range(HR):
                            at, m = (k * HR + r) * (HD + 1), b * C + k
                            last = pe.matmul(pJ[b][:, at:at + HD + 1], probT[:, r, m * N:m * N + N],
                                             c.v_aug[:, e * UB + b, k * HR + r, :], start=True, stop=True)
                    last.then_inc(pv_ready, 1)
                if exists(g + 1):
                    if e == 0:
                        turn_tokens(g + 1)
                        queries_and_keys(g + 1)
                    else:
                        values(g + 1)
                pe.wait_ge(o_ready, (U + 1) * UB)
                pe.wait_ge(probT_ready, U * HR + HR)
                if exists(g + 1) and e == 0:
                    pe.wait_ge(hT_lo_ready, (g + 1) * C + C)
                for k in range(C):
                    for b in range(UB):
                        last = pe.transpose(pT[0][:, (k * UB + b) * N:(k * UB + b) * N + N],
                                            o[:, b, k * 128:k * 128 + 128], c.ident[:])
                last.then_inc(ot_ready, 1)
                pe.wait_ge(oT_hi_ready, U * C + C)
                pe.wait_ge(oT_lo_ready, U * C + C)
                if exists(g + 1):
                    if e == 0:
                        pe.wait_ge(kT_ready, (g + 1) * C + C)
                    else:
                        pe.wait_ge(v_taken, (g + 1) * 2 + 2)
                for b in range(UB):
                    todo = [(k, wi, mi) for k in range(C) for wi, mi in ((0, 0), (0, 1), (1, 0))]
                    for n, (k, wi, mi) in enumerate(todo):
                        last = pe.matmul(pJ[0][:, b * D:b * D + D], oT[mi][:, k, b * N:b * N + N], c.wo[wi][:, k, :],
                                         start=(n == 0), stop=(n == len(todo) - 1))
                last.then_inc(w_ready, 1)

            turn_tokens(0)
            queries_and_keys(0)
            pe.wait_ge(kT_ready, C)
            values(0)
            scores(0, 0)
            over_turns(pe, turn)

        @block.scalar
        def _(act):
            def take_tokens(g):
                for k in range(C):
                    act.wait_ge(t_ready, g * C + k + 1)
                    act.activation(hT[0][:, k, :], pT[k][:], ACT.Relu).then_inc(hT_hi_ready, 1)

            def take_queries_and_keys(g):
                for k in range(C):
                    act.wait_ge(q_ready, g * C + k + 1)
                    act.activation(qT[:, k, :], pJ[k][:], ACT.Identity, bias=c.bq[:, k:k + 1], scale=float(HD) ** -0.5
                                   ).then_inc(qT_ready, 1)
                for k in range(C):
                    act.wait_ge(k_ready, g * C + k + 1)
                    act.activation(kT[:, k, :], pJ[k][:], ACT.Identity, bias=c.bk[:, k:k + 1]).then_inc(kT_ready, 1)

            def take_values(g):
                for k in range(2):
                    act.wait_ge(v_ready, g * 2 + k + 1)
                    act.activation(c.v_aug[:, 2 * k:2 * k + 2, :, 0:HD].rearrange("p b h d -> p (b h) d"),
                                   pJ[k][:].rearrange("p (m d) -> p m d", d=HD), ACT.Copy).then_inc(v_taken, 1)

            def exponentials(g, e, heads):
                U = 2 * g + e
                for r in heads:
                    act.wait_ge(shifted, U * HR + r + 1)
                    act.activation(flat(prob[e][:, r]), flat(logit[:, r]), ACT.Exp).then_inc(prob_ready, 1)

            def turn(g, e):
                U = 2 * g + e
                nxt = coming(g, e)
                for r in range(HR):
                    act.wait_ge(pt_ready, U * HR + r + 1)
                    act.activation(probT[:, r, :], pT[r % 2][:], ACT.Copy).then_inc(probT_ready, 1)
                if exists(g + 1):
                    if e == 0:
                        take_tokens(g + 1)
                        take_queries_and_keys(g + 1)
                    else:
                        take_values(g + 1)
                if nxt:
                    exponentials(*nxt, range(2))
                act.wait_ge(ot_ready, U + 1)
                for k in range(C):
                    act.activation(oT[0][:, k, :], pT[0][:, k * UB * N:(k + 1) * UB * N], ACT.Identity,
                                   bias=c.bv[:, k:k + 1]).then_inc(oT_hi_ready, 1)
                if nxt:
                    exponentials(*nxt, range(2, HR))

            take_tokens(0)
            take_queries_and_keys(0)
            take_values(0)
            exponentials(0, 0, range(HR))
            over_turns(act, turn)

        @block.gpsimd
        def _(pool):
            def shift(g, e):
                U = 2 * g + e
                for r in range(HR):
                    pool.wait_ge(top_ready, U * HR + r + 1)
                    pool.tensor_tensor(logit[:, r], logit[:, r], bcast(top[:, r], N), ALU.subtract).then_inc(shifted, 1)

            def bias(g):
                pool.wait_ge(normed, g * GB + GB)
                xg = c.x[:, bass.ds(g * GB, GB), :]
                pool.tensor_tensor(xg, xg, bcast_mid(c.bias3[:], GB), ALU.add).then_inc(biased, 1)

            def turn(g, e):
                nxt = coming(g, e)
                if nxt:
                    shift(*nxt)
                if e == 0 and exists(g + 1):
                    bias(g + 1)

            bias(0)
            shift(0, 0)
            over_turns(pool, turn)

        @block.vector
        def _(dve):
            def norm(g):
                need(dve, t_ready, g * C)
                for b in range(GB):
                    i = g * GB + b
                    dve.tensor_scalar(xn[:, b, :], flat(c.x[:, bass.ds(i, 1), :]), c.rstd[:, bass.ds(i, 1)],
                                      c.nmr[:, bass.ds(i, 1)], ALU.mult, ALU.add).then_inc(normed, 1)

            def take_tokens(g):
                for k in range(C):
                    dve.wait_ge(hT_hi_ready, g * C + k + 1)
                    dve.scalar_tensor_tensor(hT[1][:, k, :], pT[k][:], 0.0, hT[0][:, k, :].bitcast(F32),
                                             ALU.max, ALU.subtract).then_inc(hT_lo_ready, 1)

            def mask_and_top(g, e):
                U = 2 * g + e
                for r in range(HR):
                    dve.wait_ge(s_ready, U * HR + r + 1)
                    need(dve, prob_ready, (U - 1) * HR + r + 1)
                    dve.tensor_tensor(logit[:, r], pS[r][:].rearrange("p (m n) -> p m n", n=N),
                                      bcast_mid(c.mask[:], UB * C), ALU.add).then_inc(masked, 1)
                for r in range(HR):
                    dve.wait_ge(masked, U * HR + r + 1)
                    dve.tensor_reduce(top[:, r], logit[:, r], AX.X, ALU.max).then_inc(top_ready, 1)

            def turn(g, e):
                U = 2 * g + e
                nxt = coming(g, e)
                if e == 0 and exists(g + 1):
                    norm(g + 1)
                if nxt:
                    mask_and_top(*nxt)
                for b in range(UB):
                    heads = pJ[b][:, 0:H * (HD + 1)].rearrange("p (h d) -> p h d", d=HD + 1)
                    dve.wait_ge(pv_ready, U * UB + b + 1)
                    dve.reciprocal(rtotal[:, b, :].unsqueeze(2), heads[:, :, HD:HD + 1]).then_inc(rtotal_ready, 1)
                for b in range(UB):
                    heads = pJ[b][:, 0:H * (HD + 1)].rearrange("p (h d) -> p h d", d=HD + 1)
                    dve.wait_ge(rtotal_ready, U * UB + b + 1)
                    need(dve, ot_ready, U)
                    dve.tensor_tensor(o[:, b, :].rearrange("p (h d) -> p h d", d=HD), heads[:, :, 0:HD],
                                      bcast(rtotal[:, b, :], HD), ALU.mult).then_inc(o_ready, 1)
                if e == 0 and exists(g + 1):
                    take_tokens(g + 1)
                dve.wait_ge(oT_hi_ready, U * C + C)
                for k in range(C):
                    dve.scalar_tensor_tensor(oT[1][:, k, :], pT[0][:, k * UB * N:(k + 1) * UB * N], c.bv[:, k:k + 1],
                                             oT[0][:, k, :].bitcast(F32), ALU.add, ALU.subtract).then_inc(oT_lo_ready, 1)
                dve.wait_ge(w_ready, U + 1)
                dve.wait_ge(biased, g + 1)
                xu = flat(c.x[:, bass.ds(g * GB + e * UB, UB), :])
                dve.tensor_tensor(xu, pJ[0][:], xu, ALU.add).then_inc(x_ready, 1)

            norm(0)
            take_tokens(0)
            mask_and_top(0, 0)
            over_turns(dve, turn)

        @block.sync
        def _(sp):
            with sp.Fori(0, 2 * G) as U:
                sp.wait_ge(x_ready, U + 1)
                sp.dma_start(out[bass.ds(U * UB, UB)].rearrange("b n d -> n b d"), c.x[:, bass.ds(U * UB, UB), :]
                             ).then_inc(stored, 16)
            sp.wait_ge(stored, 2 * G * 16)


def build(nc, t, out):
    c = Chip()
    with ExitStack() as ctx:
        c.x = ctx.enter_context(nc.sbuf_tensor("x_stream", [128, B, D], F32))
        sb = lambda n, s, d=F32: ctx.enter_context(nc.sbuf_tensor(n, s, d))
        pair = lambda n, s: (sb(n + "_hi", s, F32R), sb(n + "_lo", s, F32R))
        c.ident, c.adj, c.adjT, c.mask = (sb(n, [128, N]) for n in ("ident", "adj", "adjT", "mask"))
        c.adjT_s = pair("adjT", [128, N])
        c.eps, c.beta = sb("eps", [128, 1]), sb("beta", [128, 1])
        c.mv, c.mv_group = sb("mv", [128, B, 2]), sb("mv_group", [128, GB, 2])
        c.rstd, c.nmr = sb("rstd", [128, B]), sb("nmr", [128, B])
        c.W0, c.W1 = sb("W0", [128, C, D]), sb("W1", [128, C, D])
        c.wa_bc = sb("wa_bc", [128, 2, C, 128])
        c.bias1, c.bias3 = sb("bias1", [128, D]), sb("bias3", [128, D])
        c.w3, c.w4, c.w5, c.u3, c.u5 = (pair(n, [128, C, D]) for n in ("w3T", "w4T", "w5T", "u3T", "u5T"))
        c.wq, c.wk, c.wv, c.wo = (pair(n, [128, C, D]) for n in ("wq", "wk", "wv", "wo"))
        c.bz, c.br, c.bh, c.bq, c.bk, c.bv = (sb(n, [128, C]) for n in ("bz", "br", "bh", "bq", "bk", "bv"))
        c.v_aug = sb("v_aug", [128, GB, H, HD + 1])
        c.settled_dve, c.settled_pool = (ctx.enter_context(nc.semaphore(n)) for n in ("settled_dve", "settled_pool"))
        prepare(nc, t, c)
        norm_factors(nc, c, "0")
        layer0(nc, c)
        norm_factors(nc, c, "1")
        layer1(nc, c)
        norm_factors(nc, c, "2")
        layer2(nc, c)
        norm_factors(nc, c, "3")
        layer3(nc, c, out)


def kernel(**inputs):
    import concourse.bacc as bacc
    from concourse.bass_utils import run_bass_kernel_spmd
    nc = bacc.Bacc("TRN2", target_bir_lowering=False, num_devices=1)
    tensors, arrays = {}, {}
    for name in INPUTS:
        a = np.ascontiguousarray(inputs[name])
        arrays["in_" + name] = a
        tensors[name] = nc.dram_tensor("in_" + name, a.shape, mybir.dt.from_np(a.dtype), kind="ExternalInput").ap()
    out = nc.dram_tensor("out_0", (B, N, D), F32, kind="ExternalOutput").ap()
    build(nc, tensors, out)
    return run_bass_kernel_spmd(nc, [arrays], core_ids=[0]).results[0]["out_0"]
```

```python
import numpy as np
import concourse.bass as bass
from concourse import mybir
from contextlib import ExitStack

F32 = mybir.dt.float32
F32R = mybir.dt.float32r
ACT = mybir.ActivationFunctionType
ALU = mybir.AluOpType
AX = mybir.AxisListType

B, N, D = 64, 128, 256
GB = 4
G = B // GB
C = D // 128
TOK = GB * N
H, HD = 8, 32
HR = 128 // HD
EPS = 1e-5
STEPS = 3
NCHUNK = 8

INPUTS = ['x', 'adj', 'L0_gnn_W', 'L0_gnn_a', 'L0_gnn_beta', 'L1_gnn_weight', 'L1_gnn_bias',
          'L2_gnn_w3_w', 'L2_gnn_w3_b', 'L2_gnn_u3_w', 'L2_gnn_u3_b', 'L2_gnn_w4_w', 'L2_gnn_w4_b',
          'L2_gnn_w5_w', 'L2_gnn_w5_b', 'L2_gnn_u5_w', 'L2_gnn_u5_b', 'L3_gnn_Wq', 'L3_gnn_bq',
          'L3_gnn_Wk', 'L3_gnn_bk', 'L3_gnn_Wv', 'L3_gnn_bv', 'L3_gnn_Wo', 'L3_gnn_bo']


def need(eng, sem, value):
    if not isinstance(value, int) or value > 0:
        eng.wait_ge(sem, value)


def settle(eng, settled):
    eng.sem_inc(settled, 1)


def over_groups(eng, body, peel=2):
    for g in range(peel):
        body(g, g % 2)
    with eng.Fori(peel, G - peel, 2) as g:
        for p in range(2):
            body(g + p, p)
    for g in range(G - peel, G):
        body(g, g % 2)


def exists(g, end=G):
    return not isinstance(g, int) or g < end


def bcast(ap, n):
    return ap.unsqueeze(2).to_broadcast([ap.shape[0], ap.shape[1], n])


def bcast_mid(ap, n):
    return ap.unsqueeze(1).to_broadcast([ap.shape[0], n, ap.shape[1]])


class Chip:
    pass


def prepare(nc, t, c):
    with ExitStack() as ctx:
        sb = lambda n, s, d=F32: ctx.enter_context(nc.sbuf_tensor(n, s, d))
        sem = lambda n: ctx.enter_context(nc.semaphore(n))
        w_raw = {k: sb(f"raw_{k}", [128, C, 2 * D]) for k in ('w3', 'w4', 'w5')}
        u_raw = {k: sb(f"raw_{k}", [128, C, D]) for k in ('u3', 'u5')}
        sums = {k: sb(f"sum_{k}", [128, C, D]) for k in ('w3', 'w4', 'w5')}
        p_raw = {k: sb(f"raw_{k}", [128, C, D]) for k in ('Wq', 'Wk', 'Wv', 'Wo')}
        a_bc = sb("a_bc", [128, 2, D])
        wa_prod = sb("wa_prod", [128, 2, C, D])
        b_raw = {k: sb(f"raw_{k}", [128, C]) for k in ('w3_b', 'w4_b', 'w5_b', 'u3_b', 'u5_b', 'bq')}
        not_adj = sb("not_adj", [128, N])
        stats = sb("stats0", [128, B, 6])
        banks = [ctx.enter_context(nc.psum_tensor(f"prep_bank{i}", [128, 512], F32)) for i in range(8)]
        x_landed = [sem(f"x_landed{i}") for i in range(NCHUNK)]
        graph_landed, l0_landed, w2_landed, b2_landed, w3_landed, l3_landed = map(
            sem, ('graph_landed', 'l0_landed', 'w2_landed', 'b2_landed', 'w3_landed', 'l3_landed'))
        ident_zero, ident_ready, sums_ready, transposed, evacuated, split_hi, split_lo = map(
            sem, ('ident_zero', 'ident_ready', 'sums_ready', 'transposed', 'evacuated', 'split_hi', 'split_lo'))
        prod_ready, wa_ready, mask_half, stats_ready, fold, ones_ready = map(
            sem, ('prod_ready', 'wa_ready', 'mask_half', 'stats_ready', 'fold', 'ones_ready'))
        block = ctx.enter_context(nc.Block())
        per = B // NCHUNK
        n_graph, n_l0, n_w2, n_b2, n_w3, n_l3 = 1, 5, 5, 5, 4, 4

        @block.sync
        def _(sp):
            sp.dma_start(c.adj[:], t['adj']).then_inc(graph_landed, 16)
            rows = lambda w: w.rearrange("(c p) d -> p c d", p=128)
            column = lambda v: v.rearrange("(c p) -> p c", p=128)
            row = lambda v, k: v.rearrange("(a n) -> a n", a=1).to_broadcast([128, k])
            for i in range(NCHUNK):
                sp.dma_start(c.x[:, i * per:(i + 1) * per, :],
                             t['x'][i * per:(i + 1) * per].rearrange("b n d -> n b d")
                             ).then_inc(x_landed[i], 16)
                if i == 1:
                    for k in ('w3', 'w4', 'w5'):
                        sp.dma_start(w_raw[k][:], rows(t[f'L2_gnn_{k}_w'])).then_inc(w2_landed, 16)
                    for k in ('u3', 'u5'):
                        sp.dma_start(u_raw[k][:], rows(t[f'L2_gnn_{k}_w'])).then_inc(w2_landed, 16)
                if i == 3:
                    sp.dma_start(c.W0[:], rows(t['L0_gnn_W'])).then_inc(l0_landed, 16)
                    sp.dma_start(c.W1[:], rows(t['L1_gnn_weight'])).then_inc(l0_landed, 16)
                    sp.dma_start(a_bc[:].rearrange("p a b -> p (a b)"),
                                 row(t['L0_gnn_a'].rearrange("n a -> (n a)"), 2 * D)).then_inc(l0_landed, 16)
                    sp.dma_start(c.beta[:], row(t['L0_gnn_beta'], 1)).then_inc(l0_landed, 16)
                    sp.dma_start(c.bias1[:], row(t['L1_gnn_bias'], D)).then_inc(l0_landed, 16)
                if i == 5:
                    for k in ('Wq', 'Wk', 'Wv', 'Wo'):
                        sp.dma_start(p_raw[k][:], rows(t[f'L3_gnn_{k}'])).then_inc(w3_landed, 16)
            for k in ('w3', 'w4', 'w5', 'u3', 'u5'):
                sp.dma_start(b_raw[k + '_b'][:], column(t[f'L2_gnn_{k}_b']),
                             allow_slow_non_contiguous=True).then_inc(b2_landed, 16)
            sp.dma_start(b_raw['bq'][:], column(t['L3_gnn_bq']), allow_slow_non_contiguous=True).then_inc(l3_landed, 16)
            sp.dma_start(c.bk[:], column(t['L3_gnn_bk']), allow_slow_non_contiguous=True).then_inc(l3_landed, 16)
            sp.dma_start(c.bv[:], column(t['L3_gnn_bv']), allow_slow_non_contiguous=True).then_inc(l3_landed, 16)
            sp.dma_start(c.bias3[:], row(t['L3_gnn_bo'], D)).then_inc(l3_landed, 16)

        order = [('w3', c.w3), ('w4', c.w4), ('w5', c.w5), ('u3', c.u3), ('u5', c.u5)]

        @block.gpsimd
        def _(pool):
            pool.memset(c.ident[:], 0.0).then_inc(ident_zero, 1)
            pool.memset(c.v_aug[:], 1.0).then_inc(ones_ready, 1)
            pool.memset(c.eps[:], EPS).then_inc(ones_ready, 1)
            pool.wait_ge(ident_zero, 1)
            pool.affine_select(out=c.ident[:], in_=c.ident[:], compare_op=ALU.not_equal, fill=1.0,
                               base=0, pattern=[[-1, N]], channel_multiplier=1).then_inc(ident_ready, 1)
            pool.wait_ge(w2_landed, 16 * n_w2)
            for k in ('w3', 'w4', 'w5'):
                pool.tensor_tensor(sums[k][:], w_raw[k][:, :, 0:D], w_raw[k][:, :, D:2 * D],
                                   ALU.add).then_inc(sums_ready, 1)
            pool.wait_ge(sums_ready, 3)
            pool.tensor_tensor(sums['w3'][:], sums['w3'][:], sums['w4'][:], ALU.subtract).then_inc(sums_ready, 1)
            pool.wait_ge(l0_landed, 16 * n_l0)
            for k in range(2):
                pool.tensor_tensor(wa_prod[:, k], c.W0[:], bcast_mid(a_bc[:, k, :], C), ALU.mult).then_inc(prod_ready, 1)
            for n, (k, (hi, lo)) in enumerate(zip(('Wq', 'Wk', 'Wv', 'Wo'), (c.wq, c.wk, c.wv, c.wo))):
                pool.wait_ge(split_hi, len(order) + n + 1)
                pool.tensor_tensor(lo[:], p_raw[k][:], hi[:].bitcast(F32), ALU.subtract).then_inc(split_lo, 1)
            pool.wait_ge(b2_landed, 16 * n_b2)
            pool.tensor_tensor(c.bz[:], b_raw['w3_b'][:], b_raw['u3_b'][:], ALU.add).then_inc(fold, 1)
            pool.tensor_tensor(c.br[:], b_raw['w4_b'][:], b_raw['u3_b'][:], ALU.add).then_inc(fold, 1)
            pool.tensor_tensor(c.bh[:], b_raw['w5_b'][:], b_raw['u5_b'][:], ALU.add).then_inc(fold, 1)

        @block.tensor
        def _(pe):
            pe.wait_ge(ident_ready, 1)
            pe.wait_ge(graph_landed, 16)
            pe.transpose(banks[7][:, 0:N], c.adj[:], c.ident[:]).then_inc(transposed, 1)
            pe.wait_ge(sums_ready, 4)
            pe.wait_ge(w2_landed, 16 * n_w2)
            for n, (k, _) in enumerate(order):
                src = sums.get(k, u_raw.get(k))
                for ci in range(C):
                    for co in range(C):
                        last = pe.transpose(banks[n][:, ci * D + co * 128:ci * D + co * 128 + 128],
                                            src[:, co, ci * 128:ci * 128 + 128], c.ident[:])
                last.then_inc(transposed, 1)

        @block.scalar
        def _(act):
            act.wait_ge(transposed, 1)
            act.activation(c.adjT[:], banks[7][:, 0:N], ACT.Copy).then_inc(evacuated, 1)
            for n, (_, (hi, lo)) in enumerate(order):
                act.wait_ge(transposed, n + 2)
                act.activation(hi[:].rearrange("p c d -> p (c d)"), banks[n][:], ACT.Copy).then_inc(split_hi, 1)
            act.wait_ge(w3_landed, 16 * n_w3)
            for k, (hi, lo) in zip(('Wq', 'Wk', 'Wv', 'Wo'), (c.wq, c.wk, c.wv, c.wo)):
                act.activation(hi[:], p_raw[k][:], ACT.Copy).then_inc(split_hi, 1)
            act.wait_ge(l3_landed, 16 * n_l3)
            act.mul(c.bq[:], b_raw['bq'][:], float(HD) ** -0.5).then_inc(evacuated, 1)

        @block.vector
        def _(dve):
            dve.wait_ge(graph_landed, 16 * n_graph)
            dve.tensor_scalar(not_adj[:], c.adj[:], -1.0, 1.0, ALU.mult, ALU.add).then_inc(mask_half, 1)
            dve.wait_ge(mask_half, 1)
            dve.tensor_scalar(c.mask[:], not_adj[:], -1e9, None, ALU.mult).then_inc(mask_half, 1)
            for i in range(NCHUNK):
                dve.wait_ge(x_landed[i], 16)
                for b in range(i * per, (i + 1) * per):
                    dve.bn_stats(stats[:, b, :], c.x[:, b, :]).then_inc(stats_ready, 1)
                dve.wait_ge(stats_ready, (i + 1) * per)
                for b in range(i * per, (i + 1) * per):
                    dve.bn_aggr(c.mv[:, b, :], stats[:, b, :]).then_inc(fold, 1)
                if i == NCHUNK - 3:
                    for n, (_, (hi, lo)) in enumerate(order):
                        dve.wait_ge(split_hi, n + 1)
                        dve.tensor_tensor(lo[:].rearrange("p c d -> p (c d)"), banks[n][:],
                                          hi[:].bitcast(F32).rearrange("p c d -> p (c d)"), ALU.subtract
                                          ).then_inc(split_lo, 1)
                    dve.wait_ge(prod_ready, 2)
                    dve.tensor_reduce(c.wa[:], wa_prod[:], AX.X, ALU.add).then_inc(wa_ready, 1)


def norm_factors(nc, c, tag):
    with ExitStack() as ctx:
        sb = lambda n: ctx.enter_context(nc.sbuf_tensor(f"{n}{tag}", [128, B], F32))
        sem = lambda n: ctx.enter_context(nc.semaphore(f"{n}{tag}"))
        ve, root, inv, mean_half = sb("ve"), sb("root"), sb("inv"), sb("half")
        root_ready, step = sem("root_ready"), sem("norm_step")
        block = ctx.enter_context(nc.Block())

        @block.scalar
        def _(act):
            act.activation(root[:], c.mv[:, :, 1], ACT.Sqrt, bias=c.eps[:]).then_inc(root_ready, 1)

        @block.vector
        def _(dve):
            dve.tensor_scalar(ve[:], c.mv[:, :, 1], EPS, None, ALU.add).then_inc(step, 1)
            dve.wait_ge(root_ready, 1)
            dve.reciprocal(inv[:], root[:]).then_inc(step, 1)
            dve.wait_ge(step, 2)
            dve.tensor_tensor(mean_half[:], ve[:], inv[:], ALU.mult).then_inc(step, 1)
            dve.wait_ge(step, 3)
            dve.tensor_tensor(ve[:], mean_half[:], root[:], ALU.add).then_inc(step, 1)
            dve.wait_ge(step, 4)
            dve.tensor_scalar(root[:], ve[:], 0.5, None, ALU.mult).then_inc(step, 1)
            dve.wait_ge(step, 5)
            dve.reciprocal(c.rstd[:], root[:]).then_inc(step, 1)
            dve.wait_ge(step, 6)
            dve.scalar_tensor_tensor(c.nmr[:], c.mv[:, :, 0], -1.0, c.rstd[:], ALU.mult, ALU.mult).then_inc(step, 1)


def group_stats(dve, c, g, stats, x_ready, x_count, stats_ready, aggregated, mv_ready):
    dve.wait_ge(x_ready, x_count)
    settle(dve, c.settled_dve)
    for b in range(GB):
        dve.bn_stats(stats[:, b, :], c.x[:, bass.ds(g * GB + b, 1), :].rearrange("p a d -> p (a d)")
                     ).then_inc(stats_ready, 1)
    dve.wait_ge(stats_ready, g * GB + GB)
    need(dve, mv_ready, g)
    settle(dve, c.settled_dve)
    for b in range(GB):
        dve.bn_aggr(c.mv_group[:, b, :], stats[:, b, :]).then_inc(aggregated, 1)
    dve.wait_ge(aggregated, g * GB + GB)
    settle(dve, c.settled_dve)
    dve.tensor_copy(c.mv[:, bass.ds(g * GB, GB), :], c.mv_group[:]).then_inc(mv_ready, 1)


def layer0(nc, c):
    with ExitStack() as ctx:
        sb = lambda n, s, d=F32: ctx.enter_context(nc.sbuf_tensor("l0_" + n, s, d))
        sem = lambda n: ctx.enter_context(nc.semaphore("l0_" + n))
        bank = lambda n: ctx.enter_context(nc.psum_tensor("l0_" + n, [128, 512], F32))
        xn = [sb(f"xn{p}", [128, GB, D]) for p in range(2)]
        hT = [sb(f"hT{p}", [128, C, TOK]) for p in range(2)]
        hw = [sb(f"hw{p}", [128, GB, D]) for p in range(2)]
        bhw = [sb(f"bhw{p}", [128, GB, D]) for p in range(2)]
        leak, e, prob = sb("leak", [128, GB, N]), sb("e", [128, GB, N]), sb("prob", [128, GB, N])
        probT = sb("probT", [128, TOK])
        rows_a, rows_b = sb("rows_a", [2, TOK]), sb("rows_b", [2, TOK])
        top, total, rtotal = sb("top", [128, GB]), sb("total", [128, GB]), sb("rtotal", [128, GB])
        u, low, ex = sb("u", [128, GB, D]), sb("low", [128, GB, D]), sb("ex", [128, GB, D])
        stats = sb("stats", [128, GB, 6])
        pT = [bank("pT0"), bank("pT1")]
        pW = [bank("pW0"), bank("pW1")]
        pS, pP = bank("pS"), bank("pP")
        pO = [bank("pO0"), bank("pO1")]
        (normed, rows_ready, rows_taken, t_ready, hT_ready, s_ready, w_ready, hw_ready, bhw_ready, leak_ready, lrelu_ready, e_ready, top_ready,
         prob_ready, total_ready, rtotal_ready, pt_ready, probT_ready, o_ready, u_ready, low_ready, ex_ready,
         elu_ready, x_ready, stats_ready, aggregated, mv_ready) = map(sem, (
            'normed', 'rows_ready', 'rows_taken', 't_ready', 'hT_ready', 's_ready', 'w_ready', 'hw_ready', 'bhw_ready', 'leak_ready', 'lrelu_ready', 'e_ready',
            'top_ready', 'prob_ready', 'total_ready', 'rtotal_ready', 'pt_ready', 'probT_ready', 'o_ready',
            'u_ready', 'low_ready', 'ex_ready', 'elu_ready', 'x_ready', 'stats_ready', 'aggregated', 'mv_ready'))
        block = ctx.enter_context(nc.Block())

        @block.tensor
        def _(pe):
            def turn_tokens(g, p):
                pe.wait_ge(normed, g * GB + GB)
                need(pe, hT_ready, g * C)
                for k in range(C):
                    for b in range(GB):
                        last = pe.transpose(pT[k][:, b * N:b * N + N], xn[p][:, b, k * 128:k * 128 + 128], c.ident[:])
                    last.then_inc(t_ready, 1)

            def token_rows(g, p):
                pe.wait_ge(hT_ready, g * C + C)
                need(pe, lrelu_ready, g)
                for k in range(C):
                    last = pe.matmul(pS[0:2, :], c.wa[:, :, k], hT[p][:, k, :], start=(k == 0), stop=(k == C - 1))
                last.then_inc(rows_ready, 1)

            def scores(g):
                pe.wait_ge(rows_taken, g * 2 + 2)
                for b in range(GB):
                    cols = slice(b * N, b * N + N)
                    last = pe.matmul(pS[:, cols], rows_a[:, cols], rows_b[:, cols], start=True, stop=True)
                last.then_inc(s_ready, 1)

            def project(g, p):
                need(pe, hw_ready, g * 2)
                for b in range(GB):
                    for k in range(C):
                        last = pe.matmul(pW[b // 2][:, (b % 2) * D:(b % 2) * D + D], hT[p][:, k, b * N:b * N + N],
                                         c.W0[:, k, :], start=(k == 0), stop=(k == C - 1))
                    if b % 2:
                        last.then_inc(w_ready, 1)

            def turn_probs(g):
                pe.wait_ge(prob_ready, g * GB + GB)
                need(pe, probT_ready, g)
                for b in range(GB):
                    last = pe.transpose(pP[:, b * N:b * N + N], prob[:, b, :], c.ident[:])
                last.then_inc(pt_ready, 1)

            def attend(g, p):
                pe.wait_ge(probT_ready, g + 1)
                pe.wait_ge(hw_ready, g * 2 + 2)
                need(pe, u_ready, g * GB)
                for b in range(GB):
                    last = pe.matmul(pO[b // 2][:, (b % 2) * D:(b % 2) * D + D], probT[:, b * N:b * N + N],
                                     hw[p][:, b, :], start=True, stop=True)
                    if b % 2:
                        last.then_inc(o_ready, 1)

            def body(g, p):
                if exists(g + 1):
                    token_rows(g + 1, 1 - p)
                if exists(g + 2):
                    turn_tokens(g + 2, p)
                if exists(g + 1):
                    scores(g + 1)
                turn_probs(g)
                if exists(g + 1):
                    project(g + 1, 1 - p)
                attend(g, p)

            turn_tokens(0, 0)
            token_rows(0, 0)
            scores(0)
            turn_tokens(1, 1)
            project(0, 0)
            over_groups(pe, body)

        @block.scalar
        def _(act):
            def norm(g, p):
                need(act, t_ready, (g - 1) * C)
                for b in range(GB):
                    i = g * GB + b
                    act.activation(xn[p][:, b, :], c.x[:, bass.ds(i, 1), :].rearrange("p a d -> p (a d)"), ACT.Relu,
                                   bias=c.nmr[:, bass.ds(i, 1)], scale=c.rstd[:, bass.ds(i, 1)]).then_inc(normed, 1)

            def take_hT(g, p):
                for k in range(C):
                    act.wait_ge(t_ready, g * C + k + 1)
                    act.activation(hT[p][:, k, :], pT[k][:], ACT.Copy).then_inc(hT_ready, 1)

            def take_rows(g):
                act.wait_ge(rows_ready, g + 1)
                need(act, s_ready, g)
                for rows, one, other in ((rows_a, 0, 1), (rows_b, 1, 0)):
                    act.activation(rows[:], pS[0:2, :], ACT.Identity, scale=c.ident[0:2, one:one + 1],
                                   bias=c.ident[0:2, other:other + 1]).then_inc(rows_taken, 1)

            def take_scores(g):
                act.wait_ge(s_ready, g + 1)
                need(act, lrelu_ready, g)
                act.mul(leak[:].rearrange("p a b -> p (a b)"), pS[:], 0.2).then_inc(leak_ready, 1)

            def take_hw(g, p):
                need(act, o_ready, (g - 1) * 2)
                need(act, bhw_ready, g - 1)
                for k in range(2):
                    act.wait_ge(w_ready, g * 2 + k + 1)
                    act.activation(hw[p][:, 2 * k:2 * k + 2, :].rearrange("p a b -> p (a b)"), pW[k][:], ACT.Copy
                                   ).then_inc(hw_ready, 1)

            def take_probT(g):
                act.wait_ge(pt_ready, g + 1)
                need(act, o_ready, g * 2)
                act.activation(probT[:], pP[:], ACT.Copy).then_inc(probT_ready, 1)

            def probs(g):
                act.wait_ge(top_ready, g + 1)
                need(act, pt_ready, g)
                need(act, rtotal_ready, g)
                for b in range(GB):
                    act.activation(prob[:, b, :], e[:, b, :], ACT.Exp, bias=top[:, b:b + 1],
                                   accum_out=total[:, b:b + 1]).then_inc(prob_ready, 1)

            def elu_exp(g):
                act.wait_ge(low_ready, g + 1)
                need(act, elu_ready, g)
                act.activation(ex[:], low[:], ACT.Exp).then_inc(ex_ready, 1)

            def body(g, p):
                if exists(g + 1):
                    take_rows(g + 1)
                if exists(g + 2):
                    take_hT(g + 2, p)
                if exists(g + 1):
                    take_scores(g + 1)
                if not isinstance(g, int) or g > 0:
                    elu_exp(g - 1)
                take_probT(g)
                if exists(g + 3):
                    norm(g + 3, 1 - p)
                if exists(g + 1):
                    take_hw(g + 1, 1 - p)
                    probs(g + 1)

            norm(0, 0)
            norm(1, 1)
            take_hT(0, 0)
            take_rows(0)
            take_scores(0)
            take_hT(1, 1)
            norm(2, 0)
            take_hw(0, 0)
            probs(0)
            over_groups(act, body, peel=4)
            elu_exp(G - 1)

        @block.gpsimd
        def _(pool):
            def scale_hw(g, p):
                pool.wait_ge(hw_ready, g * 2 + 2)
                need(pool, u_ready, (g - 1) * GB)
                settle(pool, c.settled_pool)
                pool.tensor_scalar(bhw[p][:], hw[p][:], c.beta[:], None, ALU.mult).then_inc(bhw_ready, 1)

            def body(g, p):
                pool.wait_ge(u_ready, g * GB + GB)
                need(pool, ex_ready, g)
                settle(pool, c.settled_pool)
                pool.tensor_scalar(low[:], u[:], 0.0, None, ALU.min).then_inc(low_ready, 1)
                if exists(g + 1):
                    scale_hw(g + 1, 1 - p)
            scale_hw(0, 0)
            over_groups(pool, body)

        @block.vector
        def _(dve):
            flat = lambda ap: ap.rearrange("p a b -> p (a b)")

            def masked_scores(g):
                dve.wait_ge(leak_ready, g + 1)
                need(dve, prob_ready, g * GB)
                dve.tensor_tensor(flat(e[:]), pS[:], flat(leak[:]), ALU.max).then_inc(lrelu_ready, 1)
                dve.wait_ge(lrelu_ready, g + 1)
                dve.tensor_tensor(e[:], e[:], bcast_mid(c.adj[:], GB), ALU.mult).then_inc(e_ready, 1)
                dve.wait_ge(e_ready, g + 1)
                dve.tensor_reduce(top[:], e[:], AX.X, ALU.max, negate=True).then_inc(top_ready, 1)

            def combine(g, p):
                dve.wait_ge(prob_ready, g * GB + GB)
                need(dve, u_ready, g * GB)
                dve.reciprocal(rtotal[:], total[:]).then_inc(rtotal_ready, 1)
                dve.wait_ge(rtotal_ready, g + 1)
                dve.wait_ge(bhw_ready, g + 1)
                need(dve, low_ready, g)
                need(dve, elu_ready, g)
                for b in range(GB):
                    dve.wait_ge(o_ready, g * 2 + b // 2 + 1)
                    dve.scalar_tensor_tensor(u[:, b, :], pO[b // 2][:, (b % 2) * D:(b % 2) * D + D],
                                             rtotal[:, b:b + 1], bhw[p][:, b, :], ALU.mult, ALU.add
                                             ).then_inc(u_ready, 1)

            def residual(g):
                dve.wait_ge(ex_ready, g + 1)
                dve.wait_ge(u_ready, g * GB + GB)
                dve.scalar_tensor_tensor(flat(u[:]), flat(u[:]), 0.0, flat(ex[:]), ALU.max, ALU.add
                                         ).then_inc(elu_ready, 1)
                dve.wait_ge(elu_ready, g + 1)
                xg = flat(c.x[:, bass.ds(g * GB, GB), :])
                dve.scalar_tensor_tensor(xg, flat(u[:]), -1.0, xg, ALU.add, ALU.add).then_inc(x_ready, 1)

            def body(g, p):
                if exists(g + 1):
                    masked_scores(g + 1)
                if not isinstance(g, int) or g > 0:
                    residual(g - 1)
                combine(g, p)
                if not isinstance(g, int) or g > 0:
                    group_stats(dve, c, g - 1, stats, x_ready, g, stats_ready, aggregated, mv_ready)

            masked_scores(0)
            over_groups(dve, body)
            residual(G - 1)
            group_stats(dve, c, G - 1, stats, x_ready, G, stats_ready, aggregated, mv_ready)


def layer1(nc, c):
    with ExitStack() as ctx:
        sb = lambda n, s, d=F32: ctx.enter_context(nc.sbuf_tensor("l1_" + n, s, d))
        sem = lambda n: ctx.enter_context(nc.semaphore("l1_" + n))
        bank = lambda n: ctx.enter_context(nc.psum_tensor("l1_" + n, [128, 512], F32))
        h = [sb(f"h{p}", [128, GB, D]) for p in range(2)]
        yT = [sb(f"yT{p}", [128, C, TOK]) for p in range(2)]
        stats = sb("stats", [128, GB, 6])
        pY = [[bank(f"pY{p}{k}") for k in range(C)] for p in range(2)]
        pZ = [[bank(f"pZ{p}{k}") for k in range(2)] for p in range(2)]
        h_ready, biased, y_ready, yT_ready, z_ready, x_ready, stats_ready, aggregated, mv_ready = map(
            sem, ('h_ready', 'biased', 'y_ready', 'yT_ready', 'z_ready', 'x_ready', 'stats_ready', 'aggregated', 'mv_ready'))
        block = ctx.enter_context(nc.Block())

        @block.scalar
        def _(act):
            def body(g, p):
                need(act, y_ready, (g - 1) * C)
                for b in range(GB):
                    i = g * GB + b
                    act.activation(h[p][:, b, :], c.x[:, bass.ds(i, 1), :].rearrange("p a d -> p (a d)"), ACT.Relu,
                                   bias=c.nmr[:, bass.ds(i, 1)], scale=c.rstd[:, bass.ds(i, 1)]).then_inc(h_ready, 1)
            over_groups(act, body)

        @block.gpsimd
        def _(pool):
            def body(g, p):
                pool.wait_ge(h_ready, g * GB + GB)
                xg = c.x[:, bass.ds(g * GB, GB), :]
                pool.tensor_tensor(xg, xg, bcast_mid(c.bias1[:], GB), ALU.add).then_inc(biased, 1)
            over_groups(pool, body)

        @block.tensor
        def _(pe):
            def gather(g, p):
                pe.wait_ge(h_ready, g * GB + GB)
                need(pe, yT_ready, (g - 1) * C)
                for k in range(C):
                    for b in range(GB):
                        last = pe.matmul(pY[p][k][:, b * N:b * N + N], h[p][:, b, k * 128:k * 128 + 128], c.adjT[:],
                                         start=True, stop=True)
                    last.then_inc(y_ready, 1)

            def project(g, p):
                pe.wait_ge(yT_ready, g * C + C)
                need(pe, x_ready, (g - 1) * 2)
                for b in range(GB):
                    for k in range(C):
                        last = pe.matmul(pZ[p][b // 2][:, (b % 2) * D:(b % 2) * D + D], yT[p][:, k, b * N:b * N + N],
                                         c.W1[:, k, :], start=(k == 0), stop=(k == C - 1))
                    if b % 2:
                        last.then_inc(z_ready, 1)

            def body(g, p):
                if exists(g + 1):
                    gather(g + 1, 1 - p)
                project(g, p)
            gather(0, 0)
            over_groups(pe, body)

        @block.vector
        def _(dve):
            def take_y(g, p):
                need(dve, z_ready, (g - 1) * 2)
                for k in range(C):
                    dve.wait_ge(y_ready, g * C + k + 1)
                    dve.tensor_copy(yT[p][:, k, :], pY[p][k][:]).then_inc(yT_ready, 1)

            def body(g, p):
                if exists(g + 1):
                    take_y(g + 1, 1 - p)
                dve.wait_ge(biased, g + 1)
                for k in range(2):
                    dve.wait_ge(z_ready, g * 2 + k + 1)
                    xk = c.x[:, bass.ds(g * GB + 2 * k, 2), :].rearrange("p a b -> p (a b)")
                    dve.tensor_tensor(xk, pZ[p][k][:], xk, ALU.add).then_inc(x_ready, 1)
                group_stats(dve, c, g, stats, x_ready, g * 2 + 2, stats_ready, aggregated, mv_ready)
            take_y(0, 0)
            over_groups(dve, body)


def layer2(nc, c):
    PAIRS, TURNS = G // 2, 2 * STEPS
    with ExitStack() as ctx:
        sb = lambda n, s, d=F32: ctx.enter_context(nc.sbuf_tensor("l2_" + n, s, d))
        bank = lambda n: ctx.enter_context(nc.psum_tensor("l2_" + n, [128, 512], F32))
        nat = sb("nat", [128, GB, D])
        hT = [sb(f"hT{q}", [128, C, TOK]) for q in range(2)]
        hT_s = [[sb(f"hT_{n}{q}", [128, C, TOK], F32R) for n in ("hi", "lo")] for q in range(2)]
        aT = [sb(n, [128, C, TOK], F32R) for n in ("aT_hi", "aT_lo")]
        r, rsum, z, hv, rh, d = (sb(n, [128, C, TOK]) for n in ("r", "rsum", "z", "hv", "rh", "d"))
        rh_s = [sb(n, [128, C, TOK], F32R) for n in ("rh_hi", "rh_lo")]
        stats = sb("stats", [128, GB, 6])
        pR, pZ, pH, pT = ([bank(f"p{n}{k}") for k in range(C)] for n in "RZHT")
        (h0_ready, nat_ready, t_ready, hT0_ready, hT_hi_ready, hT_lo_ready, a_ready, a_hi_ready,
         a_lo_ready, r_ready, z_ready, hv_ready, r_sig, rsum_ready, zsum_ready, z_sig, hv_tanh, rh_ready, rh_hi_ready, rh_lo_ready, d_ready,
         zd_ready, new_h, f_ready, x_ready, stats_ready, aggregated, mv_ready) = (
            ctx.enter_context(nc.semaphore("l2_" + n)) for n in (
                'h0_ready', 'nat_ready', 't_ready', 'hT0_ready', 'hT_hi_ready', 'hT_lo_ready',
                'a_ready', 'a_hi_ready', 'a_lo_ready', 'r_ready', 'z_ready', 'hv_ready', 'r_sig', 'rsum_ready', 'zsum_ready', 'z_sig', 'hv_tanh',
                'rh_ready', 'rh_hi_ready', 'rh_lo_ready', 'd_ready', 'zd_ready', 'new_h', 'f_ready', 'x_ready',
                'stats_ready', 'aggregated', 'mv_ready'))
        block = ctx.enter_context(nc.Block())
        flat = lambda ap: ap.rearrange("p a b -> p (a b)")

        def over_turns(eng, turn):
            for pos in range(TURNS):
                turn(0, pos)
            with eng.Fori(1, PAIRS - 1) as j:
                for pos in range(TURNS):
                    turn(j, pos)
            for pos in range(TURNS):
                turn(PAIRS - 1, pos)

        def following(j, pos):
            if pos + 1 < TURNS:
                return j, pos + 1
            return None if isinstance(j, int) and j == PAIRS - 1 else (j + 1, 0)

        def preceding(j, pos):
            if pos:
                return j, pos - 1
            return None if isinstance(j, int) and j == 0 else (j - 1, TURNS - 1)

        def first_step(pos):
            return pos < 2

        def last_step(pos):
            return pos >= TURNS - 2

        def nats(j, pos):
            return (j * (TURNS - 2) + pos - 2) * 2

        @block.tensor
        def _(pe):
            def passes(out, weight, moving, co, first, last):
                todo = [(k, wi, mi) for k in range(C) for wi, mi in ((0, 0), (0, 1), (1, 0))]
                for n, (k, wi, mi) in enumerate(todo):
                    ins = pe.matmul(out[:], weight[wi][:, k, co * 128:co * 128 + 128], moving[mi][:, k, :],
                                    start=first and n == 0, stop=last and n == len(todo) - 1)
                return ins

            def back_to_nodes(q, ready):
                for half in range(2):
                    for b in (2 * half, 2 * half + 1):
                        for k in range(C):
                            at = (b % 2) * D + k * 128
                            last = pe.transpose(pT[half][:, at:at + 128], hT[q][:, k, b * N:b * N + N], c.ident[:])
                    last.then_inc(ready, 1)

            def turn_h(j, pos):
                K = j * TURNS + pos
                need(pe, a_lo_ready, K * C)
                if first_step(pos):
                    need(pe, x_ready, (2 * j - 1 + pos) * 2)
                    pe.wait_ge(h0_ready, (2 * j + pos + 1) * GB)
                    for k in range(C):
                        for b in range(GB):
                            last = pe.transpose(pT[k][:, b * N:b * N + N], nat[:, b, k * 128:k * 128 + 128], c.ident[:])
                        last.then_inc(t_ready, 1)
                else:
                    pe.wait_ge(new_h, (K - 1) * C)
                    back_to_nodes(pos % 2, t_ready)

            def gather(j, pos):
                K = j * TURNS + pos
                if not first_step(pos):
                    pe.wait_ge(nat_ready, nats(j, pos) + 2)
                if first_step(pos):
                    pe.wait_ge(hT0_ready, (2 * j + pos + 1) * C)
                    pe.wait_ge(hT_hi_ready, K * C + C)
                    pe.wait_ge(hT_lo_ready, K * C + C)
                for k in range(C):
                    for b in range(GB):
                        last = pe.matmul(pT[k][:, b * N:b * N + N], nat[:, b, k * 128:k * 128 + 128], c.adjT[:],
                                         start=True, stop=True)
                    last.then_inc(a_ready, 1)

            def final_h(K, q):
                pe.wait_ge(new_h, K * C)
                back_to_nodes(q, f_ready)

            def turn(j, pos):
                K = j * TURNS + pos
                nxt, prev = following(j, pos), preceding(j, pos)
                pe.wait_ge(hT_hi_ready, K * C + C)
                pe.wait_ge(hT_lo_ready, K * C + C)
                pe.wait_ge(a_hi_ready, K * C + C)
                pe.wait_ge(a_lo_ready, K * C + C)
                need(pe, r_sig, K * C)
                need(pe, rsum_ready, K * C)
                for co in range(C):
                    passes(pR[co], c.u3, hT_s[pos % 2], co, True, False)
                    passes(pR[co], c.w4, aT, co, False, True).then_inc(r_ready, 1)
                if prev and last_step(prev[1]):
                    final_h(K, prev[1] % 2)
                need(pe, zsum_ready, K * C)
                for co in range(C):
                    passes(pZ[co], c.w3, aT, co, True, True).then_inc(z_ready, 1)
                if nxt:
                    turn_h(*nxt)
                need(pe, hv_tanh, K * C)
                for co in range(C):
                    passes(pH[co], c.w5, aT, co, True, False)
                if nxt:
                    gather(*nxt)
                pe.wait_ge(rh_hi_ready, K * C + C)
                pe.wait_ge(rh_lo_ready, K * C + C)
                for co in range(C):
                    passes(pH[co], c.u5, rh_s, co, False, True).then_inc(hv_ready, 1)

            turn_h(0, 0)
            gather(0, 0)
            over_turns(pe, turn)
            pe.wait_ge(a_lo_ready, PAIRS * TURNS * C)
            pe.wait_ge(x_ready, (G - 1) * 2)
            final_h(PAIRS * TURNS, 1)

        @block.scalar
        def _(act):
            def make_h0(j, pos):
                K, g = j * TURNS + pos, 2 * j + pos
                need(act, a_ready, K * C)
                for b in range(GB):
                    i = g * GB + b
                    act.activation(nat[:, b, :], flat(c.x[:, bass.ds(i, 1), :]), ACT.Relu,
                                   bias=c.nmr[:, bass.ds(i, 1)], scale=c.rstd[:, bass.ds(i, 1)]).then_inc(h0_ready, 1)

            def take_turned(j, pos):
                K = j * TURNS + pos
                for k in range(2):
                    act.wait_ge(t_ready, K * 2 + k + 1)
                    if first_step(pos):
                        act.activation(hT[pos % 2][:, k, :], pT[k][:], ACT.Copy).then_inc(hT0_ready, 1)
                        act.activation(hT_s[pos % 2][0][:, k, :], pT[k][:], ACT.Copy).then_inc(hT_hi_ready, 1)
                    else:
                        act.activation(flat(nat[:, 2 * k:2 * k + 2, :]), pT[k][:], ACT.Copy).then_inc(nat_ready, 1)

            def take_gathered(j, pos):
                K = j * TURNS + pos
                for k in range(C):
                    act.wait_ge(a_ready, K * C + k + 1)
                    act.activation(aT[0][:, k, :], pT[k][:], ACT.Copy).then_inc(a_hi_ready, 1)

            def finish(j, pos):
                K = j * TURNS + pos
                need(act, d_ready, K)
                for co in range(C):
                    act.wait_ge(hv_ready, K * C + co + 1)
                    act.activation(hv[:, co, :], pH[co][:], ACT.Tanh, bias=c.bh[:, co:co + 1]).then_inc(hv_tanh, 1)

            def split_new_h(j, pos):
                K = j * TURNS + pos
                for k in range(C):
                    act.wait_ge(new_h, K * C + k + 1)
                    act.activation(hT_s[pos % 2][0][:, k, :], hT[pos % 2][:, k, :], ACT.Copy).then_inc(hT_hi_ready, 1)

            def turn(j, pos):
                K = j * TURNS + pos
                nxt, prev = following(j, pos), preceding(j, pos)
                if prev:
                    finish(*prev)
                if nxt and first_step(nxt[1]):
                    make_h0(*nxt)
                if prev and not last_step(prev[1]):
                    split_new_h(*prev)
                for co in range(C):
                    act.wait_ge(r_ready, K * C + co + 1)
                    act.activation(r[:, co, :], pR[co][:], ACT.Sigmoid, bias=c.br[:, co:co + 1]).then_inc(r_sig, 1)
                for co in range(C):
                    need(act, zsum_ready, K * C - C + co + 1)
                    act.activation(rsum[:, co, :], pR[co][:], ACT.Copy).then_inc(rsum_ready, 1)
                for co in range(C):
                    act.wait_ge(rh_ready, K * C + co + 1)
                    act.activation(rh_s[0][:, co, :], rh[:, co, :], ACT.Copy).then_inc(rh_hi_ready, 1)
                if nxt:
                    take_turned(*nxt)
                for co in range(C):
                    act.wait_ge(zsum_ready, K * C + co + 1)
                    act.activation(z[:, co, :], z[:, co, :], ACT.Sigmoid, bias=c.bz[:, co:co + 1]).then_inc(z_sig, 1)
                if nxt:
                    take_gathered(*nxt)

            make_h0(0, 0)
            take_turned(0, 0)
            take_gathered(0, 0)
            over_turns(act, turn)
            finish(PAIRS - 1, TURNS - 1)

        @block.vector
        def _(dve):
            def take_turned(j, pos):
                K = j * TURNS + pos
                if first_step(pos):
                    for k in range(C):
                        dve.wait_ge(hT_hi_ready, K * C + k + 1)
                        dve.tensor_tensor(hT_s[pos % 2][1][:, k, :], pT[k][:],
                                          hT_s[pos % 2][0][:, k, :].bitcast(F32), ALU.subtract).then_inc(hT_lo_ready, 1)

            def take_gathered(j, pos):
                K = j * TURNS + pos
                for k in range(C):
                    dve.wait_ge(a_hi_ready, K * C + k + 1)
                    dve.tensor_tensor(aT[1][:, k, :], pT[k][:], aT[0][:, k, :].bitcast(F32), ALU.subtract
                                      ).then_inc(a_lo_ready, 1)

            def finish(j, pos):
                K, q = j * TURNS + pos, pos % 2
                dve.wait_ge(hv_tanh, K * C + C)
                need(dve, zd_ready, K * C)
                dve.tensor_tensor(d[:], hv[:], hT[q][:], ALU.subtract).then_inc(d_ready, 1)
                dve.wait_ge(d_ready, K + 1)
                dve.wait_ge(z_sig, K * C + C)
                need(dve, new_h, K * C)
                for co in range(C):
                    dve.tensor_tensor(d[:, co, :], z[:, co, :], d[:, co, :], ALU.mult).then_inc(zd_ready, 1)
                for co in range(C):
                    dve.wait_ge(zd_ready, K * C + co + 1)
                    dve.tensor_tensor(hT[q][:, co, :], hT[q][:, co, :], d[:, co, :], ALU.add).then_inc(new_h, 1)
                if not last_step(pos):
                    for co in range(C):
                        dve.wait_ge(hT_hi_ready, (K + 2) * C + co + 1)
                        dve.tensor_tensor(hT_s[q][1][:, co, :], hT[q][:, co, :], hT_s[q][0][:, co, :].bitcast(F32),
                                          ALU.subtract).then_inc(hT_lo_ready, 1)

            def add_final(g):
                for half in range(2):
                    dve.wait_ge(f_ready, g * 2 + half + 1)
                    xh = flat(c.x[:, bass.ds(g * GB + 2 * half, 2), :])
                    dve.tensor_tensor(xh, pT[half][:], xh, ALU.add).then_inc(x_ready, 1)

            def turn(j, pos):
                K, q = j * TURNS + pos, pos % 2
                nxt, prev = following(j, pos), preceding(j, pos)
                if prev:
                    finish(*prev)
                for co in range(C):
                    dve.wait_ge(r_sig, K * C + co + 1)
                    dve.tensor_tensor(rh[:, co, :], r[:, co, :], hT[q][:, co, :], ALU.mult).then_inc(rh_ready, 1)
                if prev and last_step(prev[1]):
                    g = 2 * prev[0] + prev[1] % 2
                    add_final(g)
                for co in range(C):
                    dve.wait_ge(rh_hi_ready, K * C + co + 1)
                    dve.tensor_tensor(rh_s[1][:, co, :], rh[:, co, :], rh_s[0][:, co, :].bitcast(F32), ALU.subtract
                                      ).then_inc(rh_lo_ready, 1)
                if nxt:
                    take_turned(*nxt)
                for co in range(C):
                    dve.wait_ge(rsum_ready, K * C + co + 1)
                    dve.wait_ge(z_ready, K * C + co + 1)
                    dve.tensor_tensor(z[:, co, :], pZ[co][:], rsum[:, co, :], ALU.add).then_inc(zsum_ready, 1)
                if nxt:
                    take_gathered(*nxt)
                if prev and last_step(prev[1]):
                    group_stats(dve, c, g, stats, x_ready, g * 2 + 2, stats_ready, aggregated, mv_ready)

            take_turned(0, 0)
            take_gathered(0, 0)
            over_turns(dve, turn)
            finish(PAIRS - 1, TURNS - 1)
            add_final(G - 1)
            group_stats(dve, c, G - 1, stats, x_ready, G * 2, stats_ready, aggregated, mv_ready)


def layer3(nc, c, out):
    UB = GB // 2
    with ExitStack() as ctx:
        sb = lambda n, s, d=F32: ctx.enter_context(nc.sbuf_tensor("l3_" + n, s, d))
        bank = lambda n: ctx.enter_context(nc.psum_tensor("l3_" + n, [128, 512], F32))
        xn = sb("xn", [128, GB, D])
        hT = [sb(n, [128, C, TOK], F32R) for n in ("hT_hi", "hT_lo")]
        qT, kT = sb("qT", [128, C, TOK]), sb("kT", [128, C, TOK])
        logit = sb("logit", [128, HR, UB * C, N])
        prob = [sb(f"prob{e}", [128, HR, UB * C, N]) for e in range(2)]
        top = sb("top", [128, HR, UB * C])
        probT = sb("probT", [128, HR, UB * C * N])
        rtotal = sb("rtotal", [128, UB, H])
        o = sb("o", [128, UB, D])
        oT = [sb(n, [128, C, UB * N], F32R) for n in ("oT_hi", "oT_lo")]
        pS = [bank(f"pS{r}") for r in range(HR)]
        pT = [bank(f"pT{k}") for k in range(2)]
        pJ = [bank(f"pJ{k}") for k in range(2)]
        (normed, biased, t_ready, hT_hi_ready, hT_lo_ready, q_ready, qT_ready, k_ready, kT_ready, v_ready, v_taken,
         s_ready, masked, top_ready, shifted, prob_ready, pt_ready, probT_ready, pv_ready, rtotal_ready, o_ready,
         ot_ready, oT_hi_ready, oT_lo_ready, w_ready, x_ready, stored) = (
            ctx.enter_context(nc.semaphore("l3_" + n)) for n in (
                'normed', 'biased', 't_ready', 'hT_hi_ready', 'hT_lo_ready', 'q_ready', 'qT_ready', 'k_ready',
                'kT_ready', 'v_ready', 'v_taken', 's_ready', 'masked', 'top_ready', 'shifted', 'prob_ready',
                'pt_ready', 'probT_ready', 'pv_ready', 'rtotal_ready', 'o_ready', 'ot_ready', 'oT_hi_ready',
                'oT_lo_ready', 'w_ready', 'x_ready', 'stored'))
        block = ctx.enter_context(nc.Block())
        flat = lambda ap: ap.rearrange("p a b -> p (a b)")

        def over_turns(eng, turn):
            turn(0, 0)
            turn(0, 1)
            with eng.Fori(1, G - 1) as g:
                turn(g, 0)
                turn(g, 1)
            turn(G - 1, 0)
            turn(G - 1, 1)

        def coming(g, e):
            return (g, 1) if e == 0 else (g + 1, 0) if exists(g + 1) else None

        @block.tensor
        def _(pe):
            def turn_tokens(g):
                pe.wait_ge(normed, g * GB + GB)
                need(pe, probT_ready, (2 * g - 1) * HR)
                for k in range(C):
                    for b in range(GB):
                        last = pe.transpose(pT[k][:, b * N:b * N + N], xn[:, b, k * 128:k * 128 + 128], c.ident[:])
                    last.then_inc(t_ready, 1)

            def project(weight, ready, left, count):
                for co in range(C):
                    need(pe, left, count + co + 1)
                    todo = [(k, wi, mi) for k in range(C) for wi, mi in ((0, 0), (0, 1), (1, 0))]
                    for n, (k, wi, mi) in enumerate(todo):
                        last = pe.matmul(pJ[co][:], weight[wi][:, k, co * 128:co * 128 + 128], hT[mi][:, k, :],
                                         start=(n == 0), stop=(n == len(todo) - 1))
                    last.then_inc(ready, 1)

            def queries_and_keys(g):
                pe.wait_ge(hT_hi_ready, g * C + C)
                pe.wait_ge(hT_lo_ready, g * C + C)
                project(c.wq, q_ready, o_ready, (g - 1) * 2 * UB)
                project(c.wk, k_ready, qT_ready, g * C)

            def values(g):
                for b in range(GB):
                    if b % 2 == 0:
                        need(pe, o_ready, (2 * g - 1) * UB + b // 2 + 1)
                    todo = [(k, wi, mi) for k in range(C) for wi, mi in ((0, 0), (0, 1), (1, 0))]
                    for n, (k, wi, mi) in enumerate(todo):
                        last = pe.matmul(pJ[b // 2][:, (b % 2) * D:(b % 2) * D + D], hT[mi][:, k, b * N:b * N + N],
                                         c.wv[wi][:, k, :], start=(n == 0), stop=(n == len(todo) - 1))
                    if b % 2:
                        last.then_inc(v_ready, 1)

            def scores(g, e):
                U = 2 * g + e
                pe.wait_ge(qT_ready, g * C + C)
                pe.wait_ge(kT_ready, g * C + C)
                for r in range(HR):
                    need(pe, masked, (U - 1) * HR + r + 1)
                    for b in range(UB):
                        for k in range(C):
                            cols = slice((e * UB + b) * N, (e * UB + b) * N + N)
                            at = (b * C + k) * N
                            last = pe.matmul(pS[r][:, at:at + N], qT[r * HD:r * HD + HD, k, cols],
                                             kT[r * HD:r * HD + HD, k, cols], start=True, stop=True)
                    last.then_inc(s_ready, 1)

            def turn_outputs(U):
                pe.wait_ge(o_ready, (U + 1) * UB)
                for k in range(C):
                    for b in range(UB):
                        last = pe.transpose(pT[1][:, (k * UB + b) * N:(k * UB + b) * N + N],
                                            o[:, b, k * 128:k * 128 + 128], c.ident[:])
                last.then_inc(ot_ready, 1)

            def project_outputs(U):
                pe.wait_ge(oT_hi_ready, U * C + C)
                pe.wait_ge(oT_lo_ready, U * C + C)
                for b in range(UB):
                    todo = [(k, wi, mi) for k in range(C) for wi, mi in ((0, 0), (0, 1), (1, 0))]
                    for n, (k, wi, mi) in enumerate(todo):
                        last = pe.matmul(pJ[1][:, b * D:b * D + D], oT[mi][:, k, b * N:b * N + N], c.wo[wi][:, k, :],
                                         start=(n == 0), stop=(n == len(todo) - 1))
                last.then_inc(w_ready, 1)

            def probabilities(g, e, heads):
                U = 2 * g + e
                for r in heads:
                    pe.wait_ge(prob_ready, U * HR + r + 1)
                    if r == 1:
                        need(pe, oT_lo_ready, U * C)
                    if r >= 2:
                        pe.wait_ge(probT_ready, U * HR + r - 1)
                    for m in range(UB * C):
                        last = pe.transpose(pT[r % 2][:, m * N:m * N + N], prob[e][:, r, m, :], c.ident[:])
                    last.then_inc(pt_ready, 1)

            def attend(g, e, b):
                U = 2 * g + e
                for r in range(HR):
                    if b == 0:
                        pe.wait_ge(probT_ready, U * HR + r + 1)
                    for k in range(C):
                        at, m = (k * HR + r) * (HD + 1), b * C + k
                        last = pe.matmul(pJ[b][:, at:at + HD + 1], probT[:, r, m * N:m * N + N],
                                         c.v_aug[:, e * UB + b, k * HR + r, :], start=True, stop=True)
                last.then_inc(pv_ready, 1)

            def turn(g, e):
                U = 2 * g + e
                nxt = coming(g, e)
                later = not isinstance(g, int) or U > 0
                if later:
                    turn_outputs(U - 1)
                probabilities(g, e, (0,))
                if nxt:
                    scores(*nxt)
                probabilities(g, e, (1, 2))
                pe.wait_ge(v_taken, g * 2 + 2)
                if later:
                    project_outputs(U - 1)
                probabilities(g, e, (3,))
                attend(g, e, 0)
                if e == 0 and exists(g + 1):
                    turn_tokens(g + 1)
                need(pe, x_ready, U)
                attend(g, e, 1)
                if exists(g + 1):
                    if e == 0:
                        queries_and_keys(g + 1)
                    else:
                        values(g + 1)

            turn_tokens(0)
            queries_and_keys(0)
            pe.wait_ge(kT_ready, C)
            values(0)
            scores(0, 0)
            over_turns(pe, turn)
            turn_outputs(2 * G - 1)
            project_outputs(2 * G - 1)

        @block.scalar
        def _(act):
            def take_tokens(g):
                for k in range(C):
                    act.wait_ge(t_ready, g * C + k + 1)
                    act.activation(hT[0][:, k, :], pT[k][:], ACT.Relu).then_inc(hT_hi_ready, 1)

            def take_queries_and_keys(g):
                for k in range(C):
                    act.wait_ge(q_ready, g * C + k + 1)
                    act.activation(qT[:, k, :], pJ[k][:], ACT.Identity, bias=c.bq[:, k:k + 1], scale=float(HD) ** -0.5
                                   ).then_inc(qT_ready, 1)
                for k in range(C):
                    act.wait_ge(k_ready, g * C + k + 1)
                    act.activation(kT[:, k, :], pJ[k][:], ACT.Identity, bias=c.bk[:, k:k + 1]).then_inc(kT_ready, 1)

            def take_values(g):
                for k in range(2):
                    act.wait_ge(v_ready, g * 2 + k + 1)
                    act.activation(c.v_aug[:, 2 * k:2 * k + 2, :, 0:HD].rearrange("p b h d -> p (b h) d"),
                                   pJ[k][:].rearrange("p (m d) -> p m d", d=HD), ACT.Copy).then_inc(v_taken, 1)

            def take_outputs(U):
                act.wait_ge(ot_ready, U + 1)
                for k in range(C):
                    act.activation(oT[0][:, k, :], pT[1][:, k * UB * N:(k + 1) * UB * N], ACT.Identity,
                                   bias=c.bv[:, k:k + 1]).then_inc(oT_hi_ready, 1)

            def exponentials(g, e, heads):
                U = 2 * g + e
                for r in heads:
                    act.wait_ge(shifted, U * HR + r + 1)
                    act.activation(flat(prob[e][:, r]), flat(logit[:, r]), ACT.Exp).then_inc(prob_ready, 1)

            def turn(g, e):
                U = 2 * g + e
                nxt = coming(g, e)
                if not isinstance(g, int) or U > 0:
                    take_outputs(U - 1)
                for r in range(HR):
                    act.wait_ge(pt_ready, U * HR + r + 1)
                    act.activation(probT[:, r, :], pT[r % 2][:], ACT.Copy).then_inc(probT_ready, 1)
                if nxt:
                    exponentials(*nxt, range(2))
                if e == 0 and exists(g + 1):
                    take_tokens(g + 1)
                if nxt:
                    exponentials(*nxt, range(2, HR))
                if exists(g + 1):
                    if e == 0:
                        take_queries_and_keys(g + 1)
                    else:
                        take_values(g + 1)

            take_tokens(0)
            take_queries_and_keys(0)
            take_values(0)
            exponentials(0, 0, range(HR))
            over_turns(act, turn)
            take_outputs(2 * G - 1)

        @block.gpsimd
        def _(pool):
            def shift(g, e):
                U = 2 * g + e
                for r in range(HR):
                    pool.wait_ge(top_ready, U * HR + r + 1)
                    pool.tensor_tensor(logit[:, r], logit[:, r], bcast(top[:, r], N), ALU.subtract).then_inc(shifted, 1)

            def bias(g):
                pool.wait_ge(normed, g * GB + GB)
                xg = c.x[:, bass.ds(g * GB, GB), :]
                pool.tensor_tensor(xg, xg, bcast_mid(c.bias3[:], GB), ALU.add).then_inc(biased, 1)

            def turn(g, e):
                nxt = coming(g, e)
                if nxt:
                    shift(*nxt)
                if e == 0 and exists(g + 1):
                    bias(g + 1)

            bias(0)
            shift(0, 0)
            over_turns(pool, turn)

        @block.vector
        def _(dve):
            def norm(g):
                need(dve, t_ready, g * C)
                for b in range(GB):
                    i = g * GB + b
                    dve.tensor_scalar(xn[:, b, :], flat(c.x[:, bass.ds(i, 1), :]), c.rstd[:, bass.ds(i, 1)],
                                      c.nmr[:, bass.ds(i, 1)], ALU.mult, ALU.add).then_inc(normed, 1)

            def take_tokens(g):
                for k in range(C):
                    dve.wait_ge(hT_hi_ready, g * C + k + 1)
                    dve.scalar_tensor_tensor(hT[1][:, k, :], pT[k][:], 0.0, hT[0][:, k, :].bitcast(F32),
                                             ALU.max, ALU.subtract).then_inc(hT_lo_ready, 1)

            def mask_and_top(g, e):
                U = 2 * g + e

                def mask(r):
                    dve.wait_ge(s_ready, U * HR + r + 1)
                    need(dve, prob_ready, (U - 1) * HR + r + 1)
                    dve.tensor_tensor(logit[:, r], pS[r][:].rearrange("p (m n) -> p m n", n=N),
                                      bcast_mid(c.mask[:], UB * C), ALU.add).then_inc(masked, 1)

                mask(0)
                for r in range(HR):
                    if r + 1 < HR:
                        mask(r + 1)
                    dve.wait_ge(masked, U * HR + r + 1)
                    dve.tensor_reduce(top[:, r], logit[:, r], AX.X, ALU.max).then_inc(top_ready, 1)

            def outputs(U):
                for b in range(UB):
                    heads = pJ[b][:, 0:H * (HD + 1)].rearrange("p (h d) -> p h d", d=HD + 1)
                    dve.wait_ge(pv_ready, U * UB + b + 1)
                    dve.reciprocal(rtotal[:, b, :].unsqueeze(2), heads[:, :, HD:HD + 1]).then_inc(rtotal_ready, 1)
                    dve.wait_ge(rtotal_ready, U * UB + b + 1)
                    need(dve, ot_ready, U)
                    dve.tensor_tensor(o[:, b, :].rearrange("p (h d) -> p h d", d=HD), heads[:, :, 0:HD],
                                      bcast(rtotal[:, b, :], HD), ALU.mult).then_inc(o_ready, 1)

            def take_outputs(U):
                dve.wait_ge(oT_hi_ready, U * C + C)
                for k in range(C):
                    dve.scalar_tensor_tensor(oT[1][:, k, :], pT[1][:, k * UB * N:(k + 1) * UB * N], c.bv[:, k:k + 1],
                                             oT[0][:, k, :].bitcast(F32), ALU.add, ALU.subtract).then_inc(oT_lo_ready, 1)

            def add_outputs(U, at, g):
                dve.wait_ge(w_ready, U + 1)
                dve.wait_ge(biased, g + 1)
                xu = flat(c.x[:, bass.ds(at, UB), :])
                dve.tensor_tensor(xu, pJ[1][:], xu, ALU.add).then_inc(x_ready, 1)

            def turn(g, e):
                U = 2 * g + e
                nxt = coming(g, e)
                later = not isinstance(g, int) or U > 0
                if later:
                    take_outputs(U - 1)
                if nxt:
                    mask_and_top(*nxt)
                if e == 0 and exists(g + 1):
                    norm(g + 1)
                if later:
                    add_outputs(U - 1, (U - 1) * UB, g if e else g - 1)
                if e == 0 and exists(g + 1):
                    take_tokens(g + 1)
                outputs(U)

            norm(0)
            take_tokens(0)
            mask_and_top(0, 0)
            over_turns(dve, turn)
            take_outputs(2 * G - 1)
            add_outputs(2 * G - 1, (2 * G - 1) * UB, G - 1)

        @block.sync
        def _(sp):
            with sp.Fori(0, 2 * G) as U:
                sp.wait_ge(x_ready, U + 1)
                sp.dma_start(out[bass.ds(U * UB, UB)].rearrange("b n d -> n b d"), c.x[:, bass.ds(U * UB, UB), :]
                             ).then_inc(stored, 16)
            sp.wait_ge(stored, 2 * G * 16)


def build(nc, t, out):
    c = Chip()
    with ExitStack() as ctx:
        c.x = ctx.enter_context(nc.sbuf_tensor("x_stream", [128, B, D], F32))
        sb = lambda n, s, d=F32: ctx.enter_context(nc.sbuf_tensor(n, s, d))
        pair = lambda n, s: (sb(n + "_hi", s, F32R), sb(n + "_lo", s, F32R))
        c.ident, c.adj, c.adjT, c.mask = (sb(n, [128, N]) for n in ("ident", "adj", "adjT", "mask"))
        c.eps, c.beta = sb("eps", [128, 1]), sb("beta", [128, 1])
        c.mv, c.mv_group = sb("mv", [128, B, 2]), sb("mv_group", [128, GB, 2])
        c.rstd, c.nmr = sb("rstd", [128, B]), sb("nmr", [128, B])
        c.W0, c.W1 = sb("W0", [128, C, D]), sb("W1", [128, C, D])
        c.wa = sb("wa", [128, 2, C])
        c.bias1, c.bias3 = sb("bias1", [128, D]), sb("bias3", [128, D])
        c.w3, c.w4, c.w5, c.u3, c.u5 = (pair(n, [128, C, D]) for n in ("w3T", "w4T", "w5T", "u3T", "u5T"))
        c.wq, c.wk, c.wv, c.wo = (pair(n, [128, C, D]) for n in ("wq", "wk", "wv", "wo"))
        c.bz, c.br, c.bh, c.bq, c.bk, c.bv = (sb(n, [128, C]) for n in ("bz", "br", "bh", "bq", "bk", "bv"))
        c.v_aug = sb("v_aug", [128, GB, H, HD + 1])
        c.settled_dve, c.settled_pool = (ctx.enter_context(nc.semaphore(n)) for n in ("settled_dve", "settled_pool"))
        prepare(nc, t, c)
        norm_factors(nc, c, "0")
        layer0(nc, c)
        norm_factors(nc, c, "1")
        layer1(nc, c)
        norm_factors(nc, c, "2")
        layer2(nc, c)
        norm_factors(nc, c, "3")
        layer3(nc, c, out)


def kernel(**inputs):
    import concourse.bacc as bacc
    from concourse.bass_utils import run_bass_kernel_spmd
    nc = bacc.Bacc("TRN2", target_bir_lowering=False, num_devices=1)
    tensors, arrays = {}, {}
    for name in INPUTS:
        a = np.ascontiguousarray(inputs[name])
        arrays["in_" + name] = a
        tensors[name] = nc.dram_tensor("in_" + name, a.shape, mybir.dt.from_np(a.dtype), kind="ExternalInput").ap()
    out = nc.dram_tensor("out_0", (B, N, D), F32, kind="ExternalOutput").ap()
    build(nc, tensors, out)
    return run_bass_kernel_spmd(nc, [arrays], core_ids=[0]).results[0]["out_0"]
```

```python
import numpy as np
import concourse.bass as bass
from concourse import mybir
from contextlib import ExitStack

F32 = mybir.dt.float32
F32R = mybir.dt.float32r
ACT = mybir.ActivationFunctionType
ALU = mybir.AluOpType
AX = mybir.AxisListType

B, N, D = 64, 128, 256
GB = 4
G = B // GB
C = D // 128
TOK = GB * N
H, HD = 8, 32
HR = 128 // HD
EPS = 1e-5
AHEAD = 4
STEPS = 3

INPUTS = ['x', 'adj', 'L0_gnn_W', 'L0_gnn_a', 'L0_gnn_beta', 'L1_gnn_weight', 'L1_gnn_bias',
          'L2_gnn_w3_w', 'L2_gnn_w3_b', 'L2_gnn_u3_w', 'L2_gnn_u3_b', 'L2_gnn_w4_w', 'L2_gnn_w4_b',
          'L2_gnn_w5_w', 'L2_gnn_w5_b', 'L2_gnn_u5_w', 'L2_gnn_u5_b', 'L3_gnn_Wq', 'L3_gnn_bq',
          'L3_gnn_Wk', 'L3_gnn_bk', 'L3_gnn_Wv', 'L3_gnn_bv', 'L3_gnn_Wo', 'L3_gnn_bo']


def need(eng, sem, value):
    if not isinstance(value, int) or value > 0:
        eng.wait_ge(sem, value)


def settle(eng, settled):
    eng.sem_inc(settled, 1)


def over_groups(eng, body, peel=2):
    for g in range(peel):
        body(g, g % 2)
    with eng.Fori(peel, G - peel, 2) as g:
        for p in range(2):
            body(g + p, p)
    for g in range(G - peel, G):
        body(g, g % 2)


def exists(g, end=G):
    return not isinstance(g, int) or g < end


def bcast(ap, n):
    return ap.unsqueeze(2).to_broadcast([ap.shape[0], ap.shape[1], n])


def bcast_mid(ap, n):
    return ap.unsqueeze(1).to_broadcast([ap.shape[0], n, ap.shape[1]])


class Chip:
    pass


def rows_of(w):
    return w.rearrange("(c p) d -> p c d", p=128)


def column_of(v):
    return v.rearrange("(c p) -> p c", p=128)


def row_of(v, k):
    return v.rearrange("(a n) -> a n", a=1).to_broadcast([128, k])


def load_x(sp, t, c, g):
    sp.dma_start(c.x[:, g * GB:(g + 1) * GB, :],
                 t['x'][g * GB:(g + 1) * GB].rearrange("b n d -> n b d")).then_inc(c.x_landed[g], 16)


def prepare(nc, t, c):
    with ExitStack() as ctx:
        sb = lambda n, s, d=F32: ctx.enter_context(nc.sbuf_tensor(n, s, d))
        sem = lambda n: ctx.enter_context(nc.semaphore(n))
        a_bc = sb("a_bc", [128, 2, D])
        wa_prod = sb("wa_prod", [128, 2, C, D])
        not_adj = sb("not_adj", [128, N])
        bank = ctx.enter_context(nc.psum_tensor("prep_bank", [128, 512], F32))
        adj_landed, w_landed, cleared, ident_ready, transposed, evacuated, mask_half, prod_ready, wa_ready = map(sem, (
            'adj_landed', 'w_landed', 'cleared', 'ident_ready', 'transposed', 'evacuated', 'mask_half', 'prod_ready',
            'wa_ready'))
        block = ctx.enter_context(nc.Block())

        @block.sync
        def _(sp):
            load_x(sp, t, c, 0)
            sp.dma_start(c.adj[:], t['adj']).then_inc(adj_landed, 16)
            sp.dma_start(a_bc[:].rearrange("p a b -> p (a b)"),
                         row_of(t['L0_gnn_a'].rearrange("n a -> (n a)"), 2 * D)).then_inc(w_landed, 16)
            sp.dma_start(c.W0[:], rows_of(t['L0_gnn_W'])).then_inc(w_landed, 16)
            sp.dma_start(c.beta[:], row_of(t['L0_gnn_beta'], 1)).then_inc(w_landed, 16)
            for g in range(1, AHEAD):
                load_x(sp, t, c, g)

        @block.gpsimd
        def _(pool):
            pool.memset(c.ident[:], 0.0).then_inc(cleared, 1)
            pool.memset(c.eps[:], EPS).then_inc(cleared, 1)
            pool.memset(c.power[:], -0.5).then_inc(cleared, 1)
            pool.memset(c.minus[:], -1.0).then_inc(cleared, 1)
            pool.wait_ge(cleared, 1)
            pool.affine_select(out=c.ident[:], in_=c.ident[:], compare_op=ALU.not_equal, fill=1.0,
                               base=0, pattern=[[-1, N]], channel_multiplier=1).then_inc(ident_ready, 1)
            pool.memset(c.v_aug[:], 1.0).then_inc(cleared, 1)

        @block.tensor
        def _(pe):
            pe.wait_ge(ident_ready, 1)
            pe.wait_ge(adj_landed, 16)
            pe.transpose(bank[:, 0:N], c.adj[:], c.ident[:]).then_inc(transposed, 1)

        @block.scalar
        def _(act):
            act.wait_ge(transposed, 1)
            act.activation(c.adjT[:], bank[:, 0:N], ACT.Copy).then_inc(evacuated, 1)

        @block.vector
        def _(dve):
            dve.wait_ge(adj_landed, 16)
            dve.tensor_scalar(not_adj[:], c.adj[:], -1.0, 1.0, ALU.mult, ALU.add).then_inc(mask_half, 1)
            dve.wait_ge(mask_half, 1)
            dve.tensor_scalar(c.mask[:], not_adj[:], -1e9, None, ALU.mult).then_inc(mask_half, 1)
            dve.wait_ge(w_landed, 3 * 16)
            for k in range(2):
                dve.tensor_tensor(wa_prod[:, k], c.W0[:], bcast_mid(a_bc[:, k, :], C), ALU.mult).then_inc(prod_ready, 1)
            dve.wait_ge(prod_ready, 2)
            dve.tensor_reduce(c.wa[:], wa_prod[:], AX.X, ALU.add).then_inc(wa_ready, 1)


class Norm:

    def __init__(self, nc, ctx, tag):
        sb = lambda n, s: ctx.enter_context(nc.sbuf_tensor(tag + n, s, F32))
        sem = lambda n: ctx.enter_context(nc.semaphore(tag + n))
        self.stats, self.mv = sb("stats", [128, GB, 6]), sb("mv", [128, GB, 2])
        self.ve, self.neg = sb("ve", [128, GB]), sb("neg", [128, GB])
        self.stats_ready, self.aggregated, self.taken = sem("stats_ready"), sem("aggregated"), sem("taken")
        self.rstd_ready, self.factors_ready = sem("rstd_ready"), sem("factors_ready")


def norm_statistics(dve, c, norm, g):
    need(dve, norm.aggregated, g * GB)
    settle(dve, c.settled_dve)
    for b in range(GB):
        dve.bn_stats(norm.stats[:, b, :], c.x[:, bass.ds(g * GB + b, 1), :].rearrange("p a d -> p (a d)")
                     ).then_inc(norm.stats_ready, 1)


def norm_moments(dve, c, norm, g):
    dve.wait_ge(norm.stats_ready, g * GB + GB)
    need(dve, norm.taken, g * 2)
    settle(dve, c.settled_dve)
    for b in range(GB):
        dve.bn_aggr(norm.mv[:, b, :], norm.stats[:, b, :]).then_inc(norm.aggregated, 1)


def norm_factors(pool, c, norm, g):
    at = bass.ds(g * GB, GB)
    pool.wait_ge(norm.aggregated, g * GB + GB)
    need(pool, norm.factors_ready, g)
    pool.tensor_tensor(norm.ve[:], norm.mv[:, :, 1], c.eps[:], ALU.add).then_inc(norm.taken, 1)
    pool.tensor_tensor(norm.neg[:], norm.mv[:, :, 0], c.minus[:], ALU.mult).then_inc(norm.taken, 1)
    pool.wait_ge(norm.taken, g * 2 + 2)
    pool.tensor_tensor(c.rstd[:, at], norm.ve[:], c.power[:], ALU.pow).then_inc(norm.rstd_ready, 1)
    pool.wait_ge(norm.rstd_ready, g + 1)
    pool.tensor_tensor(c.nmr[:, at], norm.neg[:], c.rstd[:, at], ALU.mult).then_inc(norm.factors_ready, 1)


class Gather:

    def __init__(self, nc, ctx, banks_ctx):
        self.h = [ctx.enter_context(nc.sbuf_tensor(f"h{p}", [128, GB, D], F32)) for p in range(2)]
        self.banks = [banks_ctx.enter_context(nc.psum_tensor(f"y{k}", [128, 512], F32)) for k in range(C)]
        self.h_ready, self.y_ready = (ctx.enter_context(nc.semaphore("l1_" + n)) for n in ('h_ready', 'y_ready'))


def layer0(nc, t, c, gth):
    PEEL = AHEAD + 2
    with ExitStack() as ctx:
        sb = lambda n, s, d=F32: ctx.enter_context(nc.sbuf_tensor("l0_" + n, s, d))
        sem = lambda n: ctx.enter_context(nc.semaphore("l0_" + n))
        bank = lambda n: ctx.enter_context(nc.psum_tensor("l0_" + n, [128, 512], F32))
        xn = gth.h
        hT = [sb(f"hT{p}", [128, C, TOK]) for p in range(2)]
        hw = [sb(f"hw{p}", [128, GB, D]) for p in range(2)]
        bhw = [sb(f"bhw{p}", [128, GB, D]) for p in range(2)]
        leak, e, prob = sb("leak", [128, GB, N]), sb("e", [128, GB, N]), sb("prob", [128, GB, N])
        probT = sb("probT", [128, TOK])
        rows_a, rows_b = sb("rows_a", [2, TOK]), sb("rows_b", [2, TOK])
        top, total, rtotal = sb("top", [128, GB]), sb("total", [128, GB]), sb("rtotal", [128, GB])
        u, low, ex = sb("u", [128, GB, D]), sb("low", [128, GB, D]), sb("ex", [128, GB, D])
        w_raw = {k: sb(f"raw_{k}", [128, C, 2 * D]) for k in ('w3', 'w4', 'w5')}
        u_raw = {k: sb(f"raw_{k}", [128, C, D]) for k in ('u3', 'u5')}
        b_raw = {k: sb(f"raw_{k}", [128, C]) for k in ('w3_b', 'w4_b', 'w5_b', 'u3_b', 'u5_b', 'bq')}
        gated = [(u_raw['u3'], c.u3), (u_raw['u5'], c.u5), (w_raw['w5'], c.w5), (w_raw['w4'], c.w4),
                 (w_raw['w3'], c.w3)]
        straight = [('L3_gnn_Wq', c.wq), ('L3_gnn_Wk', c.wk), ('L3_gnn_Wv', c.wv), ('L3_gnn_Wo', c.wo),
                    ('L1_gnn_weight', c.W1)]
        straight_raw = [sb(k, [128, C, D]) for k, _ in straight]
        biases = 4 + len(b_raw)
        norm_in, norm_out = Norm(nc, ctx, "l0_in_"), Norm(nc, ctx, "l0_out_")
        pT = [bank("pT0"), bank("pT1")]
        pW = [bank("pW0"), bank("pW1")]
        pS, pP = gth.banks
        pO = [bank("pO0"), bank("pO1")]
        next_y = [pS, pP]
        turned = [pT[0], pT[1], pW[0], pW[1], pT[0]]
        (straight_landed, gated_landed, biases_landed, sums_ready, turned_ready, gated_hi, gated_lo, straight_hi,
         straight_lo, biases_ready, last_bhw_ready) = map(sem, (
            'straight_landed', 'gated_landed', 'biases_landed', 'sums_ready', 'turned_ready', 'gated_hi', 'gated_lo',
            'straight_hi', 'straight_lo', 'biases_ready', 'last_bhw_ready'))
        (normed, rows_ready, rows_taken, t_ready, hT_ready, s_ready, w_ready, hw_ready, bhw_ready, leak_ready,
         lrelu_ready, e_ready, top_ready,
         prob_ready, total_ready, rtotal_ready, pt_ready, probT_ready, o_ready, u_ready, low_ready, ex_ready,
         elu_ready, x_ready) = map(sem, (
            'normed', 'rows_ready', 'rows_taken', 't_ready', 'hT_ready', 's_ready', 'w_ready', 'hw_ready',
            'bhw_ready', 'leak_ready', 'lrelu_ready', 'e_ready',
            'top_ready', 'prob_ready', 'total_ready', 'rtotal_ready', 'pt_ready', 'probT_ready', 'o_ready',
            'u_ready', 'low_ready', 'ex_ready', 'elu_ready', 'x_ready'))
        block = ctx.enter_context(nc.Block())

        @block.sync
        def _(sp):
            for g in range(AHEAD, G):
                load_x(sp, t, c, g)
            for k, w in [*w_raw.items(), *u_raw.items()]:
                sp.dma_start(w[:], rows_of(t[f'L2_gnn_{k}_w'])).then_inc(gated_landed, 16)
            for (k, _), raw in zip(straight, straight_raw):
                sp.dma_start(raw[:], rows_of(t[k])).then_inc(straight_landed, 16)
            for k, v in b_raw.items():
                source = t['L3_gnn_bq'] if k == 'bq' else t[f'L2_gnn_{k}']
                sp.dma_start(v[:], column_of(source), allow_slow_non_contiguous=True).then_inc(biases_landed, 16)
            for k, v in (('bk', c.bk), ('bv', c.bv)):
                sp.dma_start(v[:], column_of(t[f'L3_gnn_{k}']), allow_slow_non_contiguous=True
                             ).then_inc(biases_landed, 16)
            sp.dma_start(c.bias1[:], row_of(t['L1_gnn_bias'], D)).then_inc(biases_landed, 16)
            sp.dma_start(c.bias3[:], row_of(t['L3_gnn_bo'], D)).then_inc(biases_landed, 16)

        @block.tensor
        def _(pe):
            def turn_tokens(g, p):
                pe.wait_ge(normed, g * GB + GB)
                need(pe, hT_ready, g * C)
                for k in range(C):
                    for b in range(GB):
                        last = pe.transpose(pT[k][:, b * N:b * N + N], xn[p][:, b, k * 128:k * 128 + 128], c.ident[:])
                    last.then_inc(t_ready, 1)

            def token_rows(g, p):
                pe.wait_ge(hT_ready, g * C + C)
                need(pe, lrelu_ready, g)
                for k in range(C):
                    last = pe.matmul(pS[0:2, :], c.wa[:, :, k], hT[p][:, k, :], start=(k == 0), stop=(k == C - 1))
                last.then_inc(rows_ready, 1)

            def scores(g):
                pe.wait_ge(rows_taken, g * 2 + 2)
                for b in range(GB):
                    cols = slice(b * N, b * N + N)
                    last = pe.matmul(pS[:, cols], rows_a[:, cols], rows_b[:, cols], start=True, stop=True)
                last.then_inc(s_ready, 1)

            def project(g, p):
                need(pe, hw_ready, g * 2)
                for b in range(GB):
                    for k in range(C):
                        last = pe.matmul(pW[b // 2][:, (b % 2) * D:(b % 2) * D + D], hT[p][:, k, b * N:b * N + N],
                                         c.W0[:, k, :], start=(k == 0), stop=(k == C - 1))
                    if b % 2:
                        last.then_inc(w_ready, 1)

            def turn_probs(g):
                pe.wait_ge(prob_ready, g * GB + GB)
                need(pe, probT_ready, g)
                for b in range(GB):
                    last = pe.transpose(pP[:, b * N:b * N + N], prob[:, b, :], c.ident[:])
                last.then_inc(pt_ready, 1)

            def attend(g, p):
                pe.wait_ge(probT_ready, g + 1)
                pe.wait_ge(hw_ready, g * 2 + 2)
                need(pe, u_ready, g * GB)
                for b in range(GB):
                    last = pe.matmul(pO[b // 2][:, (b % 2) * D:(b % 2) * D + D], probT[:, b * N:b * N + N],
                                     hw[p][:, b, :], start=True, stop=True)
                    if b % 2:
                        last.then_inc(o_ready, 1)

            def turn_weights(some):
                for n in some:
                    if n < 2:
                        pe.wait_ge(gated_landed, len(gated) * 16)
                        pe.wait_ge(hT_ready, G * C)
                    elif n < 4:
                        pe.wait_ge(sums_ready, 4)
                        pe.wait_ge(hw_ready, G * 2)
                    else:
                        pe.wait_ge(gated_lo, 1)
                    for ci in range(C):
                        for co in range(C):
                            at = ci * D + co * 128
                            last = pe.transpose(turned[n][:, at:at + 128], gated[n][0][:, co, ci * 128:ci * 128 + 128],
                                                c.ident[:])
                    last.then_inc(turned_ready, 1)

            def body(g, p):
                if exists(g + 1):
                    token_rows(g + 1, 1 - p)
                if exists(g + 2):
                    turn_tokens(g + 2, p)
                turn_probs(g)
                if exists(g + 1):
                    scores(g + 1)
                    project(g + 1, 1 - p)
                if isinstance(g, int) and g >= G - 2:
                    turn_weights((0, 1) if g == G - 2 else (2, 3))
                attend(g, p)

            turn_tokens(0, 0)
            token_rows(0, 0)
            scores(0)
            turn_tokens(1, 1)
            project(0, 0)
            over_groups(pe, body)
            turn_weights((4,))
            pe.wait_ge(gth.h_ready, GB)
            pe.wait_ge(lrelu_ready, G)
            pe.wait_ge(probT_ready, G)
            for k in range(C):
                for b in range(GB):
                    last = pe.matmul(next_y[k][:, b * N:b * N + N], gth.h[0][:, b, k * 128:k * 128 + 128], c.adjT[:],
                                     start=True, stop=True)
                last.then_inc(gth.y_ready, 1)

        @block.scalar
        def _(act):
            def norm(g, p):
                act.wait_ge(norm_in.factors_ready, g + 1)
                need(act, t_ready, (g - 1) * C)
                for b in range(GB):
                    i = g * GB + b
                    act.activation(xn[p][:, b, :], c.x[:, bass.ds(i, 1), :].rearrange("p a d -> p (a d)"), ACT.Relu,
                                   bias=c.nmr[:, bass.ds(i, 1)], scale=c.rstd[:, bass.ds(i, 1)]).then_inc(normed, 1)

            def take_hT(g, p):
                for k in range(C):
                    act.wait_ge(t_ready, g * C + k + 1)
                    act.activation(hT[p][:, k, :], pT[k][:], ACT.Copy).then_inc(hT_ready, 1)

            def take_rows(g):
                act.wait_ge(rows_ready, g + 1)
                need(act, s_ready, g)
                for rows, one, other in ((rows_a, 0, 1), (rows_b, 1, 0)):
                    act.activation(rows[:], pS[0:2, :], ACT.Identity, scale=c.ident[0:2, one:one + 1],
                                   bias=c.ident[0:2, other:other + 1]).then_inc(rows_taken, 1)

            def take_scores(g):
                act.wait_ge(s_ready, g + 1)
                need(act, lrelu_ready, g)
                act.mul(leak[:].rearrange("p a b -> p (a b)"), pS[:], 0.2).then_inc(leak_ready, 1)

            def take_hw(g, p):
                need(act, o_ready, (g - 1) * 2)
                need(act, bhw_ready, g - 1)
                for k in range(2):
                    act.wait_ge(w_ready, g * 2 + k + 1)
                    act.activation(hw[p][:, 2 * k:2 * k + 2, :].rearrange("p a b -> p (a b)"), pW[k][:], ACT.Copy
                                   ).then_inc(hw_ready, 1)

            def take_probT(g):
                act.wait_ge(pt_ready, g + 1)
                need(act, o_ready, g * 2)
                act.activation(probT[:], pP[:], ACT.Copy).then_inc(probT_ready, 1)

            def probs(g):
                act.wait_ge(top_ready, g + 1)
                need(act, pt_ready, g)
                need(act, rtotal_ready, g)
                for b in range(GB):
                    act.activation(prob[:, b, :], e[:, b, :], ACT.Exp, bias=top[:, b:b + 1],
                                   accum_out=total[:, b:b + 1]).then_inc(prob_ready, 1)

            def elu_exp(g):
                act.wait_ge(low_ready, g + 1)
                need(act, x_ready, g)
                act.activation(ex[:], low[:], ACT.Exp).then_inc(ex_ready, 1)

            def split_straight(n):
                act.wait_ge(straight_landed, len(straight) * 16)
                act.activation(straight[n][1][0][:], straight_raw[n][:], ACT.Copy).then_inc(straight_hi, 1)

            def take_weights(some):
                for n in some:
                    act.wait_ge(turned_ready, n + 1)
                    act.activation(gated[n][1][0][:].rearrange("p c d -> p (c d)"), turned[n][:], ACT.Copy
                                   ).then_inc(gated_hi, 1)

            def next_norm(g):
                act.wait_ge(t_ready, G * C)
                act.wait_ge(norm_out.factors_ready, g + 1)
                for b in range(GB):
                    i = g * GB + b
                    act.activation(gth.h[g][:, b, :], c.x[:, i, :], ACT.Relu, bias=c.nmr[:, i:i + 1],
                                   scale=c.rstd[:, i:i + 1]).then_inc(gth.h_ready, 1)

            def body(g, p):
                if exists(g + 1):
                    take_rows(g + 1)
                if exists(g + 2):
                    take_hT(g + 2, p)
                if exists(g + 1):
                    take_scores(g + 1)
                if not isinstance(g, int) or g > 0:
                    elu_exp(g - 1)
                take_probT(g)
                if exists(g + 3):
                    norm(g + 3, 1 - p)
                if exists(g + 1):
                    take_hw(g + 1, 1 - p)
                    if isinstance(g, int) and g == G - 2:
                        act.wait_ge(hw_ready, G * 2)
                        act.activation(bhw[1][:], hw[1][:], ACT.Copy, scale=c.beta[:]
                                       ).then_inc(last_bhw_ready, 1)
                    probs(g + 1)
                if isinstance(g, int) and g >= G - 4:
                    split_straight(g - G + 4)
                if isinstance(g, int) and g == G - 1:
                    split_straight(4)
                if isinstance(g, int) and g >= G - 2:
                    take_weights((0, 1) if g == G - 2 else (2, 3))

            norm(0, 0)
            norm(1, 1)
            take_hT(0, 0)
            take_rows(0)
            take_scores(0)
            take_hT(1, 1)
            norm(2, 0)
            take_hw(0, 0)
            probs(0)
            over_groups(act, body, peel=4)
            next_norm(0)
            elu_exp(G - 1)
            act.wait_ge(biases_landed, biases * 16)
            act.mul(c.bq[:], b_raw['bq'][:], float(HD) ** -0.5).then_inc(biases_ready, 1)
            take_weights((4,))
            next_norm(1)

        @block.gpsimd
        def _(pool):
            def scale_hw(g, p):
                pool.wait_ge(hw_ready, g * 2 + 2)
                need(pool, u_ready, (g - 1) * GB)
                pool.tensor_tensor(bhw[p][:], hw[p][:], bcast(c.beta[:].to_broadcast([128, GB]), D), ALU.mult
                                   ).then_inc(bhw_ready, 1)

            def low_straight(some):
                for n in some:
                    hi, lo = straight[n][1]
                    pool.wait_ge(straight_hi, n + 1)
                    pool.tensor_tensor(lo[:], straight_raw[n][:], hi[:].bitcast(F32), ALU.subtract
                                       ).then_inc(straight_lo, 1)

            def body(g, p):
                if exists(g, G - 2):
                    pool.wait_ge(u_ready, g * GB + GB)
                    need(pool, ex_ready, g)
                    settle(pool, c.settled_pool)
                    pool.tensor_scalar(low[:], u[:], 0.0, None, ALU.min).then_inc(low_ready, 1)
                if exists(g + AHEAD):
                    norm_factors(pool, c, norm_in, g + AHEAD)
                if exists(g + 1, G - 1):
                    scale_hw(g + 1, 1 - p)
                if isinstance(g, int) and g >= G - 2:
                    low_straight((0, 1, 2) if g == G - 2 else (3, 4))
                if not isinstance(g, int) or g > 0:
                    norm_factors(pool, c, norm_out, g - 1)
            for g in range(AHEAD):
                norm_factors(pool, c, norm_in, g)
            scale_hw(0, 0)
            over_groups(pool, body, peel=PEEL)
            pool.wait_ge(biases_landed, biases * 16)
            for out, one, other in ((c.bz, 'w3_b', 'u3_b'), (c.br, 'w4_b', 'u3_b'), (c.bh, 'w5_b', 'u5_b')):
                pool.tensor_tensor(out[:], b_raw[one][:], b_raw[other][:], ALU.add).then_inc(biases_ready, 1)
            norm_factors(pool, c, norm_out, G - 1)

        @block.vector
        def _(dve):
            flat = lambda ap: ap.rearrange("p a b -> p (a b)")

            def leaky_scores(g):
                dve.wait_ge(leak_ready, g + 1)
                need(dve, prob_ready, g * GB)
                dve.tensor_tensor(flat(e[:]), pS[:], flat(leak[:]), ALU.max).then_inc(lrelu_ready, 1)

            def mask_scores(g):
                dve.wait_ge(lrelu_ready, g + 1)
                dve.tensor_tensor(e[:], e[:], bcast_mid(c.adj[:], GB), ALU.mult).then_inc(e_ready, 1)

            def maxima(g):
                dve.wait_ge(e_ready, g + 1)
                dve.tensor_reduce(top[:], e[:], AX.X, ALU.max, negate=True).then_inc(top_ready, 1)

            def invert_totals(g):
                dve.wait_ge(prob_ready, g * GB + GB)
                need(dve, u_ready, g * GB)
                dve.reciprocal(rtotal[:], total[:]).then_inc(rtotal_ready, 1)

            def combine(g, p):
                dve.wait_ge(rtotal_ready, g + 1)
                if exists(g, G - 1):
                    dve.wait_ge(bhw_ready, g + 1)
                else:
                    dve.wait_ge(last_bhw_ready, 1)
                need(dve, low_ready, g)
                need(dve, elu_ready, g)
                for b in range(GB):
                    dve.wait_ge(o_ready, g * 2 + b // 2 + 1)
                    dve.scalar_tensor_tensor(u[:, b, :], pO[b // 2][:, (b % 2) * D:(b % 2) * D + D],
                                             rtotal[:, b:b + 1], bhw[p][:, b, :], ALU.mult, ALU.add
                                             ).then_inc(u_ready, 1)

            def clip(g):
                dve.wait_ge(u_ready, g * GB + GB)
                dve.wait_ge(ex_ready, g)
                dve.tensor_scalar(low[:], u[:], 0.0, None, ALU.min).then_inc(low_ready, 1)

            def sum_halves(k):
                w = w_raw[k]
                dve.wait_ge(gated_landed, len(gated) * 16)
                dve.tensor_tensor(w[:, :, 0:D], w[:, :, 0:D], w[:, :, D:2 * D], ALU.add).then_inc(sums_ready, 1)

            def low_weights(some):
                for n in some:
                    dve.wait_ge(gated_hi, n + 1)
                    hi, lo = gated[n][1]
                    dve.tensor_tensor(flat(lo[:]), turned[n][:], flat(hi[:].bitcast(F32)), ALU.subtract
                                      ).then_inc(gated_lo, 1)

            def elu(g):
                dve.wait_ge(ex_ready, g + 1)
                dve.wait_ge(u_ready, g * GB + GB)
                dve.scalar_tensor_tensor(flat(ex[:]), flat(u[:]), 0.0, flat(ex[:]), ALU.max, ALU.add
                                         ).then_inc(elu_ready, 1)

            def residual(g):
                dve.wait_ge(elu_ready, g + 1)
                xg = flat(c.x[:, bass.ds(g * GB, GB), :])
                dve.scalar_tensor_tensor(xg, flat(ex[:]), -1.0, xg, ALU.add, ALU.add).then_inc(x_ready, 1)

            def body(g, p):
                if exists(g + 1):
                    leaky_scores(g + 1)
                invert_totals(g)
                if exists(g + 1):
                    mask_scores(g + 1)
                if not isinstance(g, int) or g > 0:
                    elu(g - 1)
                if exists(g + 1):
                    maxima(g + 1)
                if not isinstance(g, int) or g > 0:
                    residual(g - 1)
                combine(g, p)
                if isinstance(g, int) and g >= G - 2:
                    clip(g)
                if exists(g + AHEAD):
                    if isinstance(g, int):
                        dve.wait_ge(c.x_landed[g + AHEAD], 16)
                    norm_statistics(dve, c, norm_in, g + AHEAD)
                if isinstance(g, int) and g == PEEL - 1:
                    for later in range(g + 1 + AHEAD, G):
                        dve.wait_ge(c.x_landed[later], 16)
                if not isinstance(g, int) or g > 0:
                    dve.wait_ge(x_ready, g)
                    norm_statistics(dve, c, norm_out, g - 1)
                if exists(g + AHEAD):
                    norm_moments(dve, c, norm_in, g + AHEAD)
                if not isinstance(g, int) or g > 0:
                    norm_moments(dve, c, norm_out, g - 1)
                if isinstance(g, int) and g == G - 4:
                    sum_halves('w3')
                    sum_halves('w4')
                elif isinstance(g, int) and g == G - 3:
                    sum_halves('w5')
                    dve.wait_ge(sums_ready, 2)
                    dve.tensor_tensor(w_raw['w3'][:, :, 0:D], w_raw['w3'][:, :, 0:D], w_raw['w4'][:, :, 0:D],
                                      ALU.subtract).then_inc(sums_ready, 1)
                elif isinstance(g, int) and g >= G - 2:
                    low_weights((0, 1) if g == G - 2 else (2, 3))

            for g in range(AHEAD):
                dve.wait_ge(c.x_landed[g], 16)
                norm_statistics(dve, c, norm_in, g)
                norm_moments(dve, c, norm_in, g)
            leaky_scores(0)
            mask_scores(0)
            maxima(0)
            over_groups(dve, body, peel=PEEL)
            elu(G - 1)
            residual(G - 1)
            dve.wait_ge(x_ready, G)
            norm_statistics(dve, c, norm_out, G - 1)
            norm_moments(dve, c, norm_out, G - 1)
            low_weights((4,))


class Gated:

    def __init__(self, nc, ctx):
        sb = lambda n, s, d=F32: ctx.enter_context(nc.sbuf_tensor("l2_" + n, s, d))
        self.nat = sb("nat", [128, GB, D])
        self.hT = [sb(f"hT{q}", [128, C, TOK]) for q in range(2)]
        self.hT_s = [[sb(f"hT_{n}{q}", [128, C, TOK], F32R) for n in ("hi", "lo")] for q in range(2)]
        self.aT = [sb(n, [128, C, TOK], F32R) for n in ("aT_hi", "aT_lo")]
        (self.h0_ready, self.t_ready, self.hT0_ready, self.hT_hi_ready, self.hT_lo_ready, self.a_ready,
         self.a_hi_ready, self.a_lo_ready) = (
            ctx.enter_context(nc.semaphore("l2_" + n)) for n in (
                'h0_ready', 't_ready', 'hT0_ready', 'hT_hi_ready', 'hT_lo_ready', 'a_ready', 'a_hi_ready',
                'a_lo_ready'))


def layer1(nc, c, gth, gat):
    with ExitStack() as ctx:
        sb = lambda n, s, d=F32: ctx.enter_context(nc.sbuf_tensor("l1_" + n, s, d))
        sem = lambda n: ctx.enter_context(nc.semaphore("l1_" + n))
        bank = lambda n: ctx.enter_context(nc.psum_tensor("l1_" + n, [128, 512], F32))
        h = gth.h
        yT = [[sb(f"yT_{n}{p}", [128, C, TOK], F32R) for n in ("hi", "lo")] for p in range(2)]
        norm = Norm(nc, ctx, "l1_")
        pY = [gth.banks, [bank(f"pY1{k}") for k in range(C)]]
        pZ = [[bank(f"pZ{p}{k}") for k in range(2)] for p in range(2)]
        h_ready, y_ready = gth.h_ready, gth.y_ready
        biased, y_hi_ready, y_lo_ready, z_ready, x_ready = map(sem, (
            'biased', 'y_hi_ready', 'y_lo_ready', 'z_ready', 'x_ready'))
        block = ctx.enter_context(nc.Block())

        @block.scalar
        def _(act):
            def take_y(g, p):
                need(act, z_ready, (g - 1) * 2)
                for k in range(C):
                    act.wait_ge(y_ready, g * C + k + 1)
                    act.activation(yT[p][0][:, k, :], pY[p][k][:], ACT.Copy).then_inc(y_hi_ready, 1)

            def normed(g, p):
                need(act, y_ready, (g - 1) * C)
                for b in range(GB):
                    i = g * GB + b
                    act.activation(h[p][:, b, :], c.x[:, bass.ds(i, 1), :].rearrange("p a d -> p (a d)"), ACT.Relu,
                                   bias=c.nmr[:, bass.ds(i, 1)], scale=c.rstd[:, bass.ds(i, 1)]).then_inc(h_ready, 1)

            def body(g, p):
                if exists(g + 2):
                    normed(g + 2, p)
                if exists(g + 1):
                    take_y(g + 1, 1 - p)

            take_y(0, 0)
            over_groups(act, body, peel=4)
            act.wait_ge(norm.factors_ready, 1)
            for b in range(GB):
                act.activation(gat.nat[:, b, :], c.x[:, b, :], ACT.Relu, bias=c.nmr[:, b:b + 1],
                               scale=c.rstd[:, b:b + 1]).then_inc(gat.h0_ready, 1)
            for k in range(C):
                act.wait_ge(gat.t_ready, k + 1)
                act.activation(gat.hT_s[0][0][:, k, :], pY[0][k][:], ACT.Copy).then_inc(gat.hT_hi_ready, 1)
            for k in range(C):
                act.activation(gat.hT[0][:, k, :], pY[0][k][:], ACT.Copy).then_inc(gat.hT0_ready, 1)
            for k in range(C):
                act.wait_ge(gat.a_ready, k + 1)
                act.activation(gat.aT[0][:, k, :], pZ[0][k][:], ACT.Copy).then_inc(gat.a_hi_ready, 1)

        @block.gpsimd
        def _(pool):
            def body(g, p):
                pool.wait_ge(h_ready, g * GB + GB)
                xg = c.x[:, bass.ds(g * GB, GB), :]
                pool.tensor_tensor(xg, xg, bcast_mid(c.bias1[:], GB), ALU.add).then_inc(biased, 1)
                if not isinstance(g, int) or g > 0:
                    norm_factors(pool, c, norm, g - 1)

            over_groups(pool, body)
            norm_factors(pool, c, norm, G - 1)

        @block.tensor
        def _(pe):
            def gather(g, p):
                pe.wait_ge(h_ready, g * GB + GB)
                need(pe, y_lo_ready, (g - 1) * C)
                for k in range(C):
                    for b in range(GB):
                        last = pe.matmul(pY[p][k][:, b * N:b * N + N], h[p][:, b, k * 128:k * 128 + 128], c.adjT[:],
                                         start=True, stop=True)
                    last.then_inc(y_ready, 1)

            def project(g, p):
                pe.wait_ge(y_hi_ready, g * C + C)
                pe.wait_ge(y_lo_ready, g * C + C)
                need(pe, x_ready, (g - 1) * 2)
                for b in range(GB):
                    todo = [(k, yi, wi) for k in range(C) for yi, wi in ((0, 0), (0, 1), (1, 0))]
                    for n, (k, yi, wi) in enumerate(todo):
                        last = pe.matmul(pZ[p][b // 2][:, (b % 2) * D:(b % 2) * D + D],
                                         yT[p][yi][:, k, b * N:b * N + N], c.W1[wi][:, k, :],
                                         start=(n == 0), stop=(n == len(todo) - 1))
                    if b % 2:
                        last.then_inc(z_ready, 1)

            def body(g, p):
                if exists(g + 1):
                    gather(g + 1, 1 - p)
                project(g, p)
            over_groups(pe, body)
            pe.wait_ge(gat.h0_ready, GB)
            for k in range(C):
                for b in range(GB):
                    last = pe.transpose(pY[0][k][:, b * N:b * N + N], gat.nat[:, b, k * 128:k * 128 + 128], c.ident[:])
                last.then_inc(gat.t_ready, 1)
            pe.wait_ge(x_ready, (G - 1) * 2)
            for k in range(C):
                for b in range(GB):
                    last = pe.matmul(pZ[0][k][:, b * N:b * N + N], gat.nat[:, b, k * 128:k * 128 + 128], c.adjT[:],
                                     start=True, stop=True)
                last.then_inc(gat.a_ready, 1)

        @block.vector
        def _(dve):
            def take_y(g, p):
                for k in range(C):
                    dve.wait_ge(y_hi_ready, g * C + k + 1)
                    dve.tensor_tensor(yT[p][1][:, k, :], pY[p][k][:], yT[p][0][:, k, :].bitcast(F32), ALU.subtract
                                      ).then_inc(y_lo_ready, 1)

            def body(g, p):
                if exists(g + 1):
                    take_y(g + 1, 1 - p)
                dve.wait_ge(biased, g + 1)
                for k in range(2):
                    dve.wait_ge(z_ready, g * 2 + k + 1)
                    xk = c.x[:, bass.ds(g * GB + 2 * k, 2), :].rearrange("p a b -> p (a b)")
                    dve.tensor_tensor(xk, pZ[p][k][:], xk, ALU.add).then_inc(x_ready, 1)
                dve.wait_ge(x_ready, g * 2 + 2)
                norm_statistics(dve, c, norm, g)
                norm_moments(dve, c, norm, g)

            take_y(0, 0)
            over_groups(dve, body)
            for k in range(C):
                dve.wait_ge(gat.hT_hi_ready, k + 1)
                dve.wait_ge(gat.hT0_ready, k + 1)
                dve.tensor_tensor(gat.hT_s[0][1][:, k, :], pY[0][k][:], gat.hT_s[0][0][:, k, :].bitcast(F32),
                                  ALU.subtract).then_inc(gat.hT_lo_ready, 1)
            for k in range(C):
                dve.wait_ge(gat.a_hi_ready, k + 1)
                dve.tensor_tensor(gat.aT[1][:, k, :], pZ[0][k][:], gat.aT[0][:, k, :].bitcast(F32), ALU.subtract
                                  ).then_inc(gat.a_lo_ready, 1)


class Attention:

    def __init__(self, nc, ctx):
        self.qT, self.kT = (ctx.enter_context(nc.sbuf_tensor("l3_" + n, [128, C, TOK], F32)) for n in ("qT", "kT"))
        (self.normed, self.t_ready, self.hT_hi_ready, self.hT_lo_ready, self.q_ready, self.qT_ready, self.k_ready,
         self.kT_ready, self.v_ready, self.v_taken) = (
            ctx.enter_context(nc.semaphore("l3_" + n)) for n in (
                'normed', 't_ready', 'hT_hi_ready', 'hT_lo_ready', 'q_ready', 'qT_ready', 'k_ready', 'kT_ready',
                'v_ready', 'v_taken'))


def project_feature(pe, out, weight, hT, co):
    todo = [(k, wi, mi) for k in range(C) for wi, mi in ((0, 0), (0, 1), (1, 0))]
    for n, (k, wi, mi) in enumerate(todo):
        last = pe.matmul(out[:], weight[wi][:, k, co * 128:co * 128 + 128], hT[mi][:, k, :],
                         start=(n == 0), stop=(n == len(todo) - 1))
    return last


def project_values(pe, out, weight, hT, b):
    todo = [(k, wi, mi) for k in range(C) for wi, mi in ((0, 0), (0, 1), (1, 0))]
    for n, (k, wi, mi) in enumerate(todo):
        last = pe.matmul(out[:, (b % 2) * D:(b % 2) * D + D], hT[mi][:, k, b * N:b * N + N], weight[wi][:, k, :],
                         start=(n == 0), stop=(n == len(todo) - 1))
    return last


def take_query(act, c, out, bank, k):
    return act.activation(out[:, k, :], bank[:], ACT.Identity, bias=c.bq[:, k:k + 1], scale=float(HD) ** -0.5)


def take_key(act, c, out, bank, k):
    return act.activation(out[:, k, :], bank[:], ACT.Identity, bias=c.bk[:, k:k + 1])


def take_value(act, c, bank, half):
    return act.activation(c.v_aug[:, 2 * half:2 * half + 2, :, 0:HD].rearrange("p b h d -> p (b h) d"),
                          bank[:].rearrange("p (m d) -> p m d", d=HD), ACT.Copy)


def layer2(nc, c, gat, att):
    PAIRS, TURNS = G // 2, 2 * STEPS
    with ExitStack() as ctx:
        sb = lambda n, s, d=F32: ctx.enter_context(nc.sbuf_tensor("l2_" + n, s, d))
        bank = lambda n: ctx.enter_context(nc.psum_tensor("l2_" + n, [128, 512], F32))
        nat, hT, hT_s, aT = gat.nat, gat.hT, gat.hT_s, gat.aT
        r, rsum, z, hv, rh, d = (sb(n, [128, C, TOK]) for n in ("r", "rsum", "z", "hv", "rh", "d"))
        rh_s = [sb(n, [128, C, TOK], F32R) for n in ("rh_hi", "rh_lo")]
        norm = Norm(nc, ctx, "l2_")
        first_hT = hT_s[0]
        pR, pZ, pH, pT = ([bank(f"p{n}{k}") for k in range(C)] for n in "RZHT")
        h0_ready, t_ready, hT0_ready = gat.h0_ready, gat.t_ready, gat.hT0_ready
        hT_hi_ready, hT_lo_ready = gat.hT_hi_ready, gat.hT_lo_ready
        a_ready, a_hi_ready, a_lo_ready = gat.a_ready, gat.a_hi_ready, gat.a_lo_ready
        (nat_ready, r_ready, z_ready, hv_ready, r_sig, rsum_ready, zsum_ready, z_sig, hv_tanh, rh_ready, rh_hi_ready,
         rh_lo_ready, d_ready, zd_ready, new_h, f_ready, x_ready) = (
            ctx.enter_context(nc.semaphore("l2_" + n)) for n in (
                'nat_ready', 'r_ready', 'z_ready', 'hv_ready', 'r_sig', 'rsum_ready', 'zsum_ready', 'z_sig',
                'hv_tanh', 'rh_ready', 'rh_hi_ready', 'rh_lo_ready', 'd_ready', 'zd_ready', 'new_h', 'f_ready',
                'x_ready'))
        block = ctx.enter_context(nc.Block())
        flat = lambda ap: ap.rearrange("p a b -> p (a b)")

        def over_turns(eng, turn):
            for pos in range(TURNS):
                turn(0, pos)
            with eng.Fori(1, PAIRS - 1) as j:
                for pos in range(TURNS):
                    turn(j, pos)
            for pos in range(TURNS):
                turn(PAIRS - 1, pos)

        def following(j, pos):
            if pos + 1 < TURNS:
                return j, pos + 1
            return None if isinstance(j, int) and j == PAIRS - 1 else (j + 1, 0)

        def preceding(j, pos):
            if pos:
                return j, pos - 1
            return None if isinstance(j, int) and j == 0 else (j - 1, TURNS - 1)

        def first_step(pos):
            return pos < 2

        def last_step(pos):
            return pos >= TURNS - 2

        def nats(j, pos):
            return (j * (TURNS - 2) + pos - 2) * 2

        @block.tensor
        def _(pe):
            def passes(out, weight, moving, co, first, last):
                todo = [(k, wi, mi) for k in range(C) for wi, mi in ((0, 0), (0, 1), (1, 0))]
                for n, (k, wi, mi) in enumerate(todo):
                    ins = pe.matmul(out[:], weight[wi][:, k, co * 128:co * 128 + 128], moving[mi][:, k, :],
                                    start=first and n == 0, stop=last and n == len(todo) - 1)
                return ins

            def back_to_nodes(q, ready):
                for half in range(2):
                    for b in (2 * half, 2 * half + 1):
                        for k in range(C):
                            at = (b % 2) * D + k * 128
                            last = pe.transpose(pT[half][:, at:at + 128], hT[q][:, k, b * N:b * N + N], c.ident[:])
                    last.then_inc(ready, 1)

            def turn_h(j, pos):
                K = j * TURNS + pos
                need(pe, a_lo_ready, K * C)
                if first_step(pos):
                    need(pe, x_ready, (2 * j - 1 + pos) * 2)
                    pe.wait_ge(h0_ready, (2 * j + pos + 1) * GB)
                    for k in range(C):
                        for b in range(GB):
                            last = pe.transpose(pT[k][:, b * N:b * N + N], nat[:, b, k * 128:k * 128 + 128], c.ident[:])
                        last.then_inc(t_ready, 1)
                else:
                    pe.wait_ge(new_h, (K - 1) * C)
                    back_to_nodes(pos % 2, t_ready)

            def gather(j, pos):
                K = j * TURNS + pos
                if not first_step(pos):
                    pe.wait_ge(nat_ready, nats(j, pos) + 2)
                if first_step(pos):
                    pe.wait_ge(hT0_ready, (2 * j + pos + 1) * C)
                    pe.wait_ge(hT_hi_ready, K * C + C)
                    pe.wait_ge(hT_lo_ready, K * C + C)
                for k in range(C):
                    for b in range(GB):
                        last = pe.matmul(pT[k][:, b * N:b * N + N], nat[:, b, k * 128:k * 128 + 128], c.adjT[:],
                                         start=True, stop=True)
                    last.then_inc(a_ready, 1)

            def final_h(K, q):
                pe.wait_ge(new_h, K * C)
                back_to_nodes(q, f_ready)

            def turn(j, pos):
                K = j * TURNS + pos
                nxt, prev = following(j, pos), preceding(j, pos)
                pe.wait_ge(hT_hi_ready, K * C + C)
                pe.wait_ge(hT_lo_ready, K * C + C)
                pe.wait_ge(a_hi_ready, K * C + C)
                pe.wait_ge(a_lo_ready, K * C + C)
                need(pe, r_sig, K * C)
                need(pe, rsum_ready, K * C)
                for co in range(C):
                    passes(pR[co], c.u3, hT_s[pos % 2], co, True, False)
                    passes(pR[co], c.w4, aT, co, False, True).then_inc(r_ready, 1)
                if prev and last_step(prev[1]):
                    final_h(K, prev[1] % 2)
                need(pe, zsum_ready, K * C)
                for co in range(C):
                    passes(pZ[co], c.w3, aT, co, True, True).then_inc(z_ready, 1)
                if nxt:
                    turn_h(*nxt)
                need(pe, hv_tanh, K * C)
                for co in range(C):
                    passes(pH[co], c.w5, aT, co, True, False)
                if nxt:
                    gather(*nxt)
                else:
                    first_tokens()
                pe.wait_ge(rh_hi_ready, K * C + C)
                pe.wait_ge(rh_lo_ready, K * C + C)
                for co in range(C):
                    passes(pH[co], c.u5, rh_s, co, False, True).then_inc(hv_ready, 1)

            def first_tokens():
                pe.wait_ge(att.normed, GB)
                pe.wait_ge(x_ready, (G - 1) * 2)
                for k in range(C):
                    for b in range(GB):
                        last = pe.transpose(pT[k][:, b * N:b * N + N], nat[:, b, k * 128:k * 128 + 128], c.ident[:])
                    last.then_inc(att.t_ready, 1)

            over_turns(pe, turn)
            pe.wait_ge(att.hT_hi_ready, C)
            pe.wait_ge(att.hT_lo_ready, C)
            pe.wait_ge(rsum_ready, PAIRS * TURNS * C)
            for co in range(C):
                project_feature(pe, pR[co], c.wq, first_hT, co).then_inc(att.q_ready, 1)
            pe.wait_ge(zsum_ready, PAIRS * TURNS * C)
            for co in range(C):
                project_feature(pe, pZ[co], c.wk, first_hT, co).then_inc(att.k_ready, 1)
            final_h(PAIRS * TURNS, 1)
            for b in range(GB):
                if b % 2 == 0:
                    pe.wait_ge(att.qT_ready, b // 2 + 1)
                last = project_values(pe, pR[b // 2], c.wv, first_hT, b)
                if b % 2:
                    last.then_inc(att.v_ready, 1)

        @block.scalar
        def _(act):
            def make_h0(j, pos):
                K, g = j * TURNS + pos, 2 * j + pos
                need(act, a_ready, K * C)
                for b in range(GB):
                    i = g * GB + b
                    act.activation(nat[:, b, :], flat(c.x[:, bass.ds(i, 1), :]), ACT.Relu,
                                   bias=c.nmr[:, bass.ds(i, 1)], scale=c.rstd[:, bass.ds(i, 1)]).then_inc(h0_ready, 1)

            def take_turned(j, pos):
                K = j * TURNS + pos
                for k in range(2):
                    act.wait_ge(t_ready, K * 2 + k + 1)
                    if first_step(pos):
                        act.activation(hT[pos % 2][:, k, :], pT[k][:], ACT.Copy).then_inc(hT0_ready, 1)
                        act.activation(hT_s[pos % 2][0][:, k, :], pT[k][:], ACT.Copy).then_inc(hT_hi_ready, 1)
                    else:
                        act.activation(flat(nat[:, 2 * k:2 * k + 2, :]), pT[k][:], ACT.Copy).then_inc(nat_ready, 1)

            def take_gathered(j, pos):
                K = j * TURNS + pos
                for k in range(C):
                    act.wait_ge(a_ready, K * C + k + 1)
                    act.activation(aT[0][:, k, :], pT[k][:], ACT.Copy).then_inc(a_hi_ready, 1)

            def finish(j, pos):
                K = j * TURNS + pos
                need(act, d_ready, K)
                for co in range(C):
                    act.wait_ge(hv_ready, K * C + co + 1)
                    act.activation(hv[:, co, :], pH[co][:], ACT.Tanh, bias=c.bh[:, co:co + 1]).then_inc(hv_tanh, 1)

            def split_new_h(j, pos):
                K = j * TURNS + pos
                for k in range(C):
                    act.wait_ge(new_h, K * C + k + 1)
                    act.activation(hT_s[pos % 2][0][:, k, :], hT[pos % 2][:, k, :], ACT.Copy).then_inc(hT_hi_ready, 1)

            def turn(j, pos):
                K = j * TURNS + pos
                nxt, prev = following(j, pos), preceding(j, pos)
                if prev:
                    finish(*prev)
                if not nxt:
                    act.wait_ge(norm.factors_ready, 1)
                    act.wait_ge(a_ready, PAIRS * TURNS * C)
                    for b in range(GB):
                        act.activation(nat[:, b, :], c.x[:, b, :], ACT.Relu, bias=c.nmr[:, b:b + 1],
                                       scale=c.rstd[:, b:b + 1]).then_inc(att.normed, 1)
                if nxt and first_step(nxt[1]):
                    make_h0(*nxt)
                if prev and not last_step(prev[1]):
                    split_new_h(*prev)
                for co in range(C):
                    act.wait_ge(r_ready, K * C + co + 1)
                    act.activation(r[:, co, :], pR[co][:], ACT.Sigmoid, bias=c.br[:, co:co + 1]).then_inc(r_sig, 1)
                for co in range(C):
                    need(act, zsum_ready, K * C - C + co + 1)
                    act.activation(rsum[:, co, :], pR[co][:], ACT.Copy).then_inc(rsum_ready, 1)
                for co in range(C):
                    act.wait_ge(rh_ready, K * C + co + 1)
                    act.activation(rh_s[0][:, co, :], rh[:, co, :], ACT.Copy).then_inc(rh_hi_ready, 1)
                if nxt:
                    take_turned(*nxt)
                for co in range(C):
                    act.wait_ge(zsum_ready, K * C + co + 1)
                    act.activation(z[:, co, :], z[:, co, :], ACT.Sigmoid, bias=c.bz[:, co:co + 1]).then_inc(z_sig, 1)
                if nxt:
                    take_gathered(*nxt)
                else:
                    for k in range(C):
                        act.wait_ge(att.t_ready, k + 1)
                        act.activation(first_hT[0][:, k, :], pT[k][:], ACT.Copy).then_inc(att.hT_hi_ready, 1)

            over_turns(act, turn)
            finish(PAIRS - 1, TURNS - 1)
            for k in range(C):
                act.wait_ge(att.q_ready, k + 1)
                take_query(act, c, att.qT, pR[k], k).then_inc(att.qT_ready, 1)
            for k in range(C):
                act.wait_ge(att.k_ready, k + 1)
                take_key(act, c, att.kT, pZ[k], k).then_inc(att.kT_ready, 1)
            for half in range(2):
                act.wait_ge(att.v_ready, half + 1)
                take_value(act, c, pR[half], half).then_inc(att.v_taken, 1)

        @block.gpsimd
        def _(pool):
            with pool.Fori(0, G) as g:
                norm_factors(pool, c, norm, g)

        @block.vector
        def _(dve):
            def take_turned(j, pos):
                K = j * TURNS + pos
                if first_step(pos):
                    for k in range(C):
                        dve.wait_ge(hT_hi_ready, K * C + k + 1)
                        dve.tensor_tensor(hT_s[pos % 2][1][:, k, :], pT[k][:],
                                          hT_s[pos % 2][0][:, k, :].bitcast(F32), ALU.subtract).then_inc(hT_lo_ready, 1)

            def take_gathered(j, pos):
                K = j * TURNS + pos
                for k in range(C):
                    dve.wait_ge(a_hi_ready, K * C + k + 1)
                    dve.tensor_tensor(aT[1][:, k, :], pT[k][:], aT[0][:, k, :].bitcast(F32), ALU.subtract
                                      ).then_inc(a_lo_ready, 1)

            def finish(j, pos):
                K, q = j * TURNS + pos, pos % 2
                dve.wait_ge(hv_tanh, K * C + C)
                need(dve, zd_ready, K * C)
                dve.tensor_tensor(d[:], hv[:], hT[q][:], ALU.subtract).then_inc(d_ready, 1)
                dve.wait_ge(d_ready, K + 1)
                dve.wait_ge(z_sig, K * C + C)
                need(dve, new_h, K * C)
                for co in range(C):
                    dve.tensor_tensor(d[:, co, :], z[:, co, :], d[:, co, :], ALU.mult).then_inc(zd_ready, 1)
                for co in range(C):
                    dve.wait_ge(zd_ready, K * C + co + 1)
                    dve.tensor_tensor(hT[q][:, co, :], hT[q][:, co, :], d[:, co, :], ALU.add).then_inc(new_h, 1)
                if not last_step(pos):
                    for co in range(C):
                        dve.wait_ge(hT_hi_ready, (K + 2) * C + co + 1)
                        dve.tensor_tensor(hT_s[q][1][:, co, :], hT[q][:, co, :], hT_s[q][0][:, co, :].bitcast(F32),
                                          ALU.subtract).then_inc(hT_lo_ready, 1)

            def add_final(g):
                for half in range(2):
                    dve.wait_ge(f_ready, g * 2 + half + 1)
                    xh = flat(c.x[:, bass.ds(g * GB + 2 * half, 2), :])
                    dve.tensor_tensor(xh, pT[half][:], xh, ALU.add).then_inc(x_ready, 1)

            def turn(j, pos):
                K, q = j * TURNS + pos, pos % 2
                nxt, prev = following(j, pos), preceding(j, pos)
                if prev:
                    finish(*prev)
                for co in range(C):
                    dve.wait_ge(r_sig, K * C + co + 1)
                    dve.tensor_tensor(rh[:, co, :], r[:, co, :], hT[q][:, co, :], ALU.mult).then_inc(rh_ready, 1)
                if prev and last_step(prev[1]):
                    g = 2 * prev[0] + prev[1] % 2
                    add_final(g)
                for co in range(C):
                    dve.wait_ge(rh_hi_ready, K * C + co + 1)
                    dve.tensor_tensor(rh_s[1][:, co, :], rh[:, co, :], rh_s[0][:, co, :].bitcast(F32), ALU.subtract
                                      ).then_inc(rh_lo_ready, 1)
                if nxt:
                    take_turned(*nxt)
                for co in range(C):
                    dve.wait_ge(rsum_ready, K * C + co + 1)
                    dve.wait_ge(z_ready, K * C + co + 1)
                    dve.tensor_tensor(z[:, co, :], pZ[co][:], rsum[:, co, :], ALU.add).then_inc(zsum_ready, 1)
                if nxt:
                    take_gathered(*nxt)
                if prev and last_step(prev[1]):
                    dve.wait_ge(x_ready, g * 2 + 2)
                    norm_statistics(dve, c, norm, g)
                    norm_moments(dve, c, norm, g)
                if not nxt:
                    for k in range(C):
                        dve.wait_ge(att.hT_hi_ready, k + 1)
                        dve.tensor_tensor(first_hT[1][:, k, :], pT[k][:], first_hT[0][:, k, :].bitcast(F32),
                                          ALU.subtract).then_inc(att.hT_lo_ready, 1)

            over_turns(dve, turn)
            finish(PAIRS - 1, TURNS - 1)
            add_final(G - 1)
            dve.wait_ge(x_ready, G * 2)
            norm_statistics(dve, c, norm, G - 1)
            norm_moments(dve, c, norm, G - 1)


def layer3(nc, c, att, out):
    UB = GB // 2
    with ExitStack() as ctx:
        sb = lambda n, s, d=F32: ctx.enter_context(nc.sbuf_tensor("l3_" + n, s, d))
        bank = lambda n: ctx.enter_context(nc.psum_tensor("l3_" + n, [128, 512], F32))
        xn = sb("xn", [128, GB, D])
        hT = [sb(n, [128, C, TOK], F32R) for n in ("hT_hi", "hT_lo")]
        qT, kT = att.qT, att.kT
        logit = sb("logit", [128, HR, UB * C, N])
        prob = [sb(f"prob{e}", [128, HR, UB * C, N]) for e in range(2)]
        top = sb("top", [128, HR, UB * C])
        probT = sb("probT", [128, HR, UB * C * N])
        rtotal = sb("rtotal", [128, UB, H])
        o = sb("o", [128, UB, D])
        oT = [sb(n, [128, C, UB * N], F32R) for n in ("oT_hi", "oT_lo")]
        pS = [bank(f"pS{r}") for r in range(HR)]
        pT = [bank(f"pT{k}") for k in range(2)]
        pJ = [bank(f"pJ{k}") for k in range(2)]
        v_banks = [pT[0], pJ[0]]
        normed, t_ready, hT_hi_ready, hT_lo_ready = att.normed, att.t_ready, att.hT_hi_ready, att.hT_lo_ready
        q_ready, qT_ready, k_ready, kT_ready = att.q_ready, att.qT_ready, att.k_ready, att.kT_ready
        v_ready, v_taken = att.v_ready, att.v_taken
        (biased, s_ready, masked, top_ready, shifted, prob_ready, pt_ready, probT_ready, pv_ready, rtotal_ready,
         o_ready, ot_ready, oT_hi_ready, oT_lo_ready, w_ready, x_ready, stored) = (
            ctx.enter_context(nc.semaphore("l3_" + n)) for n in (
                'biased', 's_ready', 'masked', 'top_ready', 'shifted', 'prob_ready', 'pt_ready', 'probT_ready',
                'pv_ready', 'rtotal_ready', 'o_ready', 'ot_ready', 'oT_hi_ready', 'oT_lo_ready', 'w_ready', 'x_ready',
                'stored'))
        block = ctx.enter_context(nc.Block())
        flat = lambda ap: ap.rearrange("p a b -> p (a b)")

        def over_turns(eng, turn):
            turn(0, 0)
            turn(0, 1)
            with eng.Fori(1, G - 1) as g:
                turn(g, 0)
                turn(g, 1)
            turn(G - 1, 0)
            turn(G - 1, 1)

        def coming(g, e):
            return (g, 1) if e == 0 else (g + 1, 0) if exists(g + 1) else None

        @block.tensor
        def _(pe):
            def turn_tokens(g):
                pe.wait_ge(normed, g * GB + GB)
                need(pe, probT_ready, (2 * g - 1) * HR)
                for k in range(C):
                    for b in range(GB):
                        last = pe.transpose(pT[k][:, b * N:b * N + N], xn[:, b, k * 128:k * 128 + 128], c.ident[:])
                    last.then_inc(t_ready, 1)

            def project(weight, ready, left, count):
                for co in range(C):
                    need(pe, left, count + co + 1)
                    project_feature(pe, pJ[co], weight, hT, co).then_inc(ready, 1)

            def queries_and_keys(g):
                pe.wait_ge(hT_hi_ready, g * C + C)
                pe.wait_ge(hT_lo_ready, g * C + C)
                project(c.wq, q_ready, o_ready, (g - 1) * 2 * UB)
                project(c.wk, k_ready, qT_ready, g * C)

            def values(g, half):
                if half == 0:
                    pe.wait_ge(probT_ready, (2 * g - 1) * HR + 3)
                else:
                    pe.wait_ge(o_ready, (2 * g - 1) * UB + 1)
                for b in (2 * half, 2 * half + 1):
                    last = project_values(pe, v_banks[half], c.wv, hT, b)
                last.then_inc(v_ready, 1)

            def scores(g, e, first):
                U = 2 * g + e
                pe.wait_ge(qT_ready, g * C + C)
                pe.wait_ge(kT_ready, g * C + C)
                need(pe, masked, (U - 1) * HR + first + 2)
                for b in range(UB):
                    for k in range(C):
                        for r in (first, first + 1):
                            cols = slice((e * UB + b) * N, (e * UB + b) * N + N)
                            at = (b * C + k) * N
                            last = pe.matmul(pS[r][:, at:at + N], qT[r * HD:r * HD + HD, k, cols],
                                             kT[r * HD:r * HD + HD, k, cols], start=True, stop=True)
                            if b * C + k == UB * C - 1:
                                last.then_inc(s_ready, 1)

            def turn_outputs(U):
                pe.wait_ge(o_ready, (U + 1) * UB)
                for k in range(C):
                    for b in range(UB):
                        last = pe.transpose(pT[1][:, (k * UB + b) * N:(k * UB + b) * N + N],
                                            o[:, b, k * 128:k * 128 + 128], c.ident[:])
                last.then_inc(ot_ready, 1)

            def project_outputs(U):
                pe.wait_ge(oT_hi_ready, U * C + C)
                pe.wait_ge(oT_lo_ready, U * C + C)
                for b in range(UB):
                    todo = [(k, wi, mi) for k in range(C) for wi, mi in ((0, 0), (0, 1), (1, 0))]
                    for n, (k, wi, mi) in enumerate(todo):
                        last = pe.matmul(pJ[1][:, b * D:b * D + D], oT[mi][:, k, b * N:b * N + N], c.wo[wi][:, k, :],
                                         start=(n == 0), stop=(n == len(todo) - 1))
                last.then_inc(w_ready, 1)

            def probabilities(g, e, heads):
                U = 2 * g + e
                for r in heads:
                    pe.wait_ge(prob_ready, U * HR + r + 1)
                    if r == 1:
                        need(pe, oT_lo_ready, U * C)
                    if r >= 2:
                        pe.wait_ge(probT_ready, U * HR + r - 1)
                    for m in range(UB * C):
                        last = pe.transpose(pT[r % 2][:, m * N:m * N + N], prob[e][:, r, m, :], c.ident[:])
                    last.then_inc(pt_ready, 1)

            def attend(g, e, b):
                U = 2 * g + e
                for r in range(HR):
                    if b == 0:
                        pe.wait_ge(probT_ready, U * HR + r + 1)
                    for k in range(C):
                        at, m = (k * HR + r) * (HD + 1), b * C + k
                        last = pe.matmul(pJ[b][:, at:at + HD + 1], probT[:, r, m * N:m * N + N],
                                         c.v_aug[:, e * UB + b, k * HR + r, :], start=True, stop=True)
                last.then_inc(pv_ready, 1)

            def turn(g, e):
                U = 2 * g + e
                nxt = coming(g, e)
                later = not isinstance(g, int) or U > 0
                if later:
                    turn_outputs(U - 1)
                if e == 0:
                    pe.wait_ge(v_taken, g * 2 + 1)
                probabilities(g, e, (0,))
                if nxt:
                    scores(*nxt, 0)
                if later:
                    project_outputs(U - 1)
                probabilities(g, e, (1,))
                if nxt:
                    scores(*nxt, 2)
                probabilities(g, e, (2, 3))
                if e == 0:
                    pe.wait_ge(v_taken, g * 2 + 2)
                attend(g, e, 0)
                if exists(g + 1):
                    if e == 0:
                        turn_tokens(g + 1)
                    else:
                        values(g + 1, 0)
                need(pe, x_ready, U)
                attend(g, e, 1)
                if exists(g + 1):
                    if e == 0:
                        queries_and_keys(g + 1)
                    else:
                        values(g + 1, 1)

            scores(0, 0, 0)
            scores(0, 0, 2)
            over_turns(pe, turn)
            turn_outputs(2 * G - 1)
            project_outputs(2 * G - 1)

        @block.scalar
        def _(act):
            def take_tokens(g):
                for k in range(C):
                    act.wait_ge(t_ready, g * C + k + 1)
                    act.activation(hT[0][:, k, :], pT[k][:], ACT.Relu).then_inc(hT_hi_ready, 1)

            def take_queries_and_keys(g):
                for k in range(C):
                    act.wait_ge(q_ready, g * C + k + 1)
                    take_query(act, c, qT, pJ[k], k).then_inc(qT_ready, 1)
                for k in range(C):
                    act.wait_ge(k_ready, g * C + k + 1)
                    take_key(act, c, kT, pJ[k], k).then_inc(kT_ready, 1)

            def take_values(g):
                for k in range(2):
                    act.wait_ge(v_ready, g * 2 + k + 1)
                    take_value(act, c, v_banks[k], k).then_inc(v_taken, 1)

            def take_outputs(U):
                act.wait_ge(ot_ready, U + 1)
                for k in range(C):
                    act.activation(oT[0][:, k, :], pT[1][:, k * UB * N:(k + 1) * UB * N], ACT.Identity,
                                   bias=c.bv[:, k:k + 1]).then_inc(oT_hi_ready, 1)

            def exponentials(g, e, heads):
                U = 2 * g + e
                for r in heads:
                    act.wait_ge(shifted, U * HR + r + 1)
                    act.activation(flat(prob[e][:, r]), flat(logit[:, r]), ACT.Exp).then_inc(prob_ready, 1)

            def turn(g, e):
                U = 2 * g + e
                nxt = coming(g, e)
                if not isinstance(g, int) or U > 0:
                    take_outputs(U - 1)
                for r in range(HR):
                    act.wait_ge(pt_ready, U * HR + r + 1)
                    act.activation(probT[:, r, :], pT[r % 2][:], ACT.Copy).then_inc(probT_ready, 1)
                if nxt:
                    exponentials(*nxt, range(2))
                if e == 0 and exists(g + 1):
                    take_tokens(g + 1)
                if nxt:
                    exponentials(*nxt, range(2, HR))
                if exists(g + 1):
                    if e == 0:
                        take_queries_and_keys(g + 1)
                    else:
                        take_values(g + 1)

            exponentials(0, 0, range(HR))
            over_turns(act, turn)
            take_outputs(2 * G - 1)

        @block.gpsimd
        def _(pool):
            def shift(g, e):
                U = 2 * g + e
                for r in range(HR):
                    pool.wait_ge(top_ready, U * HR + r + 1)
                    pool.tensor_tensor(logit[:, r], logit[:, r], bcast(top[:, r], N), ALU.subtract).then_inc(shifted, 1)

            def bias(g):
                pool.wait_ge(normed, g * GB + GB)
                xg = c.x[:, bass.ds(g * GB, GB), :]
                pool.tensor_tensor(xg, xg, bcast_mid(c.bias3[:], GB), ALU.add).then_inc(biased, 1)

            def turn(g, e):
                nxt = coming(g, e)
                if nxt:
                    shift(*nxt)
                if e == 0 and exists(g + 1):
                    bias(g + 1)

            bias(0)
            shift(0, 0)
            over_turns(pool, turn)

        @block.vector
        def _(dve):
            def norm(g):
                need(dve, t_ready, g * C)
                for b in range(GB):
                    i = g * GB + b
                    dve.tensor_scalar(xn[:, b, :], flat(c.x[:, bass.ds(i, 1), :]), c.rstd[:, bass.ds(i, 1)],
                                      c.nmr[:, bass.ds(i, 1)], ALU.mult, ALU.add).then_inc(normed, 1)

            def take_tokens(g):
                for k in range(C):
                    dve.wait_ge(hT_hi_ready, g * C + k + 1)
                    dve.scalar_tensor_tensor(hT[1][:, k, :], pT[k][:], 0.0, hT[0][:, k, :].bitcast(F32),
                                             ALU.max, ALU.subtract).then_inc(hT_lo_ready, 1)

            def mask_and_top(g, e, first):
                U = 2 * g + e

                def mask(r):
                    dve.wait_ge(s_ready, U * HR + r + 1)
                    need(dve, prob_ready, (U - 1) * HR + r + 1)
                    dve.tensor_tensor(logit[:, r], pS[r][:].rearrange("p (m n) -> p m n", n=N),
                                      bcast_mid(c.mask[:], UB * C), ALU.add).then_inc(masked, 1)

                mask(first)
                mask(first + 1)
                for r in (first, first + 1):
                    dve.wait_ge(masked, U * HR + r + 1)
                    dve.tensor_reduce(top[:, r], logit[:, r], AX.X, ALU.max).then_inc(top_ready, 1)

            def outputs(U, graphs):
                for b in graphs:
                    heads = pJ[b][:, 0:H * (HD + 1)].rearrange("p (h d) -> p h d", d=HD + 1)
                    dve.wait_ge(pv_ready, U * UB + b + 1)
                    dve.reciprocal(rtotal[:, b, :].unsqueeze(2), heads[:, :, HD:HD + 1]).then_inc(rtotal_ready, 1)
                    dve.wait_ge(rtotal_ready, U * UB + b + 1)
                    need(dve, ot_ready, U)
                    dve.tensor_tensor(o[:, b, :].rearrange("p (h d) -> p h d", d=HD), heads[:, :, 0:HD],
                                      bcast(rtotal[:, b, :], HD), ALU.mult).then_inc(o_ready, 1)

            def take_outputs(U):
                dve.wait_ge(oT_hi_ready, U * C + C)
                for k in range(C):
                    dve.scalar_tensor_tensor(oT[1][:, k, :], pT[1][:, k * UB * N:(k + 1) * UB * N], c.bv[:, k:k + 1],
                                             oT[0][:, k, :].bitcast(F32), ALU.add, ALU.subtract
                                             ).then_inc(oT_lo_ready, 1)

            def add_outputs(U, at, g):
                dve.wait_ge(w_ready, U + 1)
                dve.wait_ge(biased, g + 1)
                xu = flat(c.x[:, bass.ds(at, UB), :])
                dve.tensor_tensor(xu, pJ[1][:], xu, ALU.add).then_inc(x_ready, 1)

            def turn(g, e):
                U = 2 * g + e
                nxt = coming(g, e)
                later = not isinstance(g, int) or U > 0
                if later:
                    take_outputs(U - 1)
                if e == 0 and exists(g + 1):
                    norm(g + 1)
                if nxt:
                    mask_and_top(*nxt, 0)
                if later:
                    add_outputs(U - 1, (U - 1) * UB, g if e else g - 1)
                if nxt:
                    mask_and_top(*nxt, 2)
                outputs(U, (0,))
                if e == 0 and exists(g + 1):
                    take_tokens(g + 1)
                outputs(U, (1,))

            mask_and_top(0, 0, 0)
            mask_and_top(0, 0, 2)
            over_turns(dve, turn)
            take_outputs(2 * G - 1)
            add_outputs(2 * G - 1, (2 * G - 1) * UB, G - 1)

        @block.sync
        def _(sp):
            with sp.Fori(0, 2 * G) as U:
                sp.wait_ge(x_ready, U + 1)
                sp.dma_start(out[bass.ds(U * UB, UB)].rearrange("b n d -> n b d"), c.x[:, bass.ds(U * UB, UB), :]
                             ).then_inc(stored, 16)
            sp.wait_ge(stored, 2 * G * 16)


def build(nc, t, out):
    c = Chip()
    with ExitStack() as ctx:
        c.x = ctx.enter_context(nc.sbuf_tensor("x_stream", [128, B, D], F32))
        sb = lambda n, s, d=F32: ctx.enter_context(nc.sbuf_tensor(n, s, d))
        pair = lambda n, s: (sb(n + "_hi", s, F32R), sb(n + "_lo", s, F32R))
        c.ident, c.adj, c.adjT, c.mask = (sb(n, [128, N]) for n in ("ident", "adj", "adjT", "mask"))
        c.beta = sb("beta", [128, 1])
        c.eps, c.power, c.minus = (sb(n, [128, GB]) for n in ("eps", "power", "minus"))
        c.x_landed = [ctx.enter_context(nc.semaphore(f"x_landed{g}")) for g in range(G)]
        c.rstd, c.nmr = sb("rstd", [128, B]), sb("nmr", [128, B])
        c.W0 = sb("W0", [128, C, D])
        c.wa = sb("wa", [128, 2, C])
        c.bias1, c.bias3 = sb("bias1", [128, D]), sb("bias3", [128, D])
        c.W1 = pair("W1", [128, C, D])
        c.w3, c.w4, c.w5, c.u3, c.u5 = (pair(n, [128, C, D]) for n in ("w3T", "w4T", "w5T", "u3T", "u5T"))
        c.wq, c.wk, c.wv, c.wo = (pair(n, [128, C, D]) for n in ("wq", "wk", "wv", "wo"))
        c.bz, c.br, c.bh, c.bq, c.bk, c.bv = (sb(n, [128, C]) for n in ("bz", "br", "bh", "bq", "bk", "bv"))
        c.v_aug = sb("v_aug", [128, GB, H, HD + 1])
        c.settled_dve, c.settled_pool = (ctx.enter_context(nc.semaphore(n)) for n in ("settled_dve", "settled_pool"))
        prepare(nc, t, c)
        with ExitStack() as gated_start:
            with ExitStack() as banks:
                gth = Gather(nc, ctx, banks)
                layer0(nc, t, c, gth)
                att = Attention(nc, ctx)
                gat = Gated(nc, gated_start)
                layer1(nc, c, gth, gat)
            layer2(nc, c, gat, att)
        layer3(nc, c, att, out)


def kernel(**inputs):
    import concourse.bacc as bacc
    from concourse.bass_utils import run_bass_kernel_spmd
    nc = bacc.Bacc("TRN2", target_bir_lowering=False, num_devices=1)
    tensors, arrays = {}, {}
    for name in INPUTS:
        a = np.ascontiguousarray(inputs[name])
        arrays["in_" + name] = a
        tensors[name] = nc.dram_tensor("in_" + name, a.shape, mybir.dt.from_np(a.dtype), kind="ExternalInput").ap()
    out = nc.dram_tensor("out_0", (B, N, D), F32, kind="ExternalOutput").ap()
    build(nc, tensors, out)
    return run_bass_kernel_spmd(nc, [arrays], core_ids=[0]).results[0]["out_0"]
```
